# Optimizing a Trainium2 kernel written in Bass

```python
import numpy as np
import jax
import jax.numpy as jnp

def _softmax(x, axis=-1):
    return jax.nn.softmax(x, axis=axis)

def _gelu(x):
    return jax.nn.gelu(x, approximate=True)

def _silu(x):
    return jax.nn.silu(x)

def _sigmoid(x):
    return jax.nn.sigmoid(x)

def _layernorm(x, axis=-1, eps=1e-05):
    m = jnp.mean(x, axis=axis, keepdims=True)
    v = jnp.var(x, axis=axis, keepdims=True)
    return (x - m) / jnp.sqrt(v + eps)

def _scatter_add(tgt, idx, src, axis=0):
    return tgt.at[idx].add(src)

def _segment_sum(src, seg, n):
    return jax.ops.segment_sum(src, seg, n)
kernel_name = 'mk_adj_ffn_d2_adj_r2_6aa6e4'

def setup_inputs(seed: int=0):
    np.random.seed(seed)
    _w = jnp.asarray

    def _rec_inputs():
        import jax
        import jax.numpy as jnp
        _gk = jax.random.key(seed)
        x = -0.0002928 + 1 * jax.random.normal(jax.random.fold_in(_gk, 1), (8, 1024, 128), jnp.float32)
        _a = jax.random.bernoulli(jax.random.fold_in(_gk, 2), 0.0078125, (8, 1024, 1024))
        _a = jnp.logical_or(_a, jnp.swapaxes(_a, -1, -2))
        _a = jnp.logical_or(_a, jnp.eye(1024, dtype=bool))
        _af = _a.astype(jnp.float32)
        _af = _af * jax.random.uniform(jax.random.fold_in(_gk, 3), (8, 1024, 1024), jnp.float32, 0.05, 1)
        adj = _af
        return (x, adj)
    x, adj = _rec_inputs()

    def _L0_gnn_setup():
        import jax, jax.numpy as jnp
        import numpy as np
        B, N, D, H = (8, 1024, 128, 512)
        RMS_EPS = 1e-06

        def _rmsnorm(h, w, eps=RMS_EPS):
            var = jnp.mean(jnp.square(h), axis=-1, keepdims=True)
            return h * jax.lax.rsqrt(var + eps) * w
        key = jax.random.key(seed)
        ks = jax.random.split(key, 5)
        x = jax.random.normal(ks[0], (B, N, D), dtype=jnp.float32)
        adjacency = jax.random.uniform(ks[1], (B, N, N), dtype=jnp.float32)
        epsilon = jnp.zeros((), dtype=jnp.float32)
        W1 = jax.random.normal(ks[2], (D, H), dtype=jnp.float32) * (1.0 / np.sqrt(D))
        b1 = jnp.zeros((H,), dtype=jnp.float32)
        rms_weight = jnp.ones((H,), dtype=jnp.float32)
        W2 = jax.random.normal(ks[3], (H, D), dtype=jnp.float32) * (1.0 / np.sqrt(H))
        b2 = jnp.zeros((D,), dtype=jnp.float32)
        return {'x': x, 'adjacency': adjacency, 'epsilon': epsilon, 'W1': W1, 'b1': b1, 'rms_weight': rms_weight, 'W2': W2, 'b2': b2}
    _L0_gnn_all = _L0_gnn_setup()
    _L0_gnn_in = {k: v for k, v in _L0_gnn_all.items() if k in ('epsilon', 'W1', 'b1', 'rms_weight', 'W2', 'b2')}
    del _L0_gnn_all

    def _L0_ffn_setup():
        import jax, jax.numpy as jnp
        import numpy as np
        E = 8
        K = 2
        D = 128
        H = 256
        DOUT = 128
        EPS = 1e-05
        key = jax.random.key(seed)
        ks = jax.random.split(key, 9)
        s = 0.02
        return {'x': jax.random.normal(ks[0], (4, 4096, D), jnp.float32), 'gamma': 1.0 + 0.05 * jax.random.normal(ks[1], (D,), jnp.float32), 'beta': 0.05 * jax.random.normal(ks[2], (D,), jnp.float32), 'Wr': 0.01 * jax.random.normal(ks[3], (D, E), jnp.float32), 'br': jnp.zeros((E,), jnp.float32), 'W1': s * jax.random.normal(ks[4], (E, D, H), jnp.float32), 'b1': s * jax.random.normal(ks[5], (E, H), jnp.float32), 'W2': s * jax.random.normal(ks[6], (E, H, DOUT), jnp.float32), 'b2': s * jax.random.normal(ks[7], (E, DOUT), jnp.float32)}
    _L0_ffn_all = _L0_ffn_setup()
    _L0_ffn_in = {k: v for k, v in _L0_ffn_all.items() if k in ('gamma', 'beta', 'Wr', 'br', 'W1', 'b1', 'W2', 'b2')}
    del _L0_ffn_all

    def _L1_gnn_setup():
        import jax, jax.numpy as jnp
        import numpy as np
        LN_EPS = 1e-05
        key = jax.random.key(seed)
        k1, k2, k3, k4 = jax.random.split(key, 4)
        B, N, F, O = (8, 1024, 128, 128)
        x = jax.random.normal(k1, (B, N, F), dtype=jnp.float32)
        adj = jax.random.uniform(k2, (B, N, N), dtype=jnp.float32)
        gamma = jnp.ones((F,), jnp.float32)
        beta = jnp.zeros((F,), jnp.float32)
        W_self = jax.random.normal(k3, (F, O), dtype=jnp.float32) * (1.0 / np.sqrt(F))
        W_neigh = jax.random.normal(k4, (F, O), dtype=jnp.float32) * (1.0 / np.sqrt(F))
        return {'x': x, 'adj': adj, 'gamma': gamma, 'beta': beta, 'W_self': W_self, 'W_neigh': W_neigh}
    _L1_gnn_all = _L1_gnn_setup()
    _L1_gnn_in = {k: v for k, v in _L1_gnn_all.items() if k in ('gamma', 'beta', 'W_self', 'W_neigh')}
    del _L1_gnn_all

    def _L1_ffn_setup():
        import jax, jax.numpy as jnp
        import numpy as np
        B, T, IN_DIM = (64, 128, 128)
        HID, OUT_DIM = (256, 128)
        N_LAYERS, N_EXPERTS, N_SHARED = (2, 16, 1)
        key = jax.random.key(seed)
        ks = jax.random.split(key, 10)
        s = 0.02
        x = jax.random.normal(ks[0], (B, T, IN_DIM), dtype=jnp.float32)
        route_id = jax.random.randint(ks[1], (B,), 0, N_EXPERTS)
        Wi = jax.random.normal(ks[2], (HID, IN_DIM), dtype=jnp.float32) * s
        bi = jnp.zeros((HID,), dtype=jnp.float32)
        Wr = jax.random.normal(ks[3], (N_LAYERS, N_EXPERTS, HID, HID), dtype=jnp.float32) * s
        br = jax.random.normal(ks[4], (N_LAYERS, N_EXPERTS, HID), dtype=jnp.float32) * s
        Ws = jax.random.normal(ks[5], (N_LAYERS, N_SHARED, HID, HID), dtype=jnp.float32) * s
        bs = jax.random.normal(ks[6], (N_LAYERS, N_SHARED, HID), dtype=jnp.float32) * s
        Wo = jax.random.normal(ks[7], (OUT_DIM, HID), dtype=jnp.float32) * s
        bo = jnp.zeros((OUT_DIM,), dtype=jnp.float32)
        return {'x': x, 'route_id': route_id, 'Wi': Wi, 'bi': bi, 'Wr': Wr, 'br': br, 'Ws': Ws, 'bs': bs, 'Wo': Wo, 'bo': bo}
    _L1_ffn_all = _L1_ffn_setup()
    _L1_ffn_in = {k: v for k, v in _L1_ffn_all.items() if k in ('route_id', 'Wi', 'bi', 'Wr', 'br', 'Ws', 'bs', 'Wo', 'bo')}
    del _L1_ffn_all
    return {'x': x, 'adj': adj, 'L0_gnn_epsilon': _L0_gnn_in['epsilon'], 'L0_gnn_W1': _L0_gnn_in['W1'], 'L0_gnn_b1': _L0_gnn_in['b1'], 'L0_gnn_rms_weight': _L0_gnn_in['rms_weight'], 'L0_gnn_W2': _L0_gnn_in['W2'], 'L0_gnn_b2': _L0_gnn_in['b2'], 'L0_ffn_gamma': _L0_ffn_in['gamma'], 'L0_ffn_beta': _L0_ffn_in['beta'], 'L0_ffn_Wr': _L0_ffn_in['Wr'], 'L0_ffn_br': _L0_ffn_in['br'], 'L0_ffn_W1': _L0_ffn_in['W1'], 'L0_ffn_b1': _L0_ffn_in['b1'], 'L0_ffn_W2': _L0_ffn_in['W2'], 'L0_ffn_b2': _L0_ffn_in['b2'], 'L1_gnn_gamma': _L1_gnn_in['gamma'], 'L1_gnn_beta': _L1_gnn_in['beta'], 'L1_gnn_W_self': _L1_gnn_in['W_self'], 'L1_gnn_W_neigh': _L1_gnn_in['W_neigh'], 'L1_ffn_route_id': _L1_ffn_in['route_id'], 'L1_ffn_Wi': _L1_ffn_in['Wi'], 'L1_ffn_bi': _L1_ffn_in['bi'], 'L1_ffn_Wr': _L1_ffn_in['Wr'], 'L1_ffn_br': _L1_ffn_in['br'], 'L1_ffn_Ws': _L1_ffn_in['Ws'], 'L1_ffn_bs': _L1_ffn_in['bs'], 'L1_ffn_Wo': _L1_ffn_in['Wo'], 'L1_ffn_bo': _L1_ffn_in['bo']}

def reference(x, adj, L0_gnn_epsilon, L0_gnn_W1, L0_gnn_b1, L0_gnn_rms_weight, L0_gnn_W2, L0_gnn_b2, L0_ffn_gamma, L0_ffn_beta, L0_ffn_Wr, L0_ffn_br, L0_ffn_W1, L0_ffn_b1, L0_ffn_W2, L0_ffn_b2, L1_gnn_gamma, L1_gnn_beta, L1_gnn_W_self, L1_gnn_W_neigh, L1_ffn_route_id, L1_ffn_Wi, L1_ffn_bi, L1_ffn_Wr, L1_ffn_br, L1_ffn_Ws, L1_ffn_bs, L1_ffn_Wo, L1_ffn_bo):
    import jax
    import jax.numpy as jnp

    def _L0_gnn_ref(x, adjacency, epsilon, W1, b1, rms_weight, W2, b2):
        import jax, jax.numpy as jnp
        import numpy as np
        B, N, D, H = (8, 1024, 128, 512)
        RMS_EPS = 1e-06

        def _rmsnorm(h, w, eps=RMS_EPS):
            var = jnp.mean(jnp.square(h), axis=-1, keepdims=True)
            return h * jax.lax.rsqrt(var + eps) * w
        neighbor_sum = jnp.einsum('bnm,bmd->bnd', adjacency, x)
        agg = epsilon * x + neighbor_sum
        h = jnp.einsum('bnd,dh->bnh', agg, W1) + b1
        h = jax.nn.silu(_rmsnorm(h, rms_weight))
        out = jnp.einsum('bnh,hd->bnd', h, W2) + b2
        return out

    def _L0_ffn_ref(x, gamma, beta, Wr, br, W1, b1, W2, b2):
        import jax, jax.numpy as jnp
        import numpy as np
        E = 8
        K = 2
        D = 128
        H = 256
        DOUT = 128
        EPS = 1e-05
        mu = jnp.mean(x, axis=-1, keepdims=True)
        var = jnp.mean(jnp.square(x - mu), axis=-1, keepdims=True)
        xn = (x - mu) * jax.lax.rsqrt(var + EPS) * gamma + beta
        logits = jnp.einsum('bsd,de->bse', xn, Wr) + br
        top_vals, top_idx = jax.lax.top_k(logits, K)
        w = jax.nn.softmax(top_vals, axis=-1)
        w_full = jnp.einsum('bsk,bske->bse', w, jax.nn.one_hot(top_idx, E, dtype=w.dtype))
        y = jnp.zeros(x.shape[:-1] + (DOUT,), x.dtype)
        for e in range(E):
            h = jax.nn.gelu(jnp.einsum('bsd,dh->bsh', xn, W1[e]) + b1[e], approximate=False)
            y_e = jnp.einsum('bsh,hd->bsd', h, W2[e]) + b2[e]
            y = y + y_e * w_full[..., e, None]
        return y

    def _L1_gnn_ref(x, adj, gamma, beta, W_self, W_neigh):
        import jax, jax.numpy as jnp
        import numpy as np
        LN_EPS = 1e-05
        mu = jnp.mean(x, axis=-1, keepdims=True)
        var = jnp.mean(jnp.square(x - mu), axis=-1, keepdims=True)
        xn = (x - mu) * jax.lax.rsqrt(var + LN_EPS) * gamma + beta
        d_out = jnp.sum(adj, axis=1)
        d_in = jnp.sum(adj, axis=2)
        s_out = jnp.where(d_out != 0, jax.lax.rsqrt(d_out), 0.0)
        s_in = jnp.where(d_in != 0, jax.lax.rsqrt(d_in), 0.0)
        A_norm = s_out[:, :, None] * adj * s_in[:, None, :]
        eye = jnp.eye(adj.shape[1], dtype=adj.dtype)
        L = eye[None, :, :] - A_norm
        neighbor = jnp.einsum('bij,bjf->bif', L, xn)
        pre = xn @ W_self + neighbor @ W_neigh
        return jax.nn.softplus(pre)

    def _L1_ffn_ref(x, route_id, Wi, bi, Wr, br, Ws, bs, Wo, bo):
        import jax, jax.numpy as jnp
        import numpy as np
        B, T, IN_DIM = (64, 128, 128)
        HID, OUT_DIM = (256, 128)
        N_LAYERS, N_EXPERTS, N_SHARED = (2, 16, 1)
        flat = x.reshape(-1, x.shape[-1])
        n_tok = flat.shape[0]
        route = jnp.repeat(route_id, n_tok // route_id.shape[0])
        h = jax.nn.relu(flat @ Wi.T + bi)
        n_layers, n_experts = (Wr.shape[0], Wr.shape[1])
        for l in range(n_layers):
            shared = (jnp.einsum('nd,shd->snh', h, Ws[l]) + bs[l][:, None, :]).mean(axis=0)
            routed = jnp.zeros_like(h)
            for e in range(n_experts):
                ye = h @ Wr[l, e].T + br[l, e]
                routed = routed + jnp.where((route == e)[:, None], ye, 0.0)
            h = jax.nn.relu(shared + routed + h)
        out = h @ Wo.T + bo
        return out.reshape(*x.shape[:-1], out.shape[-1])
    x = x + _L0_gnn_ref(_layernorm(x, axis=-1), adj, L0_gnn_epsilon, L0_gnn_W1, L0_gnn_b1, L0_gnn_rms_weight, L0_gnn_W2, L0_gnn_b2)
    x = x + _L0_ffn_ref(_layernorm(x, axis=-1), L0_ffn_gamma, L0_ffn_beta, L0_ffn_Wr, L0_ffn_br, L0_ffn_W1, L0_ffn_b1, L0_ffn_W2, L0_ffn_b2)
    x = x + _L1_gnn_ref(_layernorm(x, axis=-1), adj, L1_gnn_gamma, L1_gnn_beta, L1_gnn_W_self, L1_gnn_W_neigh)
    x = x + _L1_ffn_ref(_layernorm(x, axis=-1), L1_ffn_route_id, L1_ffn_Wi, L1_ffn_bi, L1_ffn_Wr, L1_ffn_br, L1_ffn_Ws, L1_ffn_bs, L1_ffn_Wo, L1_ffn_bo)
    return x

_drawn_inputs = setup_inputs


def setup_inputs(seed=0):
    import zlib

    import numpy as np

    out = dict(_drawn_inputs(seed))
    spreads = {'L0_gnn_b1': (0.0, 0.382),
     'L0_gnn_rms_weight': (1.0, 0.2),
     'L0_gnn_b2': (0.0, 0.1),
     'L0_ffn_br': (0.0, 0.343),
     'L1_gnn_gamma': (1.0, 0.2),
     'L1_gnn_beta': (0.0, 0.396),
     'L1_ffn_bi': (0.0, 0.623),
     'L1_ffn_bo': (0.0, 0.304)}
    factors = {'L0_ffn_gamma': 8.0,
     'L0_ffn_beta': 8.0,
     'L0_ffn_Wr': 4.419,
     'L0_ffn_W1': 2.977,
     'L0_ffn_b1': 8.0,
     'L0_ffn_W2': 2.909,
     'L0_ffn_b2': 6.242,
     'L1_ffn_Wr': 4.471,
     'L1_ffn_br': 8.0,
     'L1_ffn_Ws': 4.571,
     'L1_ffn_bs': 8.0}
    for name, (base, spread) in spreads.items():
        noise = np.random.default_rng([zlib.crc32(name.encode()), seed]).standard_normal(out[name].shape)
        drawn = base * np.exp(spread * noise) if base else spread * noise
        out[name] = jnp.asarray(drawn.astype(out[name].dtype))
    for name, factor in factors.items():
        out[name] = (out[name] * factor).astype(out[name].dtype)
    return out
```

```python
from contextlib import ExitStack

import concourse.bass as bass
from concourse import mybir

ALU = mybir.AluOpType
ACT = mybir.ActivationFunctionType
F32 = mybir.dt.float32
F16 = mybir.dt.float16
BF16 = mybir.dt.bfloat16
I32 = mybir.dt.int32
U32 = mybir.dt.uint32
AX_X = mybir.AxisListType.X

P = 128
B, N, D = 8, 1024, 128
T = B * N // P
TB = N // P
H0 = 512
HC = H0 // P
E, HE = 8, 256
HB = HE // P
TS = 256
NT = (2 * B * N + E * (TS - 1)) // TS
CAP = B * N + TS
L1, E1 = 2, 16
LN_EPS = 1e-5
RMS_EPS = 1e-6
WSCALE = 16.0
UA = 2 * TB
LAG_A = 13
UD = 16
LAG_D = 7


class Tile:

    def __init__(self, base, j, unroll):
        self.n = base * unroll + j
        self.s = j % unroll
        self.g = base * (unroll // TB) + j // TB if unroll >= TB else None
        self.base, self.j = base, j


def lagged(eng, emit, total, unroll, lag):
    def at(step):
        return lambda k: Tile(0, step - k, unroll) if 0 <= step - k < total else None
    first, loops = max(1, -(-lag // unroll)), total // unroll
    for step in range(first * unroll):
        emit(at(step))
    with eng.Fori(first, loops) as base:
        for j in range(unroll):
            emit(lambda k: Tile(base, j - k, unroll))
    for step in range(loops * unroll, total + lag):
        emit(at(step))


def at_least(eng, sem, n):
    if not isinstance(n, int) or n > 0:
        eng.wait_ge(sem, n)


def settled(eng, passed):
    eng.sem_inc(passed, 1)


def row(t, i):
    return t[:, i] if isinstance(i, int) else t[:, bass.ds(i, 1)].rearrange("p a b -> p (a b)")


def build(nc, inp, out, stages="ARBCD"):
    with ExitStack() as ctx:
        def sb(name, shape, dt=F32):
            return ctx.enter_context(nc.sbuf_tensor(name, shape, dt))

        def sem(name):
            return ctx.enter_context(nc.semaphore(name))

        ps = ctx.enter_context(nc.psum_tensor("ps", [P, 8, 512], F32))

        x = sb("x", [P, T, D])
        adjT = sb("adjT", [P, 2, TB, N])
        ident = sb("ident", [P, P])
        ident16 = sb("ident16", [P, P], F16)
        tri = sb("tri", [P, P], BF16)
        ones = sb("ones", [P, P], BF16)
        tri_f = sb("tri_f", [P, P])
        iota_e = sb("iota_e", [P, TB, E])
        ecap = sb("ecap", [P, TB, E])
        mhalf = sb("mhalf", [P, T])
        sel3 = sb("sel3", [P, 3])
        w1 = sb("w1", [P, H0])
        w2 = sb("w2", [P, HC, D])
        rmsw = sb("rmsw", [P, H0])
        epsx = sb("epsx", [P, 1])
        ew1_f = sb("ew1_f", [P, E, HE])
        beta_b = sb("beta_b", [P, P])
        iotap = sb("iotap", [P, 1])
        rows = sb("rows", [3, H0 + 2 * D], BF16)
        gcol = sb("gcol", [P, 3])
        ew1 = sb("ew1", [P, E * 2, HE], F16)
        ew2 = sb("ew2", [P, E, HB * D])
        eb1 = sb("eb1", [P, E * HB])
        eb2 = sb("eb2", [P, E, D])
        rw_f = sb("rw_f", [P, 2, E])
        rw = sb("rw", [P, 2, E], F16)
        rb = sb("rb", [P, TB, E])
        lng = sb("lng", [P, 2, D])
        wsn = sb("wsn", [P, 2, D])
        wi = sb("wi", [P, HE])
        bi = sb("bi", [P, HB])
        ws = sb("ws", [P, L1 * HB, HE])
        bs = sb("bs", [P, L1 * HB])
        btab = sb("btab", [P, L1 * HB, E1])
        wo = sb("wo", [P, HB, D])
        route = sb("route", [1, T], I32)
        din = sb("din", [P, T])
        s_in = sb("s_in", [P, T])
        smask = sb("smask", [P, T])
        gap = sb("gap", [P, T])
        gw = sb("gw", [P, 2, T])
        onehot = sb("onehot", [P, T, 2, E])
        rank = sb("rank", [P, T, E])
        etab = sb("etab", [1, NT], I32)
        btable = sb("btable", [1, NT], I32)
        back = sb("back", [P, T, 2], U32)
        WORK = 10800
        work = sb("work", [P, WORK])

        def carver():
            at = [0]

            def carve(shape, dt=F32):
                n = 1
                for k in shape:
                    n *= k
                words = (n * mybir.dt.size(dt) + 3) // 4
                a = work[:, at[0]:at[0] + words]
                at[0] += words
                assert at[0] <= WORK, at[0]
                if dt != F32:
                    a = a.bitcast(dt)
                names = " ".join("abcd"[:len(shape)])
                return a.rearrange(f"p ({names}) -> p {names}", **dict(zip("abcd", shape)))
            return carve

        xs_rows = nc.dram_tensor("expert_rows", [E * CAP + TS, 2 * D], F16, kind="Internal").ap()
        y_rows = nc.dram_tensor("expert_out", [NT * TS, D], F32, kind="Internal").ap()

        block = ctx.enter_context(nc.Block())

        s_const = sem("s_const")
        s_x0 = sem("s_x0")
        s_x1 = sem("s_x1")
        s_prep_v = sem("s_prep_v")
        s_prep_t = sem("s_prep_t")
        s_adj = [sem("s_adj0"), sem("s_adj1")]
        s_stats = sem("s_stats")
        s_rstd = sem("s_rstd")
        s_norm = sem("s_norm")
        s_agg = sem("s_agg")
        s_aggv = sem("s_aggv")
        s_aggt = sem("s_aggt")
        s_aggc = sem("s_aggc")
        s_h = sem("s_h")
        s_sq = sem("s_sq")
        s_rms = sem("s_rms")
        s_u = sem("s_u")
        s_silu = sem("s_silu")
        s_st = sem("s_st")
        s_stc = sem("s_stc")
        s_y = sem("s_y")
        s_x = sem("s_x")
        s_pc = sem("s_pc")
        s_vc = sem("s_vc")
        s_passed_v = sem("s_passed_v")
        s_passed_p = sem("s_passed_p")
        s_out = sem("s_out")
        c_agg = sem("c_agg")
        c_dout = sem("c_dout")
        c_pc = sem("c_pc")
        c_sin = sem("c_sin")
        c_places = sem("c_places")
        c_comb = sem("c_comb")
        c_stats = sem("c_stats")
        c_pv = sem("c_pv")
        c_rs = sem("c_rs")
        c_q = sem("c_q")
        c_pd = sem("c_pd")
        c_nso = sem("c_nso")
        c_vp = sem("c_vp")
        c_gexp = sem("c_gexp")
        c_v0 = sem("c_v0")
        c_bn = sem("c_bn")
        c_z = sem("c_z")
        c_zg = sem("c_zg")
        c_xn = sem("c_xn")
        c_xs = sem("c_xs")
        c_tr = sem("c_tr")
        c_tc = sem("c_tc")
        c_pre = sem("c_pre")
        c_abs = sem("c_abs")
        c_exp = sem("c_exp")
        c_ln = sem("c_ln")
        c_sp = sem("c_sp")
        c_x = sem("c_x")
        s_const3 = sem("s_const3")
        c_adj = [sem("c_adj0"), sem("c_adj1")]
        c_gath = [sem("c_gath0"), sem("c_gath1")]
        d_wr = [sem(f"d_wr{l}") for l in range(L1)]
        d_bn = sem("d_bn")
        d_stats = sem("d_stats")
        d_pv = sem("d_pv")
        d_rs = sem("d_rs")
        d_z = sem("d_z")
        d_tr = sem("d_tr")
        d_zt = sem("d_zt")
        d_weff = [sem(f"d_weff{l}") for l in range(L1)]
        d_h = [sem(f"d_h{l}") for l in range(L1 + 1)]
        d_r = [sem(f"d_r{l}") for l in range(L1 + 1)]
        d_o = sem("d_o")
        d_x = sem("d_x")
        r_iota = sem("r_iota")
        r_padded = sem("r_padded")
        r_zero = sem("r_zero")
        r_oh = sem("r_oh")
        r_spot = sem("r_spot")
        r_end = sem("r_end")
        r_back = sem("r_back")
        s_const2 = sem("s_const2")
        r_stats = sem("r_stats")
        r_sc = sem("r_sc")
        r_z = sem("r_z")
        r_hi = sem("r_hi")
        r_lo = sem("r_lo")
        r_tr = sem("r_tr")
        r_zt = sem("r_zt")
        r_lg = sem("r_lg")
        r_pick = sem("r_pick")
        r_cum = sem("r_cum")
        r_pos = sem("r_pos")
        r_slot = sem("r_slot")
        r_scat = sem("r_scat")
        r_vc = sem("r_vc")
        r_pc = sem("r_pc")
        r_cnt = sem("r_cnt")
        r_tab = sem("r_tab")
        r_pad = sem("r_pad")
        b_load = [sem(f"b_load{k}") for k in range(6)]
        b_tr = sem("b_tr")
        b_zt = sem("b_zt")
        b_h = sem("b_h")
        b_gelu = sem("b_gelu")
        b_y = sem("b_y")
        b_out = sem("b_out")
        b_store = [sem(f"b_store{k}") for k in range(3)]

        in_ap = inp

        wr = carver()
        z = wr([TB, D])
        zhl = wr([TB, 2 * D], F16)
        zT = wr([TB, 2, P], F16)
        bnR = wr([TB, 6])
        mvR = wr([TB, 2])
        scR = wr([TB])
        logit = wr([TB, E])
        top = wr([TB, 8])
        topi = wr([TB, 8], U32)
        topf = wr([TB, 2])
        pick = wr([TB, E])
        pick16 = wr([TB, E], BF16)
        cum = wr([TB + 1, E])
        cum16 = wr([TB, E], BF16)
        spot = wr([TB, E])
        hit = wr([2, TB, E])
        slot_f = wr([2, TB])
        slot = wr([2, TB], U32)
        cnt_i = wr([E], I32)
        tiles_e = wr([E])
        first_t = wr([E + 1])
        first_r = wr([E])
        pad_f = wr([2, E])
        pad = wr([2, E], U32)
        zrow = wr([2 * D], F16)
        iota_t = wr([NT])
        over = wr([NT, E])
        part = wr([NT, E])
        e_f = wr([NT])
        b_f = wr([NT])
        wr2 = carver()
        wh = wr2([T, E])
        hit2 = wr2([T, 2, E])
        back_f = wr2([T, 2])

        wa = carver()
        rows_f = wa([4, H0 + 2 * D])[0:3]
        xn = wa([UA, D + 1])
        agg_sb = wa([2, D])
        aggT = wa([2, D])
        u = wa([2, H0])
        su = wa([2, H0])
        sT = wa([2, H0])
        junk = wa([H0])
        mvA = wa([4, 2])
        bnA = wa([6])
        rsA = wa([4, 2])
        ssA = wa([4, 2])

        CONST = [
            (ident[:], "c_ident"), (tri_f[:], "c_tri"), (iota_e[:].rearrange("p t e -> p (t e)"), "c_iota"), (ecap[:].rearrange("p t e -> p (t e)"), "c_ecap"),
            (sel3[:], "c_sel3"),
            (w1[:], "w1"), (w2[:].rearrange("p c d -> p (c d)"), "w2"), (rmsw[:], "rmsw"), (epsx[:], "epsx"),
            (rows_f[:, 0, :], "rows"),
            (gcol[:, 0:2], "gcol"), (ew1_f[:].rearrange("p e h -> p (e h)"), "ew1"), (eb1[:], "eb1"),
            (rw_f[:, 0, :], "rw"), (rb[:].rearrange("p t e -> p (t e)"), "rb"), (iotap[:], "c_iotap"),
        ]
        CONST3 = [
            (lng[:].rearrange("p a d -> p (a d)"), "lng"), (wsn[:].rearrange("p a d -> p (a d)"), "wsn"), (wi[:], "wi"), (bi[:], "bi"),
            (ws[:].rearrange("p a h -> p (a h)"), "ws"), (bs[:], "bs"), (btab[:].rearrange("p a e -> p (a e)"), "br"),
            (wo[:].rearrange("p a d -> p (a d)"), "wo"), (route[:], "route"),
        ]
        CONST2 = [
            (ew2[:].rearrange("p e h -> p (e h)"), "ew2"), (eb2[:].rearrange("p e d -> p (e d)"), "eb2"),
        ]

        def stage_r_sp(sp):
            sp.wait_ge(s_x, T)
            sp.dma_start(iota_t[0:1], in_ap["c_iotat"]).then_inc(r_iota, 16)

        def stage_r_dve(dve):
            V = nc.vector
            dve.wait_ge(s_x, T)
            V.memset(zrow, 0.0).then_inc(r_zero, 1)
            CH = 5

            with dve.Fori(0, B) as g:
                base = g * CH
                xg = x[:, bass.ds(g * TB, TB), :]
                for i in range(TB):
                    bn = V.bn_stats(bnR[:, i], xg[:, i])
                bn.then_inc(r_vc, 1)
                dve.wait_ge(r_vc, base + 1)
                settled(dve, s_passed_v)
                for i in range(TB):
                    ag = V.bn_aggr(mvR[:, i], bnR[:, i])
                ag.then_inc(r_stats, 1)
                dve.wait_ge(r_sc, g + 1)
                for i in range(TB):
                    zi = V.tensor_scalar(z[:, i], xg[:, i], mvR[:, i, 0:1], scR[:, i:i + 1], ALU.subtract, ALU.mult)
                zi.then_inc(r_z, 1)
                dve.wait_ge(r_z, g + 1)
                dve.wait_ge(r_hi, g + 1)
                V.tensor_tensor(zhl[:, :, D:2 * D], z, zhl[:, :, 0:D], ALU.subtract).then_inc(r_lo, 1)
                dve.wait_ge(r_lg, g + 1)
                V.scalar_tensor_tensor(logit, ps[:, 2, 0:TB * E].rearrange("p (t e) -> p t e", e=E), 1.0 / WSCALE,
                                       rb[:], ALU.mult, ALU.add).then_inc(r_vc, 1)
                dve.wait_ge(r_vc, base + 2)
                settled(dve, s_passed_v)
                for i in range(TB):
                    mx = V.max(top[:, i], logit[:, i])
                mx.then_inc(r_vc, 1)
                dve.wait_ge(r_vc, base + 3)
                V.tensor_tensor(gap[:, bass.ds(g * TB, TB)], top[:, :, 1], top[:, :, 0], ALU.subtract)
                for i in range(TB):
                    mi = V.max_index(topi[:, i], top[:, i], logit[:, i])
                mi.then_inc(r_vc, 1)
                dve.wait_ge(r_vc, base + 4)
                V.tensor_copy(topf, topi[:, :, 0:2]).then_inc(r_vc, 1)
                dve.wait_ge(r_vc, base + 5)
                oh = onehot[:, bass.ds(g * TB, TB), :, :]
                for k in range(2):
                    eq = V.tensor_tensor(oh[:, :, k, :], iota_e[:], topf[:, :, k:k + 1].to_broadcast([P, TB, E]), ALU.is_equal)
                eq.then_inc(r_oh, 1)
                dve.wait_ge(r_oh, g + 1)
                V.tensor_tensor(pick, oh[:, :, 0, :], oh[:, :, 1, :], ALU.add)
                V.tensor_tensor(pick16, oh[:, :, 0, :], oh[:, :, 1, :], ALU.add).then_inc(r_pick, 1)
                dve.wait_ge(r_pos, g + 1)
                pos = ps[:, 3, 0:TB * E].rearrange("p (t e) -> p t e", e=E)
                V.tensor_copy(rank[:, bass.ds(g * TB, TB), :], pos)
                V.tensor_tensor(spot, pos, ecap[:], ALU.add).then_inc(r_spot, 1)
                dve.wait_ge(r_spot, g * 3 + 1)
                for k in range(2):
                    ht = V.tensor_tensor(hit[:, k], spot, oh[:, :, k, :], ALU.mult)
                ht.then_inc(r_spot, 1)
                dve.wait_ge(r_spot, g * 3 + 2)
                V.tensor_reduce(slot_f, hit, AX_X, ALU.add).then_inc(r_spot, 1)
                dve.wait_ge(r_spot, g * 3 + 3)
                dve.wait_ge(r_scat, g * (2 * TB * 16))
                V.tensor_copy(slot, slot_f).then_inc(r_slot, 1)

            link_n = [0]

            def link(ins):
                link_n[0] += 1
                ins.then_inc(r_end, 1)
                dve.wait_ge(r_end, link_n[0])
            dve.wait_ge(r_cnt, 1)
            cnt = ps[:, 3, 0:E]
            for s in range(TS // P):
                V.tensor_tensor(pad_f[:, s], cnt, ecap[:, 0, :], ALU.add)
            link(V.tensor_scalar(tiles_e, cnt, float(TS - 1), None, ALU.add))
            for s in range(TS // P):
                V.tensor_scalar(pad_f[:, s], pad_f[:, s], iotap[:, 0:1], float(s * P), ALU.add, ALU.add)
            link(V.tensor_copy(cnt_i, tiles_e))
            V.tensor_copy(pad, pad_f).then_inc(r_pad, 1)
            link(V.tensor_single_scalar(cnt_i, cnt_i, TS.bit_length() - 1, ALU.logical_shift_right))
            V.memset(first_t[:, 0:1], 0.0)
            link(V.tensor_copy(tiles_e, cnt_i))
            for e in range(E):
                link(V.tensor_tensor(first_t[:, e + 1:e + 2], first_t[:, e:e + 1], tiles_e[:, e:e + 1], ALU.add))
            it = iota_t[0:1]
            dve.wait_ge(r_iota, 16)
            link(V.tensor_tensor(over[0:1], it.unsqueeze(2).to_broadcast([1, NT, E]),
                                 first_t[0:1, 1:E + 1].unsqueeze(1).to_broadcast([1, NT, E]), ALU.is_ge))
            V.tensor_reduce(e_f[0:1], over[0:1], AX_X, ALU.add)
            link(V.tensor_tensor(part[0:1], over[0:1], tiles_e[0:1].unsqueeze(1).to_broadcast([1, NT, E]), ALU.mult))
            link(V.tensor_reduce(b_f[0:1], part[0:1], AX_X, ALU.add))
            link(V.tensor_tensor(b_f[0:1], it, b_f[0:1], ALU.subtract))
            link(V.tensor_scalar(b_f[0:1], b_f[0:1], float(TS), None, ALU.mult))
            link(V.scalar_tensor_tensor(b_f[0:1], e_f[0:1], float(CAP), b_f[0:1], ALU.mult, ALU.add))
            V.tensor_scalar(btable[:], b_f[0:1], float(E * CAP), None, ALU.min)
            link(V.tensor_scalar(etab[:], e_f[0:1], float(E - 1), None, ALU.min))
            V.engine_nop().then_inc(r_tab, 1)
            link(V.tensor_scalar(first_r, first_t[:, 0:E], float(TS), None, ALU.mult))
            dve.wait_ge(r_scat, B * 2 * TB * 16)
            link(V.tensor_tensor(wh, rank[:], first_r.unsqueeze(1).to_broadcast([P, T, E]), ALU.add))
            for k in range(2):
                ht = V.tensor_tensor(hit2[:, :, k, :], wh, onehot[:, :, k, :], ALU.mult)
            link(ht)
            link(V.tensor_reduce(back_f, hit2, AX_X, ALU.add))
            V.tensor_copy(back[:], back_f).then_inc(r_back, 1)

        def stage_r_pool(pool):
            G = nc.gpsimd
            pool.wait_ge(s_x, T)
            G.memset(cum[:, 0], 0.0).then_inc(r_pc, 1)
            CH = TB + 3

            with pool.Fori(0, B) as g:
                base = g * CH + 1
                pool.wait_ge(r_stats, g + 1)
                settled(pool, s_passed_p)
                G.tensor_scalar(mvR[:, :, 1], mvR[:, :, 1], 1.0 + LN_EPS, LN_EPS * LN_EPS, ALU.mult, ALU.add).then_inc(r_pc, 1)
                pool.wait_ge(r_pc, base + 1)
                G.tensor_tensor(scR, mvR[:, :, 1], mhalf[:, 0:TB], ALU.pow).then_inc(r_sc, 1)
                pool.wait_ge(r_pick, g + 1)
                for t in range(TB):
                    G.tensor_tensor(cum[:, t + 1], cum[:, t], pick[:, t], ALU.add).then_inc(r_pc, 1)
                    pool.wait_ge(r_pc, base + 2 + t)
                    settled(pool, s_passed_p)
                G.tensor_copy(cum16, cum[:, 0:TB]).then_inc(r_pc, 1)
                pool.wait_ge(r_pc, base + TB + 2)
                settled(pool, s_passed_p)
                G.tensor_copy(cum[:, 0], cum[:, TB]).then_inc(r_pc, 1)
                pool.wait_ge(r_pc, base + TB + 3)
                settled(pool, s_passed_p)
                G.engine_nop().then_inc(r_cum, 1)
                pool.wait_ge(r_slot, g + 1)
                settled(pool, s_passed_p)
                for t in range(TB):
                    for k in range(2):
                        G.indirect_dma_start(xs_rows, bass.IndirectOffsetOnAxis(slot[:, k, t:t + 1], 0),
                                             zhl[:, t, :], None).then_inc(r_scat, 16)
            pool.wait_ge(r_pos, B)
            settled(pool, s_passed_p)
            G.tensor_copy(cum16[:, 0], cum[:, 0]).then_inc(r_cum, 1)
            pool.wait_ge(r_zero, 1)
            for s in range(TS // P):
                G.dma_start(xs_rows[E * CAP + s * P:E * CAP + (s + 1) * P, :], zrow).then_inc(r_padded, 16)
            pool.wait_ge(r_pad, 1)
            for s in range(TS // P):
                for e in range(E):
                    G.indirect_dma_start(xs_rows, bass.IndirectOffsetOnAxis(pad[:, s, e:e + 1], 0), zrow, None).then_inc(r_padded, 16)

        SCATTERED = 16 * B * 2 * TB
        PADDED = 16 * TS // P * (E + 1)

        def stage_r_act(act):
            S = nc.scalar
            act.wait_ge(s_x, T)
            with act.Fori(0, B) as g:
                act.wait_ge(r_z, g + 1)
                act.wait_ge(r_scat, g * (2 * TB * 16))
                S.copy(zhl[:, :, 0:D], z).then_inc(r_hi, 1)
                act.wait_ge(r_tr, g + 1)
                S.copy(zT.rearrange("p t s q -> p (t s q)"), ps[:, 0:2].rearrange("p a b -> p (a b)").bitcast(F16)).then_inc(r_zt, 1)

        def stage_r_pe(pe):
            M = nc.tensor
            pe.wait_ge(s_x, T)
            tr = ps[:, 0:2].rearrange("p a b -> p (a b)").bitcast(F16).rearrange("p (t s q) -> p t s q", t=TB, s=2)
            with pe.Fori(0, B) as g:
                pe.wait_ge(r_lo, g + 1)
                for t in range(TB):
                    for s in range(2):
                        mm = M.transpose(tr[:, t, s], zhl[:, t, s * D:(s + 1) * D], ident16[:])
                mm.then_inc(r_tr, 1)
                pe.wait_ge(r_zt, g + 1)
                for t in range(TB):
                    for n, (a, b) in enumerate(((0, 0), (1, 0), (0, 1))):
                        mm = M.matmul(ps[:, 2, t * E:(t + 1) * E], zT[:, t, a], rw[:, b], start=(n == 0), stop=(n == 2))
                mm.then_inc(r_lg, 1)
                pe.wait_ge(r_pick, g + 1)
                pos = ps[:, 3, 0:TB * E]
                M.matmul(pos, tri[:], pick16.rearrange("p t e -> p (t e)"), start=True, stop=False)
                pe.wait_ge(r_cum, g + 1)
                M.matmul(pos, ones[:], cum16.rearrange("p t e -> p (t e)"), start=False, stop=True).then_inc(r_pos, 1)
            pe.wait_ge(r_cum, B + 1)
            pe.wait_ge(r_slot, B)
            M.matmul(ps[:, 3, 0:E], ones[:], cum16[:, 0], start=True, stop=True).then_inc(r_cnt, 1)

        wb = carver()
        zin = wb([6, TS // P, 2 * D], F16)
        zTb = wb([2, 2, TS], F16)
        hT = wb([2, HB, TS])
        yo = wb([3, TS // P, D])
        UB = 12

        def stage_b_sp(sp):
            sp.wait_ge(r_tab, 1)
            sp.wait_ge(r_scat, SCATTERED)
            sp.wait_ge(r_padded, PADDED)
            sp.wait_ge(r_back, 1)

            def emit(tile):
                if t := tile(0):
                    b = t.s % 6
                    at_least(sp, b_tr, t.n - 5)
                    row0 = sp.value_load(btable[0:1, bass.ds(t.n, 1)], min_val=0, max_val=E * CAP)
                    sp.dma_start(zin[:, b], xs_rows[bass.ds(row0, TS), :].rearrange("(s p) c -> p s c", p=P)).then_inc(b_load[b], 16)
            lagged(sp, emit, NT, UB, 0)

        def stage_b_pool(pool):
            def emit(tile):
                if t := tile(0):
                    b = t.s % 3
                    pool.wait_ge(b_out, t.n + 1)
                    nc.gpsimd.dma_start(y_rows[bass.ds(t.n * TS, TS), :].rearrange("(s p) c -> p s c", p=P), yo[:, b]).then_inc(b_store[b], 16)
            lagged(pool, emit, NT, UB, 0)

        def stage_b_pe(pe):
            M = nc.tensor

            pe.wait_ge(r_tab, 1)
            pe.wait_ge(s_const2, 16 * len(CONST2))

            def emit(tile):
                if t := tile(0):
                    b = t.s % 6
                    pe.wait_ge(b_load[b], uses_of(t, 6))
                    at_least(pe, b_zt, t.n - 1)
                    tr = ps[:, t.s % 2].bitcast(F16)[:, 0:2 * TS].rearrange("p (h q) -> p h q", h=2)
                    for s in range(TS // P):
                        for h in range(2):
                            mm = M.transpose(tr[:, h, s * P:(s + 1) * P], zin[:, b, s, h * D:(h + 1) * D], ident16[:])
                    mm.then_inc(b_tr, 1)
                if t := tile(1):
                    e = pe.value_load(etab[0:1, bass.ds(t.n, 1)], min_val=0, max_val=E - 1)
                    pe.wait_ge(b_zt, t.n + 1)
                    at_least(pe, b_gelu, t.n - 1)
                    for c in range(HB):
                        for n, (a, w) in enumerate(((0, 0), (0, 1), (1, 0))):
                            mm = M.matmul(ps[:, 2 + t.s % 2, c * TS:(c + 1) * TS],
                                          ew1[:, bass.ds(e * 2 + w, 1), c * P:(c + 1) * P].rearrange("p a b -> p (a b)"),
                                          zTb[:, t.s % 2, a], start=(n == 0), stop=(n == 2))
                    mm.then_inc(b_h, 1)
                if t := tile(2):
                    e = pe.value_load(etab[0:1, bass.ds(t.n, 1)], min_val=0, max_val=E - 1)
                    pe.wait_ge(b_gelu, t.n + 1)
                    at_least(pe, b_out, t.n - 1)
                    for s in range(TS // P):
                        for c in range(HB):
                            mm = M.matmul(ps[:, 4 + t.s % 2, s * D:(s + 1) * D], hT[:, t.s % 2, c, s * P:(s + 1) * P],
                                          ew2[:, bass.ds(e, 1), c * D:(c + 1) * D].rearrange("p a b -> p (a b)"),
                                          start=(c == 0), stop=(c == HB - 1))
                    mm.then_inc(b_y, 1)
            lagged(pe, emit, NT, UB, 2)

        def stage_b_act(act):
            S = nc.scalar
            act.wait_ge(r_tab, 1)
            act.wait_ge(r_back, 1)

            def emit(tile):
                if t := tile(1):
                    e = act.value_load(etab[0:1, bass.ds(t.n, 1)], min_val=0, max_val=E - 1)
                    act.wait_ge(b_h, t.n + 1)
                    at_least(act, b_y, t.n - 1)
                    for c in range(HB):
                        ge = S.activation(hT[:, t.s % 2, c], ps[:, 2 + t.s % 2, c * TS:(c + 1) * TS], ACT.Gelu,
                                          bias=eb1[:, bass.ds(e * HB + c, 1)], scale=1.0 / WSCALE)
                    ge.then_inc(b_gelu, 1)
            lagged(act, emit, NT, UB, 1)

        def stage_b_dve(dve):
            V = nc.vector

            def emit(tile):
                if t := tile(0):
                    dve.wait_ge(b_tr, t.n + 1)
                    at_least(dve, b_h, t.n - 1)
                    V.tensor_copy(zTb[:, t.s % 2].rearrange("p h q -> p (h q)"), ps[:, t.s % 2].bitcast(F16)[:, 0:2 * TS]).then_inc(b_zt, 1)
                if t := tile(2):
                    e = dve.value_load(etab[0:1, bass.ds(t.n, 1)], min_val=0, max_val=E - 1)
                    dve.wait_ge(b_y, t.n + 1)
                    if not (isinstance(t.n, int) and t.n < 3):
                        dve.wait_ge(b_store[t.s % 3], uses_of(t, 3) - 16)
                    V.tensor_tensor(yo[:, t.s % 3], ps[:, 4 + t.s % 2, 0:2 * D].rearrange("p (s d) -> p s d", d=D),
                                    eb2[:, bass.ds(e, 1), :].to_broadcast([P, TS // P, D]), ALU.add).then_inc(b_out, 1)
            lagged(dve, emit, NT, UB, 2)

        def uses_of(t, ring):
            return 16 * (t.n // ring + 1) if isinstance(t.n, int) else t.base * (16 * UB // ring) + 16 * (t.j // ring + 1)

        wc = carver()
        yg = wc([2, TB, 2, D])
        xnC = wc([2, TB, D])
        xsC = wc([2, TB, D])
        qC = wc([2, D])
        qxT = wc([2, 2 * D])
        soft = wc([TB, D])
        junkC = wc([N], BF16)
        bnC = wc([TB, 6])
        mvC = wc([TB, 2])
        rsC = wc([TB])
        dout = wc([2, TB])
        zero_d = wc([TB])
        nso = wc([2, TB])
        gexp = wc([T])
        places = wc([2, TB, 2], U32)
        gden = wc([T])
        FRONT, MAIN = TB, 2 * TB
        LAG_C = MAIN + 15

        def graph_loads(t):
            return (t.g - (t.s // TB)) // 2 + 1 if isinstance(t.n, int) else t.base + t.j // UA + 1

        def stage_c_sp(sp):
            sp.wait_ge(s_agg, T)
            for p in range(2):
                sp.dma_start(adjT[:, p], in_ap["adjT"][p]).then_inc(c_adj[p], 16)
            for dst, name in CONST3:
                sp.dma_start(dst, in_ap[name]).then_inc(s_const3, 16)

        def stage_c_sp_loop(sp):
            with sp.Fori(1, B // 2) as bb:
                for p in range(2):
                    sp.wait_ge(c_agg, (bb * 2 + p - 1) * TB)
                    sp.wait_ge(c_dout, (bb * 2 + p - 1) * TB)
                    sp.dma_start(adjT[:, p], in_ap["adjT"][bass.ds(bb * 2 + p, 1)].rearrange("g p m n -> (g p) m n")).then_inc(c_adj[p], 16)

        def b_is_over(eng):
            eng.wait_ge(b_out, NT)
            for k in range(3):
                eng.wait_ge(b_store[k], 16 * len(range(k, NT, 3)))

        def stage_c_pool(pool):
            G = nc.gpsimd
            b_is_over(pool)
            chain = [0]

            def link(ins):
                chain[0] += 1
                ins.then_inc(c_pc, 1)
                pool.wait_ge(c_pc, chain[0])
                settled(pool, s_passed_p)
            link(G.tensor_scalar(smask[:], din[:], 0.0, None, ALU.is_equal))
            link(G.tensor_tensor(s_in[:], din[:], smask[:], ALU.add))
            link(G.tensor_tensor(s_in[:], s_in[:], mhalf[:], ALU.pow))
            link(G.tensor_scalar(smask[:], smask[:], -1.0, 1.0, ALU.mult, ALU.add))
            G.tensor_tensor(s_in[:], s_in[:], smask[:], ALU.mult).then_inc(c_sin, 1)

            def emit(tile):
                if t := tile(0):
                    par, i = t.s // TB, t.s % TB
                    if i == 0:
                        at_least(pool, c_comb, t.g - 1)
                        settled(pool, s_passed_p)
                        G.tensor_copy(places[:, par], back[:, bass.ds(t.n, TB), :]).then_inc(c_places, 1)
                        pool.wait_ge(c_places, t.g + 1)
                        settled(pool, s_passed_p)
                    for k in range(2):
                        G.indirect_dma_start(yg[:, par, i, k, :], None, y_rows,
                                             bass.IndirectOffsetOnAxis(places[:, par, i, k:k + 1], 0)).then_inc(c_gath[par], 16)
                if (t := tile(FRONT)) and t.s % TB == 3:
                    pool.wait_ge(c_stats, t.g + 1)
                    settled(pool, s_passed_p)
                    G.tensor_scalar(mvC[:, :, 1], mvC[:, :, 1], 1.0 + LN_EPS, LN_EPS * LN_EPS, ALU.mult, ALU.add).then_inc(c_pv, 1)
                    pool.wait_ge(c_pv, t.g + 1)
                    G.tensor_tensor(rsC, mvC[:, :, 1], mhalf[:, 0:TB], ALU.pow).then_inc(c_rs, 1)
                if (t := tile(MAIN)) and t.s % TB == 0:
                    par = t.s // TB
                    pool.wait_ge(c_dout, (t.g + 1) * TB)
                    at_least(pool, c_q, (t.g - 1) * TB)
                    settled(pool, s_passed_p)
                    G.tensor_scalar(zero_d, dout[:, par], 0.0, None, ALU.is_equal).then_inc(c_pd, 1)
                    pool.wait_ge(c_pd, t.g * 4 + 1)
                    G.tensor_tensor(nso[:, par], dout[:, par], zero_d, ALU.add).then_inc(c_pd, 1)
                    pool.wait_ge(c_pd, t.g * 4 + 2)
                    G.tensor_tensor(nso[:, par], nso[:, par], mhalf[:, 0:TB], ALU.pow).then_inc(c_pd, 1)
                    G.tensor_scalar(zero_d, zero_d, -1.0, None, ALU.add).then_inc(c_pd, 1)
                    pool.wait_ge(c_pd, t.g * 4 + 4)
                    G.tensor_tensor(nso[:, par], nso[:, par], zero_d, ALU.mult).then_inc(c_nso, 1)
            lagged(pool, emit, T, UA, LAG_C)

        def stage_c_dve(dve):
            V = nc.vector
            chain = [0]

            def link(ins):
                chain[0] += 1
                ins.then_inc(c_vp, 1)
                dve.wait_ge(c_vp, chain[0])
            dve.wait_ge(s_const3, 16 * len(CONST3))
            V.tensor_tensor(wsn[:, 0], wsn[:, 0], wsn[:, 1], ALU.add)
            for l in range(L1):
                for c in range(HB):
                    k = l * HB + c
                    V.tensor_tensor(ws[:, k, c * P:(c + 1) * P], ws[:, k, c * P:(c + 1) * P], ident[:], ALU.add)
            V.tensor_tensor(btab[:], btab[:], bs[:].unsqueeze(2).to_broadcast([P, L1 * HB, E1]), ALU.add)
            dve.wait_ge(c_gexp, 1)
            link(V.tensor_scalar(gden, gexp, 1.0, None, ALU.add))
            link(V.reciprocal(gw[:, 0], gden))
            link(V.tensor_tensor(gw[:, 1], gw[:, 0], gexp, ALU.mult))

            def emit(tile):
                if t := tile(FRONT):
                    par, i = t.s // TB, t.s % TB
                    tiles = [t.n - i + k for k in range(TB)]
                    if i < 2:
                        if i == 0:
                            dve.wait_ge(c_gath[par], graph_loads(t) * (2 * TB * 16))
                        else:
                            dve.wait_ge(c_v0, t.g + 1)
                        for k in range(TB):
                            ins = V.scalar_tensor_tensor(row(x, tiles[k]), yg[:, par, k, i], gw[:, i, bass.ds(tiles[k], 1)],
                                                         row(x, tiles[k]), ALU.mult, ALU.add)
                        ins.then_inc(c_v0 if i == 0 else c_comb, 1)
                    elif i == 2:
                        dve.wait_ge(c_comb, t.g + 1)
                        settled(dve, s_passed_v)
                        for k in range(TB):
                            ins = V.bn_stats(bnC[:, k], row(x, tiles[k]))
                        ins.then_inc(c_bn, 1)
                    elif i == 3:
                        dve.wait_ge(c_bn, t.g + 1)
                        settled(dve, s_passed_v)
                        for k in range(TB):
                            ins = V.bn_aggr(mvC[:, k], bnC[:, k])
                        ins.then_inc(c_stats, 1)
                    elif i == 4:
                        dve.wait_ge(c_rs, t.g + 1)
                        at_least(dve, c_tr, (t.g - 1) * TB)
                        for k in range(TB):
                            ins = V.tensor_scalar(xnC[:, par, k], row(x, tiles[k]), mvC[:, k, 0:1], rsC[:, k:k + 1],
                                                  ALU.subtract, ALU.mult)
                        ins.then_inc(c_z, 1)
                    elif i == 5:
                        dve.wait_ge(c_z, t.g + 1)
                        V.tensor_tensor(xnC[:, par], xnC[:, par], lng[:, 0:1].to_broadcast([P, TB, D]), ALU.mult).then_inc(c_zg, 1)
                    elif i == 6:
                        dve.wait_ge(c_zg, t.g + 1)
                        V.tensor_tensor(xnC[:, par], xnC[:, par], lng[:, 1:2].to_broadcast([P, TB, D]), ALU.add).then_inc(c_xn, 1)
                    else:
                        dve.wait_ge(c_xn, t.g + 1)
                        dve.wait_ge(c_sin, 1)
                        at_least(dve, c_agg, (t.g - 1) * TB)
                        for k in range(TB):
                            ins = V.tensor_scalar(xsC[:, par, k], xnC[:, par, k], s_in[:, bass.ds(tiles[k], 1)], None, ALU.mult)
                        ins.then_inc(c_xs, 1)
                if t := tile(MAIN):
                    par, i = t.s // TB, t.s % TB
                    dve.wait_ge(c_agg, t.n + 1)
                    dve.wait_ge(c_nso, t.g + 1)
                    at_least(dve, c_tr, t.n - 1)
                    V.tensor_scalar(qC[:, t.s % 2], ps[:, t.s % 2, 0:D], nso[:, par, i:i + 1], None, ALU.mult).then_inc(c_q, 1)
                if (t := tile(MAIN + 14)) and t.s % TB == 0:
                    b0 = 4 + 2 * (t.s // TB)
                    dve.wait_ge(c_ln, t.g + 1)
                    V.scalar_tensor_tensor(soft.rearrange("p t d -> p (t d)"), ps[:, b0:b0 + 2].rearrange("p a b -> p (a b)"), 0.0,
                                           soft.rearrange("p t d -> p (t d)"), ALU.max, ALU.add).then_inc(c_sp, 1)
                if (t := tile(MAIN + 15)) and t.s % TB == 0:
                    dve.wait_ge(c_sp, t.g + 1)
                    xg = x[:, bass.ds(t.n, TB), :]
                    V.tensor_tensor(xg, xg, soft, ALU.add).then_inc(c_x, 1)
            lagged(dve, emit, T, UA, LAG_C)

        def stage_c_act(act):
            S = nc.scalar
            b_is_over(act)
            S.activation(gexp, gap[:], ACT.Exp).then_inc(c_gexp, 1)

            def emit(tile):
                if t := tile(FRONT):
                    par, i = t.s // TB, t.s % TB
                    if i == 0:
                        act.wait_ge(c_adj[par], graph_loads(t) * 16)
                        at_least(act, c_nso, t.g - 1)
                    at_least(act, c_dout, t.n)
                    S.activation(junkC, adjT[:, par, i], ACT.Identity, accum_out=dout[:, par, i:i + 1]).then_inc(c_dout, 1)
                if t := tile(MAIN + 1):
                    act.wait_ge(c_tr, t.n + 1)
                    at_least(act, c_pre, t.n - 1)
                    S.copy(qxT[:, t.s % 2], ps[:, 2 + t.s % 2, 0:2 * D]).then_inc(c_tc, 1)
                sf = soft.rearrange("p t d -> p (t d)")
                if (t := tile(MAIN + 10)) and t.s % TB == 0:
                    b0 = 4 + 2 * (t.s // TB)
                    act.wait_ge(c_pre, (t.g + 1) * TB)
                    at_least(act, c_x, t.g)
                    S.activation(sf, ps[:, b0:b0 + 2].rearrange("p a b -> p (a b)"), ACT.Abs).then_inc(c_abs, 1)
                if (t := tile(MAIN + 11)) and t.s % TB == 0:
                    act.wait_ge(c_abs, t.g + 1)
                    S.activation(sf, sf, ACT.Exp, scale=-1.0).then_inc(c_exp, 1)
                if (t := tile(MAIN + 13)) and t.s % TB == 0:
                    act.wait_ge(c_exp, t.g + 1)
                    S.activation(sf, sf, ACT.Ln, bias=1.0).then_inc(c_ln, 1)
            lagged(act, emit, T, UA, LAG_C)

        def stage_c_pe(pe):
            M = nc.tensor
            b_is_over(pe)

            def emit(tile):
                if t := tile(MAIN + 1):
                    par, i = t.s // TB, t.s % TB
                    pe.wait_ge(c_q, t.n + 1)
                    at_least(pe, c_tc, t.n - 1)
                    M.transpose(ps[:, 2 + t.s % 2, 0:D], xnC[:, par, i], ident[:])
                    M.transpose(ps[:, 2 + t.s % 2, D:2 * D], qC[:, t.s % 2], ident[:]).then_inc(c_tr, 1)
                if t := tile(MAIN):
                    par, i = t.s // TB, t.s % TB
                    pe.wait_ge(c_xs, t.g + 1)
                    at_least(pe, c_q, t.n - 1)
                    for m in range(TB):
                        mm = M.matmul(ps[:, t.s % 2, 0:D], adjT[:, par, m, i * P:(i + 1) * P], xsC[:, par, m],
                                      start=(m == 0), stop=(m == TB - 1))
                    mm.then_inc(c_agg, 1)
                if t := tile(MAIN + 2):
                    par, i = t.s // TB, t.s % TB
                    pe.wait_ge(c_tc, t.n + 1)
                    if i == 0:
                        at_least(pe, c_x, t.g - 1)
                    o = ps[:, 4 + 2 * par + i // 4, (i % 4) * D:(i % 4 + 1) * D]
                    M.matmul(o, qxT[:, t.s % 2, 0:D], wsn[:, 0], start=True, stop=False)
                    M.matmul(o, qxT[:, t.s % 2, D:2 * D], wsn[:, 1], start=False, stop=True).then_inc(c_pre, 1)
            lagged(pe, emit, T, UA, LAG_C)

        wd = carver()
        zD = wd([2, D])
        zTD = wd([2, D])
        hD = [wd([2, HB * P]) for _ in range(L1 + 1)]
        weff = [wd([2, HB, HE]) for _ in range(L1)]
        bnD = wd([2, 6])
        mvD = wd([4, 2])
        rsD = wd([4])

        def stage_d_sp(sp):
            for l in range(L1):
                sp.wait_ge(c_agg, T - (L1 - 1 - l) * TB)
                sp.wait_ge(c_dout, T - (L1 - 1 - l) * TB)
                sp.dma_start(adjT[:, l].rearrange("p a b -> p (a b)"), in_ap["wr"][:, l]).then_inc(d_wr[l], 16)

        def stage_d_out(sp):
            with sp.Fori(0, T // UD) as b:
                sp.wait_ge(d_x, (b + 1) * UD)
                sp.dma_start(out[:, bass.ds(b * UD, UD), :], x[:, bass.ds(b * UD, UD), :]).then_inc(s_out, 16)
            sp.wait_ge(s_out, 16 * (T // UD))

        def stage_d_dve(dve):
            V = nc.vector
            dve.wait_ge(c_x, B)
            wrv = [adjT[:, l].rearrange("p a b -> p (a b)").rearrange("p (e c h) -> p e c h", e=E1, c=HB) for l in range(L1)]

            def emit(tile):
                if t := tile(0):
                    V.bn_stats(bnD[:, t.s % 2], row(x, t.n)).then_inc(d_bn, 1)
                    dve.wait_ge(d_bn, t.n + 1)
                    settled(dve, s_passed_v)
                    V.bn_aggr(mvD[:, t.s % 4], bnD[:, t.s % 2]).then_inc(d_stats, 1)
                if t := tile(1):
                    dve.wait_ge(d_rs, t.n + 1)
                    at_least(dve, d_tr, t.n - 1)
                    V.tensor_scalar(zD[:, t.s % 2], row(x, t.n), mvD[:, t.s % 4, 0:1], rsD[:, t.s % 4:t.s % 4 + 1],
                                    ALU.subtract, ALU.mult).then_inc(d_z, 1)
                for l in range(L1):
                    if t := tile(3 + l):
                        e = dve.value_load(route[0:1, bass.ds(t.n, 1)], min_val=0, max_val=E1 - 1)
                        if isinstance(t.n, int):
                            dve.wait_ge(d_wr[l], 16)
                        at_least(dve, d_h[l + 1], t.n - 1)
                        V.tensor_tensor(weff[l][:, t.s % 2], wrv[l][:, bass.ds(e, 1)].rearrange("p a c h -> p (a c) h"),
                                        ws[:, l * HB:(l + 1) * HB], ALU.add).then_inc(d_weff[l], 1)
                if t := tile(7):
                    dve.wait_ge(d_o, t.n + 1)
                    V.tensor_tensor(row(x, t.n), row(x, t.n), ps[:, 6 + t.s % 2, 0:D], ALU.add).then_inc(d_x, 1)
            lagged(dve, emit, T, UD, LAG_D)

        def stage_d_pool(pool):
            G = nc.gpsimd
            pool.wait_ge(c_x, B)

            def emit(tile):
                if t := tile(0):
                    pool.wait_ge(d_stats, t.n + 1)
                    at_least(pool, d_z, t.n - 3)
                    settled(pool, s_passed_p)
                    G.tensor_scalar(mvD[:, t.s % 4, 1:2], mvD[:, t.s % 4, 1:2], LN_EPS, None, ALU.add).then_inc(d_pv, 1)
                    pool.wait_ge(d_pv, t.n + 1)
                    G.tensor_tensor(rsD[:, t.s % 4:t.s % 4 + 1], mvD[:, t.s % 4, 1:2], mhalf[:, 0:1], ALU.pow).then_inc(d_rs, 1)
            lagged(pool, emit, T, UD, LAG_D)

        def stage_d_act(act):
            S = nc.scalar
            act.wait_ge(c_x, B)

            def emit(tile):
                if t := tile(2):
                    act.wait_ge(d_tr, t.n + 1)
                    at_least(act, d_h[0], t.n - 1)
                    S.copy(zTD[:, t.s % 2], ps[:, 0, 0:P]).then_inc(d_zt, 1)
                for l in range(L1 + 1):
                    if t := tile(3 + l):
                        if l:
                            e = act.value_load(route[0:1, bass.ds(t.n, 1)], min_val=0, max_val=E1 - 1)
                        act.wait_ge(d_h[l], t.n + 1)
                        at_least(act, d_h[l + 1] if l < L1 else d_o, t.n - 1)
                        for c in range(HB):
                            src = (ps[:, 1, c * P:(c + 1) * P] if l == 0 else
                                   ps[:, 2 * l + t.s % 2, c * P:(c + 1) * P])
                            bias = bi[:, c:c + 1] if l == 0 else btab[:, (l - 1) * HB + c, bass.ds(e, 1)]
                            ins = S.activation(hD[l][:, t.s % 2, c * P:(c + 1) * P], src, ACT.Relu, bias=bias)
                        ins.then_inc(d_r[l], 1)
            lagged(act, emit, T, UD, LAG_D)

        def stage_d_pe(pe):
            M = nc.tensor
            pe.wait_ge(c_x, B)

            def emit(tile):
                if t := tile(2):
                    pe.wait_ge(d_z, t.n + 1)
                    at_least(pe, d_zt, t.n)
                    M.transpose(ps[:, 0, 0:P], zD[:, t.s % 2], ident[:]).then_inc(d_tr, 1)
                if t := tile(3):
                    pe.wait_ge(d_zt, t.n + 1)
                    at_least(pe, d_r[0], t.n)
                    for c in range(HB):
                        mm = M.matmul(ps[:, 1, c * P:(c + 1) * P], wi[:, c * P:(c + 1) * P],
                                      zTD[:, t.s % 2], start=True, stop=True)
                    mm.then_inc(d_h[0], 1)
                for l in range(L1):
                    if t := tile(4 + l):
                        pe.wait_ge(d_weff[l], t.n + 1)
                        pe.wait_ge(d_r[l], t.n + 1)
                        at_least(pe, d_r[l + 1], t.n - 1)
                        for c in range(HB):
                            for k in range(HB):
                                mm = M.matmul(ps[:, 2 + 2 * l + t.s % 2, c * P:(c + 1) * P], weff[l][:, t.s % 2, k, c * P:(c + 1) * P],
                                              hD[l][:, t.s % 2, k * P:(k + 1) * P], start=(k == 0), stop=(k == HB - 1))
                        mm.then_inc(d_h[l + 1], 1)
                if t := tile(6):
                    pe.wait_ge(d_r[L1], t.n + 1)
                    at_least(pe, d_x, t.n - 1)
                    o = ps[:, 6 + t.s % 2, 0:D]
                    for k in range(HB):
                        M.matmul(o, hD[L1][:, t.s % 2, k * P:(k + 1) * P], wo[:, k], start=(k == 0), stop=False)
                    M.matmul(o, ones[0:3, :], rows[:, H0 + D:H0 + 2 * D], start=False, stop=True).then_inc(d_o, 1)
            lagged(pe, emit, T, UD, LAG_D)


        @block.sync
        def _(sp):
            for dst, name in CONST:
                sp.dma_start(dst, in_ap[name]).then_inc(s_const, 16)
            half = 2 * TB
            sp.dma_start(x[:, 0:half, :], in_ap["x"][:, 0:half, :]).then_inc(s_x0, 16)
            sp.dma_start(x[:, half:T, :], in_ap["x"][:, half:T, :]).then_inc(s_x1, 16)

            def load(g, p, first):
                if not first:
                    sp.wait_ge(s_agg, (g - 1) * TB)
                sp.dma_start(adjT[:, p], in_ap["adjT"][bass.ds(g, 1)].rearrange("g p m n -> (g p) m n")).then_inc(s_adj[p], 16)
            load(0, 0, True)
            load(1, 1, True)
            with sp.Fori(1, B // 2) as bb:
                load(bb * 2, 0, False)
                load(bb * 2 + 1, 1, False)
            for dst, name in CONST2:
                sp.dma_start(dst, in_ap[name]).then_inc(s_const2, 16)
            if "R" in stages:
                stage_r_sp(sp)
            if "C" in stages:
                stage_c_sp(sp)
            if "B" in stages:
                stage_b_sp(sp)
            if "C" in stages:
                stage_c_sp_loop(sp)
            if stages[-1] == "C":
                sp.wait_ge(c_x, B)
                sp.dma_start(out, x[:]).then_inc(s_out, 16)
                sp.wait_ge(s_out, 16)
            if "D" in stages:
                stage_d_sp(sp)
                stage_d_out(sp)
            if stages[-1] in "ARB":
                sp.wait_ge(s_x, T)
                sp.dma_start(out, x[:]).then_inc(s_out, 16)
                sp.wait_ge(s_out, 16)

        @block.vector
        def _(dve):
            link_n = [0]

            def link(ins):
                link_n[0] += 1
                ins.then_inc(s_prep_v, 1)
                dve.wait_ge(s_prep_v, link_n[0])

            V = nc.vector
            V.memset(mhalf[:], -0.5)
            V.memset(ones[:], 1.0)
            link(V.memset(xn, 1.0))
            dve.wait_ge(s_const, 16 * len(CONST))
            link(V.tensor_copy(tri[:], tri_f[:]))
            V.tensor_copy(ident16[:], ident[:])
            bf = rows[:]
            src, a, b, c = (rows_f[:, k, :] for k in range(4))
            link(V.tensor_copy(bf, src))
            link(V.tensor_copy(a, bf))
            link(V.tensor_tensor(b, src, a, ALU.subtract))
            link(V.tensor_scalar(c, a, sel3[0:3, 0:1], None, ALU.mult))
            link(V.tensor_copy(bf, b))
            link(V.tensor_copy(a, bf))
            link(V.tensor_tensor(b, b, a, ALU.subtract))
            link(V.scalar_tensor_tensor(c, a, sel3[0:3, 1:2], c, ALU.mult, ALU.add))
            link(V.scalar_tensor_tensor(c, b, sel3[0:3, 2:3], c, ALU.mult, ALU.add))
            link(V.tensor_copy(bf, c))
            link(V.tensor_scalar(beta_b[:], ident[:], 0.0, gcol[:, 1:2], ALU.mult, ALU.add))
            link(V.tensor_scalar(gcol[:, 2:3], gcol[:, 0:1], WSCALE, None, ALU.mult))
            dve.wait_ge(s_prep_t, 1)
            V.tensor_tensor(eb1[:], eb1[:], ps[:, 7, 0:E * HB], ALU.add)
            V.tensor_tensor(rb[:], rb[:], ps[:, 7, E * HB:E * HB + E].unsqueeze(1).to_broadcast([P, TB, E]), ALU.add)
            link(V.tensor_scalar(ew1_f[:], ew1_f[:], gcol[:, 2:3], None, ALU.mult))
            link(V.tensor_scalar(rw_f[:, 0, :], rw_f[:, 0, :], gcol[:, 2:3], None, ALU.mult))
            ew1v = ew1[:].rearrange("p (e s) h -> p e s h", s=2)
            link(V.tensor_copy(ew1v[:, :, 0, :], ew1_f[:]))
            V.tensor_tensor(ew1v[:, :, 1, :], ew1_f[:], ew1v[:, :, 0, :], ALU.subtract)
            link(V.tensor_copy(rw[:, 0, :], rw_f[:, 0, :]))
            link(V.tensor_tensor(rw[:, 1, :], rw_f[:, 0, :], rw[:, 0, :], ALU.subtract))

            def emit(tile):
                if t := tile(11):
                    dve.wait_ge(s_rms, t.n + 1)
                    at_least(dve, s_silu, t.n - 1)
                    V.scalar_tensor_tensor(u[:, t.s % 2], ps[:, 3 + t.s % 2], rsA[:, t.s % 4, 1:2], rmsw[:],
                                           ALU.mult, ALU.mult).then_inc(s_u, 1)
                if t := tile(1):
                    dve.wait_ge(s_rstd, t.n + 1)
                    at_least(dve, s_agg, (t.g - 1) * TB)
                    V.tensor_scalar(xn[:, t.s, 0:D], row(x, t.n), mvA[:, t.s % 4, 0:1], rsA[:, t.s % 4, 0:1],
                                    ALU.subtract, ALU.mult).then_inc(s_norm, 1)
                if t := tile(0):
                    dve.wait_ge(s_x1 if not isinstance(t.n, int) else s_x0, 16)
                    V.bn_stats(bnA, row(x, t.n)).then_inc(s_vc, 1)
                    dve.wait_ge(s_vc, t.n + 1)
                    settled(dve, s_passed_v)
                    V.bn_aggr(mvA[:, t.s % 4, :], bnA).then_inc(s_stats, 1)
                if t := tile(9):
                    dve.wait_ge(s_agg, t.n + 1)
                    at_least(dve, s_aggt, t.n - 1)
                    V.scalar_tensor_tensor(agg_sb[:, t.s % 2], xn[:, t.s, 0:D], epsx[:, 0:1], ps[:, t.s % 2, 0:D],
                                           ALU.mult, ALU.add)
                    V.tensor_copy(din[:, bass.ds(t.n, 1)], ps[:, t.s % 2, D:D + 1]).then_inc(s_aggv, 1)
                if t := tile(13):
                    dve.wait_ge(s_y, t.n + 1)
                    V.tensor_tensor(row(x, t.n), row(x, t.n), ps[:, 6 + t.s % 2, 0:D], ALU.add).then_inc(s_x, 1)
            lagged(dve, emit, T, UA, LAG_A)
            if "R" in stages:
                stage_r_dve(dve)
            if "B" in stages:
                stage_b_dve(dve)
            if "C" in stages:
                stage_c_dve(dve)
            if "D" in stages:
                stage_d_dve(dve)

        @block.gpsimd
        def _(pool):
            G = nc.gpsimd
            pc = [0]
            dve_ready = 1
            pool.wait_ge(s_prep_v, dve_ready)

            def emit(tile):
                if t := tile(11):
                    pool.wait_ge(s_sq, t.n + 1)
                    at_least(pool, s_u, t.n - 3)
                    settled(pool, s_passed_p)
                    G.tensor_scalar(ssA[:, t.s % 4, 1:2], ssA[:, t.s % 4, 0:1], 1.0 / H0, RMS_EPS, ALU.mult, ALU.add).then_inc(s_pc, 1)
                    pool.wait_ge(s_pc, pool_count(t, 11))
                    G.tensor_tensor(rsA[:, t.s % 4, 1:2], ssA[:, t.s % 4, 1:2], mhalf[:, 0:1], ALU.pow).then_inc(s_rms, 1)
                if t := tile(0):
                    pool.wait_ge(s_stats, t.n + 1)
                    at_least(pool, s_norm, t.n - 3)
                    settled(pool, s_passed_p)
                    G.tensor_scalar(mvA[:, t.s % 4, 1:2], mvA[:, t.s % 4, 1:2], LN_EPS, None, ALU.add).then_inc(s_pc, 1)
                    pool.wait_ge(s_pc, pool_count(t, 0))
                    G.tensor_tensor(rsA[:, t.s % 4, 0:1], mvA[:, t.s % 4, 1:2], mhalf[:, 0:1], ALU.pow).then_inc(s_rstd, 1)

            def pool_count(t, lag):
                if lag == 11:
                    n = t.n + 11
                    if isinstance(t.n, int):
                        return t.n + 1 + min(n, T)
                    return t.n + 1 + n
                n = t.n
                if isinstance(n, int):
                    return n + 1 + max(0, n - 11 + 1)
                return n + 1 + n - 10
            lagged(pool, emit, T, UA, LAG_A)
            if "R" in stages:
                stage_r_pool(pool)
            if "B" in stages:
                stage_b_pool(pool)
            if "C" in stages:
                stage_c_pool(pool)
            if "D" in stages:
                stage_d_pool(pool)

        @block.scalar
        def _(act):
            S = nc.scalar

            def emit(tile):
                if t := tile(11):
                    act.wait_ge(s_u, t.n + 1)
                    at_least(act, s_st, t.n - 1)
                    S.activation(su[:, t.s % 2], u[:, t.s % 2], ACT.Silu).then_inc(s_silu, 1)
                if t := tile(10):
                    act.wait_ge(s_aggt, t.n + 1)
                    at_least(act, s_h, t.n - 1)
                    S.copy(aggT[:, t.s % 2], ps[:, 2, 0:D]).then_inc(s_aggc, 1)
                    act.wait_ge(s_h, t.n + 1)
                    at_least(act, s_rms, t.n - 3)
                    S.activation(junk, ps[:, 3 + t.s % 2], ACT.Square, accum_out=ssA[:, t.s % 4, 0:1]).then_inc(s_sq, 1)
                if t := tile(11):
                    act.wait_ge(s_st, t.n + 1)
                    at_least(act, s_y, t.n - 1)
                    S.copy(sT[:, t.s % 2], ps[:, 5]).then_inc(s_stc, 1)
            lagged(act, emit, T, UA, LAG_A)
            if "R" in stages:
                stage_r_act(act)
            if "B" in stages:
                stage_b_act(act)
            if "C" in stages:
                stage_c_act(act)
            if "D" in stages:
                stage_d_act(act)

        @block.tensor
        def _(pe):
            M = nc.tensor
            pe.wait_ge(s_const, 16 * len(CONST))
            pe.wait_ge(s_prep_v, 13)
            for k in range(E * HB):
                M.matmul(ps[:, 7, k:k + 1], ew1_f[:, k // HB, (k % HB) * P:(k % HB + 1) * P], gcol[:, 1:2],
                         start=True, stop=True)
            M.matmul(ps[:, 7, E * HB:E * HB + E], beta_b[:], rw_f[:, 0, :], start=True, stop=True).then_inc(s_prep_t, 1)

            def emit(tile):
                if t := tile(10):
                    pe.wait_ge(s_aggv, t.n + 1)
                    at_least(pe, s_aggc, t.n)
                    M.transpose(ps[:, 2, 0:D], agg_sb[:, t.s % 2], ident[:]).then_inc(s_aggt, 1)
                if t := tile(9):
                    p, i = t.s // TB, t.s % TB
                    pe.wait_ge(s_adj[p], t.g * 8 + 16 - 8 * p)
                    pe.wait_ge(s_norm, (t.g + 1) * TB)
                    at_least(pe, s_aggv, t.n - 1)
                    for m in range(TB):
                        mm = M.matmul(ps[:, t.s % 2, 0:D + 1], adjT[:, p, m, i * P:(i + 1) * P],
                                      xn[:, p * TB + m, :], start=(m == 0), stop=(m == TB - 1))
                    mm.then_inc(s_agg, 1)
                if t := tile(10):
                    pe.wait_ge(s_aggc, t.n + 1)
                    at_least(pe, s_u, t.n - 1)
                    bank = ps[:, 3 + t.s % 2]
                    M.matmul(bank, aggT[:, t.s % 2], w1[:], start=True, stop=False)
                    M.matmul(bank, ones[0:3, :], rows[:, 0:H0], start=False, stop=True).then_inc(s_h, 1)
                if t := tile(11):
                    pe.wait_ge(s_silu, t.n + 1)
                    at_least(pe, s_stc, t.n)
                    for c in range(HC):
                        mm = M.transpose(ps[:, 5, c * P:(c + 1) * P], su[:, t.s % 2, c * P:(c + 1) * P], ident[:])
                    mm.then_inc(s_st, 1)
                if t := tile(12):
                    pe.wait_ge(s_stc, t.n + 1)
                    at_least(pe, s_x, t.n - 1)
                    for c in range(HC):
                        M.matmul(ps[:, 6 + t.s % 2, 0:D], sT[:, t.s % 2, c * P:(c + 1) * P], w2[:, c, :],
                                 start=(c == 0), stop=False)
                    M.matmul(ps[:, 6 + t.s % 2, 0:D], ones[0:3, :], rows[:, H0:H0 + D], start=False, stop=True).then_inc(s_y, 1)
            lagged(pe, emit, T, UA, LAG_A)
            if "R" in stages:
                stage_r_pe(pe)
            if "B" in stages:
                stage_b_pe(pe)
            if "C" in stages:
                stage_c_pe(pe)
            if "D" in stages:
                stage_d_pe(pe)


_OUTS = [((B, N, D), "float32")]


def kernel(**inputs):
    import numpy as np
    import concourse.bacc as _bacc
    from concourse import mybir as _mybir
    from concourse.bass_utils import run_bass_kernel_spmd as _run

    f = lambda k: np.asarray(inputs[k])
    rep = lambda v, n=P: np.ascontiguousarray(np.broadcast_to(v.reshape(1, -1), (n, v.size)))
    arrays = {
        "x": f("x").reshape(T, P, D).transpose(1, 0, 2),
        "adjT": f("adj").transpose(0, 2, 1).reshape(B, TB, P, N).transpose(0, 2, 1, 3),
        "c_ident": np.eye(P, dtype=np.float32),
        "c_tri": np.triu(np.ones((P, P), np.float32), 1),
        "c_iota": rep(np.tile(np.arange(E, dtype=np.float32), TB)),
        "c_ecap": rep(np.tile(np.arange(E, dtype=np.float32) * CAP, TB)),
        "c_iotap": np.arange(P, dtype=np.float32).reshape(P, 1),
        "c_iotat": np.arange(NT, dtype=np.float32).reshape(1, NT),
        "c_sel3": np.eye(P, 3, dtype=np.float32),
        "w1": f("L0_gnn_W1"),
        "w2": f("L0_gnn_W2").reshape(HC, P, D).transpose(1, 0, 2).reshape(P, HC * D),
        "rmsw": rep(f("L0_gnn_rms_weight")),
        "epsx": rep(f("L0_gnn_epsilon")),
        "rows": rep(np.concatenate([f("L0_gnn_b1"), f("L0_gnn_b2"), f("L1_ffn_bo")]), 3),
    }
    arrays |= {
        "gcol": np.stack([f("L0_ffn_gamma"), f("L0_ffn_beta")], 1),
        "ew1": f("L0_ffn_W1").transpose(1, 0, 2).reshape(P, E * HE),
        "eb1": f("L0_ffn_b1").reshape(E, HB, P).transpose(2, 0, 1).reshape(P, E * HB),
        "rw": f("L0_ffn_Wr"),
        "rb": rep(np.tile(f("L0_ffn_br"), TB)),
        "ew2": f("L0_ffn_W2").reshape(E, HB, P, D).transpose(2, 0, 1, 3).reshape(P, E * HB * D),
        "eb2": rep(f("L0_ffn_b2")),
        "lng": rep(np.concatenate([f("L1_gnn_gamma"), f("L1_gnn_beta")])),
        "wsn": np.concatenate([f("L1_gnn_W_self"), f("L1_gnn_W_neigh")], 1),
        "wi": f("L1_ffn_Wi").T,
        "bi": f("L1_ffn_bi").reshape(HB, P).T,
        "ws": f("L1_ffn_Ws").reshape(L1, HE, HB, P).transpose(3, 0, 2, 1).reshape(P, -1),
        "bs": f("L1_ffn_bs").reshape(L1 * HB, P).T,
        "br": f("L1_ffn_br").reshape(L1, E1, HB, P).transpose(3, 0, 2, 1).reshape(P, -1),
        "wo": f("L1_ffn_Wo").T.reshape(HB, P, D).transpose(1, 0, 2).reshape(P, HB * D),
        "wr": f("L1_ffn_Wr").reshape(L1, E1, HE, HB, P).transpose(4, 0, 1, 3, 2).reshape(P, L1, -1),
        "route": f("L1_ffn_route_id").reshape(1, T),
    }
    nc = _bacc.Bacc("TRN2", target_bir_lowering=False, num_devices=1)
    aps, data = {}, {}
    for name, a in arrays.items():
        a = np.ascontiguousarray(a)
        data[f"in_{name}"] = a
        aps[name] = nc.dram_tensor(f"in_{name}", a.shape, _mybir.dt.from_np(a.dtype), kind="ExternalInput").ap()
    out = nc.dram_tensor("out_0", (P, T, D), F32, kind="ExternalOutput").ap()
    build(nc, aps, out, "ARBCD")
    r = _run(nc, [data], core_ids=[0])
    got = np.asarray(r.results[0]["out_0"])
    return np.ascontiguousarray(got.transpose(1, 0, 2)).reshape(B, N, D)
```

```python
from contextlib import ExitStack

import concourse.bass as bass
from concourse import mybir

ALU = mybir.AluOpType
ACT = mybir.ActivationFunctionType
F32 = mybir.dt.float32
F16 = mybir.dt.float16
BF16 = mybir.dt.bfloat16
I32 = mybir.dt.int32
U32 = mybir.dt.uint32
AX_X = mybir.AxisListType.X

P = 128
B, N, D = 8, 1024, 128
T = B * N // P
TB = N // P
H0 = 512
HC = H0 // P
E, HE = 8, 256
HB = HE // P
TS = 512
NT = (2 * B * N + E * (TS - 1)) // TS
CAP = B * N + TS
L1, E1 = 2, 16
LN_EPS = 1e-5
RMS_EPS = 1e-6
WSCALE = 16.0
UA = 2 * TB
UB = 12
ZIN = 4
UD = 16
LAG_D = 7


class Tile:

    def __init__(self, base, j, unroll):
        self.n = base * unroll + j
        self.s = j % unroll
        self.g = base * (unroll // TB) + j // TB if unroll >= TB else None
        self.base, self.j = base, j


def lagged(eng, emit, total, unroll, lag):
    def at(step):
        return lambda k: Tile(0, step - k, unroll) if 0 <= step - k < total else None
    first, loops = max(1, -(-lag // unroll)), total // unroll
    for step in range(first * unroll):
        emit(at(step))
    with eng.Fori(first, loops) as base:
        for j in range(unroll):
            emit(lambda k: Tile(base, j - k, unroll))
    for step in range(loops * unroll, total + lag):
        emit(at(step))


def is_tile(t, n):
    return t is not None and isinstance(t.n, int) and t.n == n


def at_least(eng, sem, n):
    if not isinstance(n, int) or n > 0:
        eng.wait_ge(sem, n)


def settled(eng, passed):
    eng.sem_inc(passed, 1)


def row(t, i):
    return t[:, i] if isinstance(i, int) else t[:, bass.ds(i, 1)].rearrange("p a b -> p (a b)")


def build(nc, inp, out):
    with ExitStack() as ctx:
        def sb(name, shape, dt=F32):
            return ctx.enter_context(nc.sbuf_tensor(name, shape, dt))

        def sem(name):
            return ctx.enter_context(nc.semaphore(name))

        ps = ctx.enter_context(nc.psum_tensor("ps", [P, 8, 512], F32))

        x = sb("x", [P, T, D])
        adjT = sb("adjT", [P, 2, TB, N])
        ident = sb("ident", [P, P])
        ident16 = sb("ident16", [P, P], F16)
        tri = sb("tri", [P, P], BF16)
        ones = sb("ones", [P, P], BF16)
        tri_f = sb("tri_f", [P, P])
        iota_e = sb("iota_e", [P, TB, E])
        ecap = sb("ecap", [P, TB, E])
        mhalf = sb("mhalf", [P, T])
        sel3 = sb("sel3", [P, 3])
        w1_f = sb("w1_f", [P, H0])
        w1 = sb("w1", [P, 2, H0], F16)
        w2 = sb("w2", [P, HC, D])
        rmsw = sb("rmsw", [P, H0])
        epsx = sb("epsx", [P, 1])
        ew1_f = sb("ew1_f", [P, E, HE])
        beta_b = sb("beta_b", [P, P])
        rows = sb("rows", [3, H0 + 2 * D], BF16)
        gcol = sb("gcol", [P, 3])
        ew1 = sb("ew1", [P, E * 2, HE], F16)
        ew2 = sb("ew2", [P, E, HB * D])
        eb1 = sb("eb1", [P, E * HB])
        eb2 = sb("eb2", [P, E, D])
        rw_f = sb("rw_f", [P, 2, E])
        rw = sb("rw", [P, 2, E], F16)
        rb = sb("rb", [P, TB, E])
        lng = sb("lng", [P, 2, D])
        wsn = sb("wsn", [P, 2, D])
        wi = sb("wi", [P, HE])
        bi = sb("bi", [P, HB])
        ws = sb("ws", [P, L1 * HB, HE])
        bs = sb("bs", [P, L1 * HB])
        btab = sb("btab", [P, L1 * HB, E1])
        wo = sb("wo", [P, HB, D])
        route = sb("route", [1, T], I32)
        din = sb("din", [P, T])
        s_in = sb("s_in", [P, T])
        dout = sb("dout", [P, T])
        s_out_neg = sb("s_out_neg", [P, T])
        smask = sb("smask", [P, T])
        gap = sb("gap", [P, T])
        gw = sb("gw", [P, 2, T])
        onehot = sb("onehot", [P, T, 2, E])
        rank = sb("rank", [P, T, E])
        etab = sb("etab", [1, NT], I32)
        btable = sb("btable", [1, NT], I32)
        back = sb("back", [P, T, 2], U32)
        WORK = 12016
        work = sb("work", [P, WORK])

        def carver(start=0):
            at = [start]

            def carve(shape, dt=F32):
                n = 1
                for k in shape:
                    n *= k
                words = (n * mybir.dt.size(dt) + 3) // 4
                a = work[:, at[0]:at[0] + words]
                at[0] += words
                assert at[0] <= WORK, at[0]
                if dt != F32:
                    a = a.bitcast(dt)
                names = " ".join("abcd"[:len(shape)])
                return a.rearrange(f"p ({names}) -> p {names}", **dict(zip("abcd", shape)))
            return carve

        xs_rows = nc.dram_tensor("expert_rows", [E * CAP + TS, 2 * D], F16, kind="Internal").ap()
        y_rows = nc.dram_tensor("expert_out", [NT * TS, D], F32, kind="Internal").ap()

        block = ctx.enter_context(nc.Block())

        s_const_rows = sem("s_const_rows")
        s_const = sem("s_const")
        s_const1 = sem("s_const1")
        s_x0 = sem("s_x0")
        s_x1 = sem("s_x1")
        s_bias = sem("s_bias")
        s_w1 = sem("s_w1")
        s_prep_v = sem("s_prep_v")
        s_prep_t = sem("s_prep_t")
        s_adj = [sem("s_adj0"), sem("s_adj1")]
        s_stats = sem("s_stats")
        s_rstd = sem("s_rstd")
        s_norm = sem("s_norm")
        s_agg = sem("s_agg")
        s_aggf = sem("s_aggf")
        s_aggv = sem("s_aggv")
        s_agglo = sem("s_agglo")
        s_aggt = sem("s_aggt")
        s_aggc = sem("s_aggc")
        s_h = sem("s_h")
        s_sq = sem("s_sq")
        s_rms = sem("s_rms")
        s_u = sem("s_u")
        s_silu = sem("s_silu")
        s_st = sem("s_st")
        s_stc = sem("s_stc")
        s_y = sem("s_y")
        s_x = sem("s_x")
        s_pc = sem("s_pc")
        s_vc = sem("s_vc")
        s_passed_v = sem("s_passed_v")
        s_passed_p = sem("s_passed_p")
        s_out = sem("s_out")
        c_agg = sem("c_agg")
        s_dout = sem("s_dout")
        c_pc = sem("c_pc")
        c_factors = sem("c_factors")
        c_places = sem("c_places")
        c_comb = sem("c_comb")
        c_stats = sem("c_stats")
        c_pv = sem("c_pv")
        c_rs = sem("c_rs")
        c_q = sem("c_q")
        c_vp = sem("c_vp")
        c_gexp = sem("c_gexp")
        c_v0 = sem("c_v0")
        c_bn = sem("c_bn")
        c_z = sem("c_z")
        c_xn = sem("c_xn")
        c_xs = sem("c_xs")
        c_tr = sem("c_tr")
        c_tc = sem("c_tc")
        c_pre = sem("c_pre")
        c_abs = sem("c_abs")
        c_exp = sem("c_exp")
        c_ln = sem("c_ln")
        c_sp = sem("c_sp")
        c_x = sem("c_x")
        s_const3 = sem("s_const3")
        c_adj = [sem("c_adj0"), sem("c_adj1")]
        c_gath = [sem("c_gath0"), sem("c_gath1")]
        d_wr = [sem(f"d_wr{l}") for l in range(L1)]
        d_bn = sem("d_bn")
        d_stats = sem("d_stats")
        d_pv = sem("d_pv")
        d_rs = sem("d_rs")
        d_z = sem("d_z")
        d_tr = sem("d_tr")
        d_zt = sem("d_zt")
        d_weff = [sem(f"d_weff{l}") for l in range(L1)]
        d_h = [sem(f"d_h{l}") for l in range(L1 + 1)]
        d_r = [sem(f"d_r{l}") for l in range(L1 + 1)]
        d_o = sem("d_o")
        d_x = sem("d_x")
        r_iota = sem("r_iota")
        r_padded = sem("r_padded")
        r_zero = sem("r_zero")
        r_oh = sem("r_oh")
        r_spot = sem("r_spot")
        r_end = sem("r_end")
        r_back = sem("r_back")
        s_const2 = sem("s_const2")
        r_stats = sem("r_stats")
        r_sc = sem("r_sc")
        r_z = sem("r_z")
        r_hi = sem("r_hi")
        r_lo = sem("r_lo")
        r_tr = sem("r_tr")
        r_zt = sem("r_zt")
        r_lg = sem("r_lg")
        r_pick = sem("r_pick")
        r_bn = sem("r_bn")
        r_pv = sem("r_pv")
        r_logit = sem("r_logit")
        r_top = sem("r_top")
        r_topi = sem("r_topi")
        r_topf = sem("r_topf")
        r_sum = sem("r_sum")
        r_hit = sem("r_hit")
        r_slotf = sem("r_slotf")
        r_chosen = sem("r_chosen")
        r_pos = sem("r_pos")
        r_slot = sem("r_slot")
        r_scat = [sem("r_scat0"), sem("r_scat1")]
        r_cnt = sem("r_cnt")
        r_tab = sem("r_tab")
        r_pad = sem("r_pad")
        b_load = [sem(f"b_load{k}") for k in range(ZIN)]
        b_tr = sem("b_tr")
        b_zt = sem("b_zt")
        b_h = sem("b_h")
        b_gelu = sem("b_gelu")
        b_y = sem("b_y")
        b_out = sem("b_out")
        b_store = [sem(f"b_store{k}") for k in range(3)]

        in_ap = inp

        wa = carver()
        z = wa([TB, D])
        zT = wa([TB, 2, P], F16)
        zhl = wa([2, TB, 2 * D], F16)
        rows_f = carver()([4, H0 + 2 * D])[0:3]
        xn = wa([UA, D + 1])
        agg_f = wa([D])
        agg_hl = wa([2, 2, D], F16)
        aggT = wa([2, 2, P], F16)
        u = wa([2, H0])
        su = wa([2, H0])
        sT = wa([2, H0])
        junk = wa([H0])
        junk_n = wa([N], BF16)
        mvA = wa([4, 2])
        bnA = wa([2, 6])
        rsA = wa([4, 2])
        ssA = wa([4, 2])
        bnR = wa([TB, 6])
        mvR = wa([TB, 2])
        scR = wa([TB])
        logit = wa([TB, E])
        top = wa([TB, 8])
        topi = wa([TB, 8], U32)
        topf = wa([TB, 2])
        pick = wa([TB, E], BF16)
        chosen = wa([E], BF16)
        chosen_g = wa([E])
        spot = wa([TB, E])
        hit = wa([2, TB, E])
        slot_f = wa([2, TB])
        slot = wa([2, 2, TB], U32)
        zrow = wa([TS // P, 2 * D], F16)
        aggT_ps = ps[:, 2].bitcast(F16)[:, 0:2 * P].rearrange("p (h q) -> p h q", h=2)
        wt = carver(4 * TB * D)
        cnt_i = wt([E], I32)
        tiles_e = wt([E])
        first_t = wt([E + 1])
        first_r = wt([E])
        pad_f = wt([E])
        pad = wt([E], I32)
        iota_t = wt([NT])
        over = wt([NT, E])
        part = wt([NT, E])
        e_f = wt([NT])
        b_f = wt([NT])
        wh = wt([T, E])
        hit2 = wt([T, 2, E])
        back_f = wt([T, 2])

        CONST_ROWS = [(sel3[:], "c_sel3"), (rows_f[:, 0, :], "rows")]
        CONST = [
            (ident[:], "c_ident"), (epsx[:], "epsx"), (w1_f[:], "w1"), (rmsw[:], "rmsw"),
            (w2[:].rearrange("p c d -> p (c d)"), "w2"),
        ]
        CONST1 = [
            (tri_f[:], "c_tri"), (iota_e[:].rearrange("p t e -> p (t e)"), "c_iota"), (ecap[:].rearrange("p t e -> p (t e)"), "c_ecap"),
            (gcol[:, 0:2], "gcol"), (ew1_f[:].rearrange("p e h -> p (e h)"), "ew1"), (eb1[:], "eb1"),
            (rw_f[:, 0, :], "rw"), (rb[:].rearrange("p t e -> p (t e)"), "rb"),
        ]
        CONST3 = [
            (lng[:].rearrange("p a d -> p (a d)"), "lng"), (wsn[:].rearrange("p a d -> p (a d)"), "wsn"), (wi[:], "wi"), (bi[:], "bi"),
            (ws[:].rearrange("p a h -> p (a h)"), "ws"), (bs[:], "bs"), (btab[:].rearrange("p a e -> p (a e)"), "br"),
            (wo[:].rearrange("p a d -> p (a d)"), "wo"), (route[:], "route"),
        ]
        CONST2 = [
            (ew2[:].rearrange("p e h -> p (e h)"), "ew2"), (eb2[:].rearrange("p e d -> p (e d)"), "eb2"),
        ]

        SCATTERS = [3, 3, 3, 2, 3, 2]
        R_STATS, R_Z, R_LO, R_LG, R_PICK, R_POS, R_SCAT = 21, 22, 23, 25, 25, 26, 27
        LAG_A = R_SCAT + len(SCATTERS) - 1
        assert sum(SCATTERS) == 2 * TB

        def graph_loads(t):
            return (t.g - (t.s // TB)) // 2 + 1 if isinstance(t.n, int) else t.base + t.j // UA + 1

        def graph_at(tile, lag):
            t = tile(lag)
            return t if t and t.s % TB == 0 else None

        def route_dve_stats(dve, tile):
            V = nc.vector
            if t := graph_at(tile, R_STATS):
                xg = x[:, bass.ds(t.n, TB), :]
                dve.wait_ge(s_x, (t.g + 1) * TB)
                settled(dve, s_passed_v)
                for i in range(TB):
                    bn = V.bn_stats(bnR[:, i], xg[:, i])
                bn.then_inc(r_bn, 1)
                dve.wait_ge(r_bn, t.g + 1)
                settled(dve, s_passed_v)
                for i in range(TB):
                    ag = V.bn_aggr(mvR[:, i], bnR[:, i])
                ag.then_inc(r_stats, 1)

        def route_dve(dve, tile):
            V = nc.vector
            if t := graph_at(tile, R_Z):
                xg = x[:, bass.ds(t.n, TB), :]
                dve.wait_ge(r_sc, t.g + 1)
                for i in range(TB):
                    zi = V.tensor_scalar(z[:, i], xg[:, i], mvR[:, i, 0:1], scR[:, i:i + 1], ALU.subtract, ALU.mult)
                zi.then_inc(r_z, 1)
            if t := graph_at(tile, R_LO):
                zg = zhl[:, t.s // TB]
                dve.wait_ge(r_z, t.g + 1)
                dve.wait_ge(r_hi, t.g + 1)
                V.tensor_tensor(zg[:, :, D:2 * D], z, zg[:, :, 0:D], ALU.subtract).then_inc(r_lo, 1)
            if t := graph_at(tile, R_LG):
                dve.wait_ge(r_lg, t.g + 1)
                V.scalar_tensor_tensor(logit, ps[:, 7, 0:TB * E].rearrange("p (t e) -> p t e", e=E), 1.0 / WSCALE,
                                       rb[:], ALU.mult, ALU.add).then_inc(r_logit, 1)
                dve.wait_ge(r_logit, t.g + 1)
                settled(dve, s_passed_v)
                for i in range(TB):
                    mx = V.max(top[:, i], logit[:, i])
                mx.then_inc(r_top, 1)
            if t := graph_at(tile, R_PICK):
                dve.wait_ge(r_top, t.g + 1)
                V.tensor_tensor(gap[:, bass.ds(t.n, TB)], top[:, :, 1], top[:, :, 0], ALU.subtract)
                for i in range(TB):
                    mi = V.max_index(topi[:, i], top[:, i], logit[:, i])
                mi.then_inc(r_topi, 1)
                dve.wait_ge(r_topi, t.g + 1)
                V.tensor_copy(topf, topi[:, :, 0:2]).then_inc(r_topf, 1)
                dve.wait_ge(r_topf, t.g + 1)
                oh = onehot[:, bass.ds(t.n, TB), :, :]
                for k in range(2):
                    eq = V.tensor_tensor(oh[:, :, k, :], iota_e[:], topf[:, :, k:k + 1].to_broadcast([P, TB, E]), ALU.is_equal)
                eq.then_inc(r_oh, 1)
                dve.wait_ge(r_oh, t.g + 1)
                V.tensor_tensor(pick, oh[:, :, 0, :], oh[:, :, 1, :], ALU.add).then_inc(r_pick, 1)
            if t := graph_at(tile, R_POS):
                oh = onehot[:, bass.ds(t.n, TB), :, :]
                dve.wait_ge(r_pick, t.g + 1)
                V.tensor_reduce(chosen_g, pick.rearrange("p t e -> p e t"), AX_X, ALU.add).then_inc(r_sum, 1)
                dve.wait_ge(r_pos, t.g + 1)
                pos = ps[:, 7, 0:TB * E].rearrange("p (t e) -> p t e", e=E)
                V.tensor_tensor(spot, pos, ecap[:], ALU.add).then_inc(r_spot, 1)
                V.tensor_copy(rank[:, bass.ds(t.n, TB), :], pos)
                dve.wait_ge(r_spot, t.g + 1)
                for k in range(2):
                    ht = V.tensor_tensor(hit[:, k], spot, oh[:, :, k, :], ALU.mult)
                ht.then_inc(r_hit, 1)
                dve.wait_ge(r_sum, t.g + 1)
                V.tensor_tensor(chosen, chosen, chosen_g, ALU.add)
                dve.wait_ge(r_hit, t.g + 1)
                V.tensor_reduce(slot_f, hit, AX_X, ALU.add).then_inc(r_slotf, 1)
                dve.wait_ge(r_slotf, t.g + 1)
                V.tensor_copy(slot[:, t.s // TB], slot_f).then_inc(r_slot, 1)

        def route_pool(pool, tile):
            G = nc.gpsimd
            if t := graph_at(tile, R_Z):
                pool.wait_ge(r_stats, t.g + 1)
                settled(pool, s_passed_p)
                G.tensor_scalar(mvR[:, :, 1], mvR[:, :, 1], 1.0 + LN_EPS, LN_EPS * LN_EPS, ALU.mult, ALU.add).then_inc(r_pv, 1)
                pool.wait_ge(r_pv, t.g + 1)
                G.tensor_tensor(scR, mvR[:, :, 1], mhalf[:, 0:TB], ALU.pow).then_inc(r_sc, 1)
            for q, count in enumerate(SCATTERS):
                if t := graph_at(tile, R_SCAT + q):
                    if q == 0:
                        pool.wait_ge(r_slot, t.g + 1)
                        settled(pool, s_passed_p)
                    par = t.s // TB
                    for n in range(sum(SCATTERS[:q]), sum(SCATTERS[:q]) + count):
                        i, k = n // 2, n % 2
                        G.indirect_dma_start(xs_rows, bass.IndirectOffsetOnAxis(slot[:, par, k, i:i + 1], 0),
                                             zhl[:, par, i, :], None).then_inc(r_scat[par], 16)

        def route_act_hi(act, tile):
            if t := graph_at(tile, R_Z):
                act.wait_ge(r_z, t.g + 1)
                at_least(act, r_scat[t.s // TB], (graph_loads(t) - 1) * (2 * TB * 16))
                nc.scalar.copy(zhl[:, t.s // TB, :, 0:D], z).then_inc(r_hi, 1)

        def route_act(act, tile, half):
            if t := graph_at(tile, R_LO + 1):
                act.wait_ge(r_tr, t.g * 2 + half + 1)
                h4 = TB // 2
                nc.scalar.copy(zT[:, half * h4:(half + 1) * h4].rearrange("p t s q -> p (t s q)"),
                               ps[:, 7].bitcast(F16)).then_inc(r_zt, 1)

        def route_transpose(pe, tile, half):
            if t := graph_at(tile, R_LO + half):
                tr = ps[:, 7].bitcast(F16).rearrange("p (t s q) -> p t s q", t=TB // 2, s=2)
                if half:
                    pe.wait_ge(r_zt, t.g * 2 + 1)
                else:
                    pe.wait_ge(r_lo, t.g + 1)
                    at_least(pe, r_slot, t.g)
                for i in range(TB // 2):
                    for s in range(2):
                        mm = nc.tensor.transpose(tr[:, i, s], zhl[:, t.s // TB, half * TB // 2 + i, s * D:(s + 1) * D], ident16[:])
                mm.then_inc(r_tr, 1)

        def route_logits(pe, tile):
            if t := graph_at(tile, R_LG):
                pe.wait_ge(r_zt, t.g * 2 + 2)
                for i in range(TB):
                    for n, (a, b) in enumerate(((0, 0), (1, 0), (0, 1))):
                        mm = nc.tensor.matmul(ps[:, 7, i * E:(i + 1) * E], zT[:, i, a], rw[:, b], start=(n == 0), stop=(n == 2))
                mm.then_inc(r_lg, 1)

        def route_ranks(pe, tile):
            M = nc.tensor
            if t := graph_at(tile, R_POS):
                pe.wait_ge(r_pick, t.g + 1)
                M.matmul(ps[:, 7, 0:TB * E], tri[:], pick.rearrange("p t e -> p (t e)"), start=True, stop=False)
                for i in range(TB - 1):
                    M.matmul(ps[:, 7, (i + 1) * E:TB * E].rearrange("p (t e) -> p t e", e=E), ones[:],
                             pick[:, i:i + 1, :].to_broadcast([P, TB - 1 - i, E]), start=False, stop=False)
                M.matmul(ps[:, 7, 0:TB * E].rearrange("p (t e) -> p t e", e=E), ones[:],
                         chosen.unsqueeze(1).to_broadcast([P, TB, E]), start=False, stop=True).then_inc(r_pos, 1)

        def route_end_dve(dve):
            V = nc.vector
            V.engine_nop().then_inc(r_chosen, 1)
            link_n = [0]

            def link(ins):
                link_n[0] += 1
                ins.then_inc(r_end, 1)
                dve.wait_ge(r_end, link_n[0])
            dve.wait_ge(r_cnt, 1)
            cnt = ps[:, 7, 0:E]
            V.tensor_tensor(pad_f, cnt, ecap[:, 0, :], ALU.add)
            link(V.tensor_scalar(tiles_e, cnt, float(TS - 1), None, ALU.add))
            V.tensor_copy(pad, pad_f).then_inc(r_pad, 1)
            link(V.tensor_copy(cnt_i, tiles_e))
            link(V.tensor_single_scalar(cnt_i, cnt_i, TS.bit_length() - 1, ALU.logical_shift_right))
            V.memset(first_t[:, 0:1], 0.0)
            link(V.tensor_copy(tiles_e, cnt_i))
            for e in range(E):
                link(V.tensor_tensor(first_t[:, e + 1:e + 2], first_t[:, e:e + 1], tiles_e[:, e:e + 1], ALU.add))
            it = iota_t[0:1]
            dve.wait_ge(r_iota, 16)
            link(V.tensor_tensor(over[0:1], it.unsqueeze(2).to_broadcast([1, NT, E]),
                                 first_t[0:1, 1:E + 1].unsqueeze(1).to_broadcast([1, NT, E]), ALU.is_ge))
            V.tensor_reduce(e_f[0:1], over[0:1], AX_X, ALU.add)
            link(V.tensor_tensor(part[0:1], over[0:1], tiles_e[0:1].unsqueeze(1).to_broadcast([1, NT, E]), ALU.mult))
            link(V.tensor_reduce(b_f[0:1], part[0:1], AX_X, ALU.add))
            link(V.tensor_tensor(b_f[0:1], it, b_f[0:1], ALU.subtract))
            link(V.tensor_scalar(b_f[0:1], b_f[0:1], float(TS), None, ALU.mult))
            link(V.scalar_tensor_tensor(b_f[0:1], e_f[0:1], float(CAP), b_f[0:1], ALU.mult, ALU.add))
            V.tensor_scalar(btable[:], b_f[0:1], float(E * CAP), None, ALU.min)
            link(V.tensor_scalar(etab[:], e_f[0:1], float(E - 1), None, ALU.min))
            V.engine_nop().then_inc(r_tab, 1)
            link(V.tensor_scalar(first_r, first_t[:, 0:E], float(TS), None, ALU.mult))
            link(V.tensor_tensor(wh, rank[:], first_r.unsqueeze(1).to_broadcast([P, T, E]), ALU.add))
            for k in range(2):
                ht = V.tensor_tensor(hit2[:, :, k, :], wh, onehot[:, :, k, :], ALU.mult)
            link(ht)
            link(V.tensor_reduce(back_f, hit2, AX_X, ALU.add))
            V.tensor_copy(back[:], back_f).then_inc(r_back, 1)

        def route_end_pe(pe):
            pe.wait_ge(r_chosen, 1)
            pe.wait_ge(r_slot, B)
            nc.tensor.matmul(ps[:, 7, 0:E], ones[:], chosen, start=True, stop=True).then_inc(r_cnt, 1)

        def route_end_sp(sp):
            sp.wait_ge(s_x, T)
            sp.dma_start(iota_t[0:1], in_ap["c_iotat"]).then_inc(r_iota, 16)
            sp.wait_ge(r_zero, 1)
            z3 = zrow
            sp.dma_start(xs_rows[E * CAP:E * CAP + TS, :].rearrange("(s p) c -> p s c", p=P), z3).then_inc(r_padded, 16)
            sp.wait_ge(r_pad, 1)
            for e in range(E):
                first = sp.value_load(pad[0:1, e:e + 1], min_val=e * CAP, max_val=e * CAP + B * N)
                sp.dma_start(xs_rows[bass.ds(first, TS), :].rearrange("(s p) c -> p s c", p=P), z3).then_inc(r_padded, 16)

        SCATTERED = 16 * (B // 2) * 2 * TB
        PADDED = 16 * (E + 1)

        wb = carver()
        zin = wb([ZIN, TS // P, 2 * D], F16)
        zTb = wb([2, 2, TS], F16)
        hT = wb([2, HB, TS])
        yo = wb([3, TS // P, D])

        def stage_b_sp(sp):
            sp.wait_ge(r_tab, 1)
            for par in range(2):
                sp.wait_ge(r_scat[par], SCATTERED)
            sp.wait_ge(r_padded, PADDED)
            sp.wait_ge(r_back, 1)

            SLICES = TB // (NT // UB - 1)

            def emit(tile):
                if t := tile(0):
                    b = t.s % ZIN
                    at_least(sp, b_tr, t.n - (ZIN - 1))
                    row0 = sp.value_load(btable[0:1, bass.ds(t.n, 1)], min_val=0, max_val=E * CAP)
                    sp.dma_start(zin[:, b], xs_rows[bass.ds(row0, TS), :].rearrange("(s p) c -> p s c", p=P)).then_inc(b_load[b], 16)
                    if is_tile(t, 2):
                        for dst, name in CONST3:
                            sp.dma_start(dst, in_ap[name]).then_inc(s_const3, 16)
                    if isinstance(t.n, int):
                        if UB - TB <= t.n < UB:
                            m = t.n - (UB - TB)
                            sp.dma_start(adjT[:, 0, m], in_ap["adjT"][0, :, m]).then_inc(c_adj[0], 16)
                    elif t.s % (UB // SLICES) == 0:
                        m = (t.base - 1) * SLICES + t.s // (UB // SLICES)
                        sp.dma_start(adjT[:, 1, bass.ds(m, 1)].rearrange("p a b -> p (a b)"),
                                     in_ap["adjT"][1, :, bass.ds(m, 1)].rearrange("p a b -> p (a b)")).then_inc(c_adj[1], 16)
            lagged(sp, emit, NT, UB, 0)

        def stage_b_pool(pool):
            def emit(tile):
                if t := tile(0):
                    b = t.s % 3
                    pool.wait_ge(b_out, t.n + 1)
                    nc.gpsimd.dma_start(y_rows[bass.ds(t.n * TS, TS), :].rearrange("(s p) c -> p s c", p=P), yo[:, b]).then_inc(b_store[b], 16)
            lagged(pool, emit, NT, UB, 0)

        def stage_b_pe(pe):
            M = nc.tensor

            pe.wait_ge(r_tab, 1)
            pe.wait_ge(s_const2, 16 * len(CONST2))

            def emit(tile):
                if t := tile(0):
                    b = t.s % ZIN
                    pe.wait_ge(b_load[b], uses_of(t, ZIN))
                    at_least(pe, b_zt, t.n - 1)
                    tr = ps[:, t.s % 2].bitcast(F16)[:, 0:2 * TS].rearrange("p (h q) -> p h q", h=2)
                    for s in range(TS // P):
                        for h in range(2):
                            mm = M.transpose(tr[:, h, s * P:(s + 1) * P], zin[:, b, s, h * D:(h + 1) * D], ident16[:])
                    mm.then_inc(b_tr, 1)
                if t := tile(1):
                    e = pe.value_load(etab[0:1, bass.ds(t.n, 1)], min_val=0, max_val=E - 1)
                    pe.wait_ge(b_zt, t.n + 1)
                    at_least(pe, b_gelu, t.n - 1)
                    for c in range(HB):
                        for n, (a, w) in enumerate(((0, 0), (0, 1), (1, 0))):
                            mm = M.matmul(ps[:, 2 + 2 * (t.s % 2) + c, 0:TS],
                                          ew1[:, bass.ds(e * 2 + w, 1), c * P:(c + 1) * P].rearrange("p a b -> p (a b)"),
                                          zTb[:, t.s % 2, a], start=(n == 0), stop=(n == 2))
                    mm.then_inc(b_h, 1)
                if t := tile(2):
                    e = pe.value_load(etab[0:1, bass.ds(t.n, 1)], min_val=0, max_val=E - 1)
                    pe.wait_ge(b_gelu, t.n + 1)
                    at_least(pe, b_out, t.n - 1)
                    for s in range(TS // P):
                        for c in range(HB):
                            mm = M.matmul(ps[:, 6 + t.s % 2, s * D:(s + 1) * D], hT[:, t.s % 2, c, s * P:(s + 1) * P],
                                          ew2[:, bass.ds(e, 1), c * D:(c + 1) * D].rearrange("p a b -> p (a b)"),
                                          start=(c == 0), stop=(c == HB - 1))
                    mm.then_inc(b_y, 1)
            lagged(pe, emit, NT, UB, 2)

        def stage_b_act(act):
            S = nc.scalar
            act.wait_ge(r_tab, 1)
            act.wait_ge(r_back, 1)

            def emit(tile):
                if t := tile(1):
                    e = act.value_load(etab[0:1, bass.ds(t.n, 1)], min_val=0, max_val=E - 1)
                    act.wait_ge(b_h, t.n + 1)
                    at_least(act, b_y, t.n - 1)
                    for c in range(HB):
                        ge = S.activation(hT[:, t.s % 2, c], ps[:, 2 + 2 * (t.s % 2) + c, 0:TS], ACT.Gelu,
                                          bias=eb1[:, bass.ds(e * HB + c, 1)], scale=1.0 / WSCALE)
                    ge.then_inc(b_gelu, 1)
            lagged(act, emit, NT, UB, 1)

        def stage_b_dve(dve):
            V = nc.vector

            def emit(tile):
                if t := tile(0):
                    dve.wait_ge(b_tr, t.n + 1)
                    at_least(dve, b_h, t.n - 1)
                    V.tensor_copy(zTb[:, t.s % 2].rearrange("p h q -> p (h q)"), ps[:, t.s % 2].bitcast(F16)[:, 0:2 * TS]).then_inc(b_zt, 1)
                if t := tile(2):
                    e = dve.value_load(etab[0:1, bass.ds(t.n, 1)], min_val=0, max_val=E - 1)
                    dve.wait_ge(b_y, t.n + 1)
                    if not (isinstance(t.n, int) and t.n < 3):
                        dve.wait_ge(b_store[t.s % 3], uses_of(t, 3) - 16)
                    V.tensor_tensor(yo[:, t.s % 3], ps[:, 6 + t.s % 2, 0:TS // P * D].rearrange("p (s d) -> p s d", d=D),
                                    eb2[:, bass.ds(e, 1), :].to_broadcast([P, TS // P, D]), ALU.add).then_inc(b_out, 1)
            lagged(dve, emit, NT, UB, 2)

        def uses_of(t, ring):
            return 16 * (t.n // ring + 1) if isinstance(t.n, int) else t.base * (16 * UB // ring) + 16 * (t.j // ring + 1)

        wc = carver()
        yg = wc([2, TB, 2, D])
        xnC = wc([2, TB, D])
        xsC = wc([2, TB, D])
        qC = wc([2, D])
        qxT = wc([2, 2 * D])
        soft = wc([TB, D])
        bnC = wc([TB, 6])
        mvC = wc([TB, 2])
        rsC = wc([TB])
        gexp = wc([T])
        places = wc([2, TB, 2], U32)
        gden = wc([T])
        FRONT, MAIN = TB, 2 * TB
        LAG_C = MAIN + 15

        def stage_c_sp_loop(sp):
            with sp.Fori(1, B // 2) as bb:
                for p in range(2):
                    sp.wait_ge(c_agg, (bb * 2 + p - 1) * TB)
                    sp.dma_start(adjT[:, p], in_ap["adjT"][bass.ds(bb * 2 + p, 1)].rearrange("g p m n -> (g p) m n")).then_inc(c_adj[p], 16)

        def b_is_over(eng):
            eng.wait_ge(b_out, NT)
            for k in range(3):
                eng.wait_ge(b_store[k], 16 * len(range(k, NT, 3)))

        def factors_pool(pool):
            G = nc.gpsimd
            pool.wait_ge(s_aggv, T)
            pool.wait_ge(s_dout, T)
            chain = [0]

            def link(ins):
                chain[0] += 1
                ins.then_inc(c_pc, 1)
                pool.wait_ge(c_pc, chain[0])
            for sums, factor, sign in ((din, s_in, 1.0), (dout, s_out_neg, -1.0)):
                link(G.tensor_scalar(smask[:], sums[:], 0.0, None, ALU.is_equal))
                link(G.tensor_tensor(factor[:], sums[:], smask[:], ALU.add))
                link(G.tensor_tensor(factor[:], factor[:], mhalf[:], ALU.pow))
                link(G.tensor_scalar(smask[:], smask[:], -sign, sign, ALU.mult, ALU.add))
                link(G.tensor_tensor(factor[:], factor[:], smask[:], ALU.mult))
            G.engine_nop().then_inc(c_factors, 1)

        def stage_c_pool(pool):
            G = nc.gpsimd
            b_is_over(pool)
            def emit(tile):
                if t := tile(0):
                    par, i = t.s // TB, t.s % TB
                    if i == 0:
                        at_least(pool, c_comb, t.g - 1)
                        settled(pool, s_passed_p)
                        G.tensor_copy(places[:, par], back[:, bass.ds(t.n, TB), :]).then_inc(c_places, 1)
                        pool.wait_ge(c_places, t.g + 1)
                        settled(pool, s_passed_p)
                    for k in range(2):
                        G.indirect_dma_start(yg[:, par, i, k, :], None, y_rows,
                                             bass.IndirectOffsetOnAxis(places[:, par, i, k:k + 1], 0)).then_inc(c_gath[par], 16)
                if (t := tile(FRONT)) and t.s % TB == 3:
                    pool.wait_ge(c_stats, t.g + 1)
                    settled(pool, s_passed_p)
                    G.tensor_scalar(mvC[:, :, 1], mvC[:, :, 1], 1.0 + LN_EPS, LN_EPS * LN_EPS, ALU.mult, ALU.add).then_inc(c_pv, 1)
                    pool.wait_ge(c_pv, t.g + 1)
                    G.tensor_tensor(rsC, mvC[:, :, 1], mhalf[:, 0:TB], ALU.pow).then_inc(c_rs, 1)
            lagged(pool, emit, T, UA, LAG_C)

        def stage_c_dve(dve):
            V = nc.vector
            chain = [0]

            def link(ins):
                chain[0] += 1
                ins.then_inc(c_vp, 1)
                dve.wait_ge(c_vp, chain[0])
            dve.wait_ge(s_const3, 16 * len(CONST3))
            V.tensor_tensor(wsn[:, 0], wsn[:, 0], wsn[:, 1], ALU.add)
            for l in range(L1):
                for c in range(HB):
                    k = l * HB + c
                    V.tensor_tensor(ws[:, k, c * P:(c + 1) * P], ws[:, k, c * P:(c + 1) * P], ident[:], ALU.add)
            V.tensor_tensor(btab[:], btab[:], bs[:].unsqueeze(2).to_broadcast([P, L1 * HB, E1]), ALU.add)
            dve.wait_ge(c_factors, 1)
            dve.wait_ge(c_gexp, 1)
            link(V.tensor_scalar(gden, gexp, 1.0, None, ALU.add))
            link(V.reciprocal(gw[:, 0], gden))
            link(V.tensor_tensor(gw[:, 1], gw[:, 0], gexp, ALU.mult))

            def emit(tile):
                if t := tile(FRONT):
                    par, i = t.s // TB, t.s % TB
                    tiles = [t.n - i + k for k in range(TB)]
                    if i < 2:
                        if i == 0:
                            dve.wait_ge(c_gath[par], graph_loads(t) * (2 * TB * 16))
                        else:
                            dve.wait_ge(c_v0, t.g + 1)
                        for k in range(TB):
                            ins = V.scalar_tensor_tensor(row(x, tiles[k]), yg[:, par, k, i], gw[:, i, bass.ds(tiles[k], 1)],
                                                         row(x, tiles[k]), ALU.mult, ALU.add)
                        ins.then_inc(c_v0 if i == 0 else c_comb, 1)
                    elif i == 2:
                        dve.wait_ge(c_comb, t.g + 1)
                        settled(dve, s_passed_v)
                        for k in range(TB):
                            ins = V.bn_stats(bnC[:, k], row(x, tiles[k]))
                        ins.then_inc(c_bn, 1)
                    elif i == 3:
                        dve.wait_ge(c_bn, t.g + 1)
                        settled(dve, s_passed_v)
                        for k in range(TB):
                            ins = V.bn_aggr(mvC[:, k], bnC[:, k])
                        ins.then_inc(c_stats, 1)
                    elif i == 4:
                        dve.wait_ge(c_stats, t.g + 1)
                        at_least(dve, c_tr, (t.g - 1) * TB)
                        for k in range(TB):
                            ins = V.scalar_tensor_tensor(xnC[:, par, k], row(x, tiles[k]), mvC[:, k, 0:1], lng[:, 0],
                                                         ALU.subtract, ALU.mult)
                        ins.then_inc(c_z, 1)
                    elif i == 5:
                        dve.wait_ge(c_z, t.g + 1)
                        dve.wait_ge(c_rs, t.g + 1)
                        for k in range(TB):
                            ins = V.scalar_tensor_tensor(xnC[:, par, k], xnC[:, par, k], rsC[:, k:k + 1], lng[:, 1],
                                                         ALU.mult, ALU.add)
                        ins.then_inc(c_xn, 1)
                    elif i == 6:
                        dve.wait_ge(c_xn, t.g + 1)
                        at_least(dve, c_agg, (t.g - 1) * TB)
                        for k in range(TB):
                            ins = V.tensor_scalar(xsC[:, par, k], xnC[:, par, k], s_in[:, bass.ds(tiles[k], 1)], None, ALU.mult)
                        ins.then_inc(c_xs, 1)
                if t := tile(MAIN):
                    par, i = t.s // TB, t.s % TB
                    dve.wait_ge(c_agg, t.n + 1)
                    at_least(dve, c_tr, t.n - 1)
                    V.tensor_scalar(qC[:, t.s % 2], ps[:, t.s % 2, 0:D], s_out_neg[:, bass.ds(t.n, 1)], None, ALU.mult).then_inc(c_q, 1)
                if (t := tile(MAIN + 14)) and t.s % TB == 0:
                    b0 = 4 + 2 * (t.s // TB)
                    dve.wait_ge(c_ln, t.g + 1)
                    V.scalar_tensor_tensor(soft.rearrange("p t d -> p (t d)"), ps[:, b0:b0 + 2].rearrange("p a b -> p (a b)"), 0.0,
                                           soft.rearrange("p t d -> p (t d)"), ALU.max, ALU.add).then_inc(c_sp, 1)
                if (t := tile(MAIN + 15)) and t.s % TB == 0:
                    dve.wait_ge(c_sp, t.g + 1)
                    xg = x[:, bass.ds(t.n, TB), :]
                    V.tensor_tensor(xg, xg, soft, ALU.add).then_inc(c_x, 1)
            lagged(dve, emit, T, UA, LAG_C)

        def stage_c_act(act):
            S = nc.scalar
            b_is_over(act)
            S.activation(gexp, gap[:], ACT.Exp).then_inc(c_gexp, 1)

            def emit(tile):
                if t := tile(MAIN + 1):
                    act.wait_ge(c_tr, t.n + 1)
                    at_least(act, c_pre, t.n - 1)
                    S.copy(qxT[:, t.s % 2], ps[:, 2 + t.s % 2, 0:2 * D]).then_inc(c_tc, 1)
                sf = soft.rearrange("p t d -> p (t d)")
                if (t := tile(MAIN + 10)) and t.s % TB == 0:
                    b0 = 4 + 2 * (t.s // TB)
                    act.wait_ge(c_pre, (t.g + 1) * TB)
                    at_least(act, c_x, t.g)
                    S.activation(sf, ps[:, b0:b0 + 2].rearrange("p a b -> p (a b)"), ACT.Abs).then_inc(c_abs, 1)
                if (t := tile(MAIN + 11)) and t.s % TB == 0:
                    act.wait_ge(c_abs, t.g + 1)
                    S.activation(sf, sf, ACT.Exp, scale=-1.0).then_inc(c_exp, 1)
                if (t := tile(MAIN + 13)) and t.s % TB == 0:
                    act.wait_ge(c_exp, t.g + 1)
                    S.activation(sf, sf, ACT.Ln, bias=1.0).then_inc(c_ln, 1)
            lagged(act, emit, T, UA, LAG_C)

        def stage_c_pe(pe):
            M = nc.tensor
            b_is_over(pe)

            def emit(tile):
                if t := tile(MAIN):
                    par, i = t.s // TB, t.s % TB
                    pe.wait_ge(c_xs, t.g + 1)
                    at_least(pe, c_q, t.n - 1)
                    pe.wait_ge(c_adj[par], (graph_loads(t) - 1 + TB) * 16)
                    for m in range(TB):
                        mm = M.matmul(ps[:, t.s % 2, 0:D], adjT[:, par, m, i * P:(i + 1) * P], xsC[:, par, m],
                                      start=(m == 0), stop=(m == TB - 1))
                    mm.then_inc(c_agg, 1)
                if t := tile(MAIN + 1):
                    par, i = t.s // TB, t.s % TB
                    pe.wait_ge(c_q, t.n + 1)
                    at_least(pe, c_tc, t.n - 1)
                    M.transpose(ps[:, 2 + t.s % 2, 0:D], xnC[:, par, i], ident[:])
                    M.transpose(ps[:, 2 + t.s % 2, D:2 * D], qC[:, t.s % 2], ident[:]).then_inc(c_tr, 1)
                if t := tile(MAIN + 2):
                    par, i = t.s // TB, t.s % TB
                    pe.wait_ge(c_tc, t.n + 1)
                    if i == 0:
                        at_least(pe, c_x, t.g - 1)
                    o = ps[:, 4 + 2 * par + i // 4, (i % 4) * D:(i % 4 + 1) * D]
                    M.matmul(o, qxT[:, t.s % 2, 0:D], wsn[:, 0], start=True, stop=False)
                    M.matmul(o, qxT[:, t.s % 2, D:2 * D], wsn[:, 1], start=False, stop=True).then_inc(c_pre, 1)
            lagged(pe, emit, T, UA, LAG_C)

        wd = carver()
        zD = wd([2, D])
        zTD = wd([2, D])
        hD = [wd([2, HB * P]) for _ in range(L1 + 1)]
        weff = [wd([2, HB, HE]) for _ in range(L1)]
        bnD = wd([2, 6])
        mvD = wd([4, 2])
        rsD = wd([4])

        def stage_d_sp(sp):
            for l in range(L1):
                sp.wait_ge(c_agg, T - (L1 - 1 - l) * TB)
                sp.dma_start(adjT[:, l].rearrange("p a b -> p (a b)"), in_ap["wr"][:, l]).then_inc(d_wr[l], 16)

        def stage_d_out(sp):
            with sp.Fori(0, T // UD) as b:
                sp.wait_ge(d_x, (b + 1) * UD)
                sp.dma_start(out[:, bass.ds(b * UD, UD), :], x[:, bass.ds(b * UD, UD), :]).then_inc(s_out, 16)
            sp.wait_ge(s_out, 16 * (T // UD))

        def stage_d_dve(dve):
            V = nc.vector
            dve.wait_ge(c_x, B)
            wrv = [adjT[:, l].rearrange("p a b -> p (a b)").rearrange("p (e c h) -> p e c h", e=E1, c=HB) for l in range(L1)]

            def emit(tile):
                if t := tile(0):
                    V.bn_stats(bnD[:, t.s % 2], row(x, t.n)).then_inc(d_bn, 1)
                    dve.wait_ge(d_bn, t.n + 1)
                    settled(dve, s_passed_v)
                    V.bn_aggr(mvD[:, t.s % 4], bnD[:, t.s % 2]).then_inc(d_stats, 1)
                if t := tile(1):
                    dve.wait_ge(d_rs, t.n + 1)
                    at_least(dve, d_tr, t.n - 1)
                    V.tensor_scalar(zD[:, t.s % 2], row(x, t.n), mvD[:, t.s % 4, 0:1], rsD[:, t.s % 4:t.s % 4 + 1],
                                    ALU.subtract, ALU.mult).then_inc(d_z, 1)
                for l in range(L1):
                    if t := tile(3 + l):
                        e = dve.value_load(route[0:1, bass.ds(t.n, 1)], min_val=0, max_val=E1 - 1)
                        if isinstance(t.n, int):
                            dve.wait_ge(d_wr[l], 16)
                        at_least(dve, d_h[l + 1], t.n - 1)
                        V.tensor_tensor(weff[l][:, t.s % 2], wrv[l][:, bass.ds(e, 1)].rearrange("p a c h -> p (a c) h"),
                                        ws[:, l * HB:(l + 1) * HB], ALU.add).then_inc(d_weff[l], 1)
                if t := tile(7):
                    dve.wait_ge(d_o, t.n + 1)
                    V.tensor_tensor(row(x, t.n), row(x, t.n), ps[:, 6 + t.s % 2, 0:D], ALU.add).then_inc(d_x, 1)
            lagged(dve, emit, T, UD, LAG_D)

        def stage_d_pool(pool):
            G = nc.gpsimd
            pool.wait_ge(c_x, B)

            def emit(tile):
                if t := tile(0):
                    pool.wait_ge(d_stats, t.n + 1)
                    at_least(pool, d_z, t.n - 3)
                    settled(pool, s_passed_p)
                    G.tensor_scalar(mvD[:, t.s % 4, 1:2], mvD[:, t.s % 4, 1:2], LN_EPS, None, ALU.add).then_inc(d_pv, 1)
                    pool.wait_ge(d_pv, t.n + 1)
                    G.tensor_tensor(rsD[:, t.s % 4:t.s % 4 + 1], mvD[:, t.s % 4, 1:2], mhalf[:, 0:1], ALU.pow).then_inc(d_rs, 1)
            lagged(pool, emit, T, UD, LAG_D)

        def stage_d_act(act):
            S = nc.scalar
            act.wait_ge(c_x, B)

            def emit(tile):
                if t := tile(2):
                    act.wait_ge(d_tr, t.n + 1)
                    at_least(act, d_h[0], t.n - 1)
                    S.copy(zTD[:, t.s % 2], ps[:, 0, 0:P]).then_inc(d_zt, 1)
                for l in range(L1 + 1):
                    if t := tile(3 + l):
                        if l:
                            e = act.value_load(route[0:1, bass.ds(t.n, 1)], min_val=0, max_val=E1 - 1)
                        act.wait_ge(d_h[l], t.n + 1)
                        at_least(act, d_h[l + 1] if l < L1 else d_o, t.n - 1)
                        for c in range(HB):
                            src = (ps[:, 1, c * P:(c + 1) * P] if l == 0 else
                                   ps[:, 2 * l + t.s % 2, c * P:(c + 1) * P])
                            bias = bi[:, c:c + 1] if l == 0 else btab[:, (l - 1) * HB + c, bass.ds(e, 1)]
                            ins = S.activation(hD[l][:, t.s % 2, c * P:(c + 1) * P], src, ACT.Relu, bias=bias)
                        ins.then_inc(d_r[l], 1)
            lagged(act, emit, T, UD, LAG_D)

        def stage_d_pe(pe):
            M = nc.tensor
            pe.wait_ge(c_x, B)

            def emit(tile):
                if t := tile(2):
                    pe.wait_ge(d_z, t.n + 1)
                    at_least(pe, d_zt, t.n)
                    M.transpose(ps[:, 0, 0:P], zD[:, t.s % 2], ident[:]).then_inc(d_tr, 1)
                if t := tile(3):
                    pe.wait_ge(d_zt, t.n + 1)
                    at_least(pe, d_r[0], t.n)
                    for c in range(HB):
                        mm = M.matmul(ps[:, 1, c * P:(c + 1) * P], wi[:, c * P:(c + 1) * P],
                                      zTD[:, t.s % 2], start=True, stop=True)
                    mm.then_inc(d_h[0], 1)
                for l in range(L1):
                    if t := tile(4 + l):
                        pe.wait_ge(d_weff[l], t.n + 1)
                        pe.wait_ge(d_r[l], t.n + 1)
                        at_least(pe, d_r[l + 1], t.n - 1)
                        for c in range(HB):
                            for k in range(HB):
                                mm = M.matmul(ps[:, 2 + 2 * l + t.s % 2, c * P:(c + 1) * P], weff[l][:, t.s % 2, k, c * P:(c + 1) * P],
                                              hD[l][:, t.s % 2, k * P:(k + 1) * P], start=(k == 0), stop=(k == HB - 1))
                        mm.then_inc(d_h[l + 1], 1)
                if t := tile(6):
                    pe.wait_ge(d_r[L1], t.n + 1)
                    at_least(pe, d_x, t.n - 1)
                    o = ps[:, 6 + t.s % 2, 0:D]
                    for k in range(HB):
                        M.matmul(o, hD[L1][:, t.s % 2, k * P:(k + 1) * P], wo[:, k], start=(k == 0), stop=False)
                    M.matmul(o, ones[0:3, :], rows[:, H0 + D:H0 + 2 * D], start=False, stop=True).then_inc(d_o, 1)
            lagged(pe, emit, T, UD, LAG_D)


        @block.sync
        def _(sp):
            for dst, name in CONST_ROWS:
                sp.dma_start(dst, in_ap[name]).then_inc(s_const_rows, 16)
            half = 2 * TB
            sp.dma_start(x[:, 0:half, :], in_ap["x"][:, 0:half, :]).then_inc(s_x0, 16)

            def load(g, p, first):
                if not first:
                    sp.wait_ge(s_agg, (g - 1) * TB)
                    sp.wait_ge(s_dout, (g - 1) * TB)
                sp.dma_start(adjT[:, p], in_ap["adjT"][bass.ds(g, 1)].rearrange("g p m n -> (g p) m n")).then_inc(s_adj[p], 16)
            load(0, 0, True)
            for dst, name in CONST:
                sp.dma_start(dst, in_ap[name]).then_inc(s_const, 16)
            load(1, 1, True)
            sp.dma_start(x[:, half:T, :], in_ap["x"][:, half:T, :]).then_inc(s_x1, 16)
            for dst, name in CONST1:
                sp.dma_start(dst, in_ap[name]).then_inc(s_const1, 16)
            with sp.Fori(1, B // 2) as bb:
                load(bb * 2, 0, False)
                load(bb * 2 + 1, 1, False)
            for dst, name in CONST2:
                sp.dma_start(dst, in_ap[name]).then_inc(s_const2, 16)
            route_end_sp(sp)
            stage_b_sp(sp)
            stage_c_sp_loop(sp)
            stage_d_sp(sp)
            stage_d_out(sp)

        @block.vector
        def _(dve):
            V = nc.vector
            V.memset(mhalf[:], -0.5)
            V.memset(ones[:], 1.0)
            V.memset(xn[:, :, D:D + 1], 1.0)
            V.memset(chosen, 0.0)
            V.memset(zrow, 0.0).then_inc(r_zero, 1)
            bias_n = [0]

            def bias_link(ins):
                bias_n[0] += 1
                ins.then_inc(s_bias, 1)
                dve.wait_ge(s_bias, bias_n[0])

            dve.wait_ge(s_const_rows, 16 * len(CONST_ROWS))
            bf = rows[:]
            src, a, b, c = (rows_f[:, k, :] for k in range(4))
            bias_link(V.tensor_scalar(src[:, 0:H0], src[:, 0:H0], WSCALE, None, ALU.mult))
            bias_link(V.tensor_copy(bf, src))
            bias_link(V.tensor_copy(a, bf))
            bias_link(V.tensor_tensor(b, src, a, ALU.subtract))
            bias_link(V.tensor_scalar(c, a, sel3[0:3, 0:1], None, ALU.mult))
            bias_link(V.tensor_copy(bf, b))
            bias_link(V.tensor_copy(a, bf))
            bias_link(V.tensor_tensor(b, b, a, ALU.subtract))
            bias_link(V.scalar_tensor_tensor(c, a, sel3[0:3, 1:2], c, ALU.mult, ALU.add))
            bias_link(V.scalar_tensor_tensor(c, b, sel3[0:3, 2:3], c, ALU.mult, ALU.add))
            bias_link(V.tensor_copy(bf, c))

            prep_n = [0]

            def link(ins):
                prep_n[0] += 1
                ins.then_inc(s_prep_v, 1)
                dve.wait_ge(s_prep_v, prep_n[0])

            def split_w1():
                dve.wait_ge(s_const, 16 * len(CONST))
                V.tensor_copy(ident16[:], ident[:])
                V.tensor_scalar(w1_f[:], w1_f[:], WSCALE, None, ALU.mult).then_inc(s_w1, 1)
                dve.wait_ge(s_w1, 1)
                V.tensor_copy(w1[:, 0], w1_f[:]).then_inc(s_w1, 1)
                dve.wait_ge(s_w1, 2)
                V.tensor_tensor(w1[:, 1], w1_f[:], w1[:, 0], ALU.subtract).then_inc(s_w1, 1)

            def prepare_first():
                dve.wait_ge(s_const1, 16 * len(CONST1))
                V.tensor_copy(tri[:], tri_f[:])
                link(V.tensor_scalar(beta_b[:], ident[:], 0.0, gcol[:, 1:2], ALU.mult, ALU.add))
                link(V.tensor_scalar(gcol[:, 2:3], gcol[:, 0:1], WSCALE, None, ALU.mult))

            def prepare_second():
                dve.wait_ge(s_prep_t, 1)
                V.tensor_tensor(eb1[:], eb1[:], ps[:, 7, 0:E * HB], ALU.add)
                V.tensor_tensor(rb[:], rb[:], ps[:, 7, E * HB:E * HB + E].unsqueeze(1).to_broadcast([P, TB, E]), ALU.add)
                link(V.tensor_scalar(ew1_f[:], ew1_f[:], gcol[:, 2:3], None, ALU.mult))
                link(V.tensor_scalar(rw_f[:, 0, :], rw_f[:, 0, :], gcol[:, 2:3], None, ALU.mult))

            def prepare_third():
                ew1v = ew1[:].rearrange("p (e s) h -> p e s h", s=2)
                link(V.tensor_copy(ew1v[:, :, 0, :], ew1_f[:]))
                V.tensor_tensor(ew1v[:, :, 1, :], ew1_f[:], ew1v[:, :, 0, :], ALU.subtract)
                link(V.tensor_copy(rw[:, 0, :], rw_f[:, 0, :]))
                link(V.tensor_tensor(rw[:, 1, :], rw_f[:, 0, :], rw[:, 0, :], ALU.subtract))

            def emit(tile):
                if t := tile(0):
                    dve.wait_ge(s_x1 if not isinstance(t.n, int) else s_x0, 16)
                    V.bn_stats(bnA[:, t.s % 2], row(x, t.n)).then_inc(s_vc, 1)
                    dve.wait_ge(s_vc, t.n + 1)
                    settled(dve, s_passed_v)
                    V.bn_aggr(mvA[:, t.s % 4, :], bnA[:, t.s % 2]).then_inc(s_stats, 1)
                if t := tile(12):
                    dve.wait_ge(s_rms, t.n + 1)
                    at_least(dve, s_silu, t.n - 1)
                    V.scalar_tensor_tensor(u[:, t.s % 2], ps[:, 3 + t.s % 2], rsA[:, t.s % 4, 1:2], rmsw[:],
                                           ALU.mult, ALU.mult).then_inc(s_u, 1)
                if t := tile(1):
                    dve.wait_ge(s_rstd, t.n + 1)
                    at_least(dve, s_agg, (t.g - 1) * TB)
                    V.tensor_scalar(xn[:, t.s, 0:D], row(x, t.n), mvA[:, t.s % 4, 0:1], rsA[:, t.s % 4, 0:1],
                                    ALU.subtract, ALU.mult).then_inc(s_norm, 1)
                if t := tile(14):
                    dve.wait_ge(s_y, t.n + 1)
                    V.tensor_tensor(row(x, t.n), row(x, t.n), ps[:, 6, 0:D], ALU.add).then_inc(s_x, 1)
                if t := tile(9):
                    if is_tile(t, 0):
                        split_w1()
                    dve.wait_ge(s_agg, t.n + 1)
                    at_least(dve, s_aggt, t.n - 1)
                    for dst in (agg_f, agg_hl[:, t.s % 2, 0]):
                        ins = V.scalar_tensor_tensor(dst, xn[:, t.s, 0:D], epsx[:, 0:1], ps[:, t.s % 2, 0:D], ALU.mult, ALU.add)
                    ins.then_inc(s_aggf, 1)
                    V.tensor_copy(din[:, bass.ds(t.n, 1)], ps[:, t.s % 2, D:D + 1]).then_inc(s_aggv, 1)
                    dve.wait_ge(s_aggf, t.n + 1)
                    V.tensor_tensor(agg_hl[:, t.s % 2, 1], agg_f, agg_hl[:, t.s % 2, 0], ALU.subtract).then_inc(s_agglo, 1)
                if is_tile(tile(13), 0):
                    prepare_first()
                if is_tile(tile(14), 0):
                    prepare_second()
                if is_tile(tile(15), 0):
                    prepare_third()
                route_dve_stats(dve, tile)
                route_dve(dve, tile)
            lagged(dve, emit, T, UA, LAG_A)
            route_end_dve(dve)
            stage_b_dve(dve)
            stage_c_dve(dve)
            stage_d_dve(dve)

        @block.gpsimd
        def _(pool):
            G = nc.gpsimd
            pool.wait_ge(s_bias, 1)

            def emit(tile):
                if t := tile(11):
                    pool.wait_ge(s_sq, t.n + 1)
                    at_least(pool, s_u, t.n - 3)
                    settled(pool, s_passed_p)
                    G.tensor_scalar(ssA[:, t.s % 4, 1:2], ssA[:, t.s % 4, 0:1], 1.0 / H0, RMS_EPS * WSCALE ** 2, ALU.mult, ALU.add).then_inc(s_pc, 1)
                    pool.wait_ge(s_pc, pool_count(t, 11))
                    G.tensor_tensor(rsA[:, t.s % 4, 1:2], ssA[:, t.s % 4, 1:2], mhalf[:, 0:1], ALU.pow).then_inc(s_rms, 1)
                if t := tile(0):
                    pool.wait_ge(s_stats, t.n + 1)
                    at_least(pool, s_norm, t.n - 3)
                    settled(pool, s_passed_p)
                    G.tensor_scalar(mvA[:, t.s % 4, 1:2], mvA[:, t.s % 4, 1:2], LN_EPS, None, ALU.add).then_inc(s_pc, 1)
                    pool.wait_ge(s_pc, pool_count(t, 0))
                    G.tensor_tensor(rsA[:, t.s % 4, 0:1], mvA[:, t.s % 4, 1:2], mhalf[:, 0:1], ALU.pow).then_inc(s_rstd, 1)
                route_pool(pool, tile)

            def pool_count(t, lag):
                if lag == 11:
                    n = t.n + 11
                    if isinstance(t.n, int):
                        return t.n + 1 + min(n, T)
                    return t.n + 1 + n
                n = t.n
                if isinstance(n, int):
                    return n + 1 + max(0, n - 11 + 1)
                return n + 1 + n - 10
            lagged(pool, emit, T, UA, LAG_A)
            factors_pool(pool)
            stage_b_pool(pool)
            stage_c_pool(pool)
            stage_d_pool(pool)

        @block.scalar
        def _(act):
            S = nc.scalar

            def emit(tile):
                if t := tile(10):
                    act.wait_ge(s_aggt, t.n + 1)
                    at_least(act, s_h, t.n - 1)
                    S.copy(aggT[:, t.s % 2], aggT_ps).then_inc(s_aggc, 1)
                if t := tile(12):
                    act.wait_ge(s_u, t.n + 1)
                    at_least(act, s_st, t.n - 1)
                    S.activation(su[:, t.s % 2], u[:, t.s % 2], ACT.Silu).then_inc(s_silu, 1)
                route_act(act, tile, 0)
                if t := tile(10):
                    act.wait_ge(s_h, t.n + 1)
                    at_least(act, s_rms, t.n - 3)
                    S.activation(junk, ps[:, 3 + t.s % 2], ACT.Square, accum_out=ssA[:, t.s % 4, 0:1]).then_inc(s_sq, 1)
                if t := tile(12):
                    act.wait_ge(s_st, t.n + 1)
                    at_least(act, s_y, t.n - 1)
                    S.copy(sT[:, t.s % 2], ps[:, 5]).then_inc(s_stc, 1)
                route_act(act, tile, 1)
                if t := tile(9):
                    p, i = t.s // TB, t.s % TB
                    act.wait_ge(s_adj[p], t.g * 8 + 16 - 8 * p)
                    at_least(act, s_dout, t.n)
                    S.activation(junk_n, adjT[:, p, i], ACT.Identity, accum_out=dout[:, bass.ds(t.n, 1)]).then_inc(s_dout, 1)
                route_act_hi(act, tile)
            lagged(act, emit, T, UA, LAG_A)
            stage_b_act(act)
            stage_c_act(act)
            stage_d_act(act)

        @block.tensor
        def _(pe):
            M = nc.tensor

            def prepare():
                pe.wait_ge(s_prep_v, 1)
                for k in range(E * HB):
                    M.matmul(ps[:, 7, k:k + 1], ew1_f[:, k // HB, (k % HB) * P:(k % HB + 1) * P], gcol[:, 1:2],
                             start=True, stop=True)
                M.matmul(ps[:, 7, E * HB:E * HB + E], beta_b[:], rw_f[:, 0, :], start=True, stop=True).then_inc(s_prep_t, 1)

            def emit(tile):
                if t := tile(10):
                    if is_tile(t, 0):
                        pe.wait_ge(s_const, 16 * len(CONST))
                        pe.wait_ge(s_bias, 11)
                        pe.wait_ge(s_w1, 3)
                    pe.wait_ge(s_agglo, t.n + 1)
                    at_least(pe, s_aggc, t.n)
                    for h in range(2):
                        mm = M.transpose(aggT_ps[:, h], agg_hl[:, t.s % 2, h], ident16[:])
                    mm.then_inc(s_aggt, 1)
                if t := tile(9):
                    p, i = t.s // TB, t.s % TB
                    pe.wait_ge(s_adj[p], t.g * 8 + 16 - 8 * p)
                    pe.wait_ge(s_norm, (t.g + 1) * TB)
                    at_least(pe, s_aggv, t.n - 1)
                    for m in range(TB):
                        mm = M.matmul(ps[:, t.s % 2, 0:D + 1], adjT[:, p, m, i * P:(i + 1) * P],
                                      xn[:, p * TB + m, :], start=(m == 0), stop=(m == TB - 1))
                    mm.then_inc(s_agg, 1)
                route_logits(pe, tile)
                route_ranks(pe, tile)
                if t := tile(10):
                    pe.wait_ge(s_aggc, t.n + 1)
                    at_least(pe, s_u, t.n - 1)
                    bank = ps[:, 3 + t.s % 2]
                    for n, (a, w) in enumerate(((0, 0), (0, 1), (1, 0))):
                        M.matmul(bank, aggT[:, t.s % 2, a], w1[:, w], start=(n == 0), stop=False)
                    M.matmul(bank, ones[0:3, :], rows[:, 0:H0], start=False, stop=True).then_inc(s_h, 1)
                route_transpose(pe, tile, 1)
                if t := tile(12):
                    pe.wait_ge(s_silu, t.n + 1)
                    at_least(pe, s_stc, t.n)
                    for c in range(HC):
                        mm = M.transpose(ps[:, 5, c * P:(c + 1) * P], su[:, t.s % 2, c * P:(c + 1) * P], ident[:])
                    mm.then_inc(s_st, 1)
                if t := tile(13):
                    pe.wait_ge(s_stc, t.n + 1)
                    at_least(pe, s_x, t.n)
                    for c in range(HC):
                        M.matmul(ps[:, 6, 0:D], sT[:, t.s % 2, c * P:(c + 1) * P], w2[:, c, :],
                                 start=(c == 0), stop=False)
                    M.matmul(ps[:, 6, 0:D], ones[0:3, :], rows[:, H0:H0 + D], start=False, stop=True).then_inc(s_y, 1)
                if is_tile(tile(14), 0):
                    prepare()
                route_transpose(pe, tile, 0)
            lagged(pe, emit, T, UA, LAG_A)
            route_end_pe(pe)
            stage_b_pe(pe)
            stage_c_pe(pe)
            stage_d_pe(pe)


_OUTS = [((B, N, D), "float32")]


def kernel(**inputs):
    import numpy as np
    import concourse.bacc as _bacc
    from concourse import mybir as _mybir
    from concourse.bass_utils import run_bass_kernel_spmd as _run

    f = lambda k: np.asarray(inputs[k])
    rep = lambda v, n=P: np.ascontiguousarray(np.broadcast_to(v.reshape(1, -1), (n, v.size)))
    arrays = {
        "x": f("x").reshape(T, P, D).transpose(1, 0, 2),
        "adjT": f("adj").transpose(0, 2, 1).reshape(B, TB, P, N).transpose(0, 2, 1, 3),
        "c_ident": np.eye(P, dtype=np.float32),
        "c_tri": np.triu(np.ones((P, P), np.float32), 1),
        "c_iota": rep(np.tile(np.arange(E, dtype=np.float32), TB)),
        "c_ecap": rep(np.tile(np.arange(E, dtype=np.float32) * CAP, TB)),
        "c_iotat": np.arange(NT, dtype=np.float32).reshape(1, NT),
        "c_sel3": np.eye(P, 3, dtype=np.float32),
        "w1": f("L0_gnn_W1"),
        "w2": f("L0_gnn_W2").reshape(HC, P, D).transpose(1, 0, 2).reshape(P, HC * D),
        "rmsw": rep(f("L0_gnn_rms_weight")),
        "epsx": rep(f("L0_gnn_epsilon")),
        "rows": rep(np.concatenate([f("L0_gnn_b1"), f("L0_gnn_b2"), f("L1_ffn_bo")]), 3),
    }
    arrays |= {
        "gcol": np.stack([f("L0_ffn_gamma"), f("L0_ffn_beta")], 1),
        "ew1": f("L0_ffn_W1").transpose(1, 0, 2).reshape(P, E * HE),
        "eb1": f("L0_ffn_b1").reshape(E, HB, P).transpose(2, 0, 1).reshape(P, E * HB),
        "rw": f("L0_ffn_Wr"),
        "rb": rep(np.tile(f("L0_ffn_br"), TB)),
        "ew2": f("L0_ffn_W2").reshape(E, HB, P, D).transpose(2, 0, 1, 3).reshape(P, E * HB * D),
        "eb2": rep(f("L0_ffn_b2")),
        "lng": rep(np.concatenate([f("L1_gnn_gamma"), f("L1_gnn_beta")])),
        "wsn": np.concatenate([f("L1_gnn_W_self"), f("L1_gnn_W_neigh")], 1),
        "wi": f("L1_ffn_Wi").T,
        "bi": f("L1_ffn_bi").reshape(HB, P).T,
        "ws": f("L1_ffn_Ws").reshape(L1, HE, HB, P).transpose(3, 0, 2, 1).reshape(P, -1),
        "bs": f("L1_ffn_bs").reshape(L1 * HB, P).T,
        "br": f("L1_ffn_br").reshape(L1, E1, HB, P).transpose(3, 0, 2, 1).reshape(P, -1),
        "wo": f("L1_ffn_Wo").T.reshape(HB, P, D).transpose(1, 0, 2).reshape(P, HB * D),
        "wr": f("L1_ffn_Wr").reshape(L1, E1, HE, HB, P).transpose(4, 0, 1, 3, 2).reshape(P, L1, -1),
        "route": f("L1_ffn_route_id").reshape(1, T),
    }
    nc = _bacc.Bacc("TRN2", target_bir_lowering=False, num_devices=1)
    aps, data = {}, {}
    for name, a in arrays.items():
        a = np.ascontiguousarray(a)
        data[f"in_{name}"] = a
        aps[name] = nc.dram_tensor(f"in_{name}", a.shape, _mybir.dt.from_np(a.dtype), kind="ExternalInput").ap()
    out = nc.dram_tensor("out_0", (P, T, D), F32, kind="ExternalOutput").ap()
    build(nc, aps, out)
    r = _run(nc, [data], core_ids=[0])
    got = np.asarray(r.results[0]["out_0"])
    return np.ascontiguousarray(got.transpose(1, 0, 2)).reshape(B, N, D)
```

```python
from contextlib import ExitStack

import concourse.bass as bass
from concourse import mybir

ALU = mybir.AluOpType
ACT = mybir.ActivationFunctionType
F32 = mybir.dt.float32
F16 = mybir.dt.float16
BF16 = mybir.dt.bfloat16
I32 = mybir.dt.int32
U32 = mybir.dt.uint32
AX_X = mybir.AxisListType.X

P = 128
B, N, D = 8, 1024, 128
T = B * N // P
TB = N // P
H0 = 512
HC = H0 // P
E, HE = 8, 256
HB = HE // P
TS = 512
NT = (2 * B * N + E * (TS - 1)) // TS
CAP = B * N + TS
L1, E1 = 2, 16
LN_EPS = 1e-5
RMS_EPS = 1e-6
WSCALE = 16.0
UA = 2 * TB
RT = 4
RINGS = UA // RT
UB = 12
ZIN = 4
UD = 16
LAG_D = 7


def at_step(step, total, unroll):
    return lambda k: Tile(0, step - k, unroll) if 0 <= step - k < total else None


class Tile:

    def __init__(self, base, j, unroll):
        self.n = base * unroll + j
        self.s = j % unroll
        self.g = base * (unroll // TB) + j // TB if unroll >= TB else None
        self.base, self.j = base, j


def lagged(eng, emit, total, unroll, lag, begun=0, following=None):
    first, loops = max(1, -(-lag // unroll)), total // unroll
    for step in range(begun, first * unroll):
        emit(at_step(step, total, unroll))
    with eng.Fori(first, loops) as base:
        for j in range(unroll):
            emit(lambda k: Tile(base, j - k, unroll))
    for step in range(loops * unroll, total + lag):
        emit(at_step(step, total, unroll))
        if following:
            following(step)


def is_tile(t, n):
    return t is not None and isinstance(t.n, int) and t.n == n


def at_least(eng, sem, n):
    if not isinstance(n, int) or n > 0:
        eng.wait_ge(sem, n)


def settled(eng, passed):
    eng.sem_inc(passed, 1)


def expert_of(known, eng, table, t, experts):
    key = (t.base if isinstance(t.base, int) else "loop", t.j)
    if key not in known:
        known[key] = eng.value_load(table[0:1, bass.ds(t.n, 1)], min_val=0, max_val=experts - 1)
    return known[key]


def row(t, i):
    return t[:, i] if isinstance(i, int) else t[:, bass.ds(i, 1)].rearrange("p a b -> p (a b)")


def build(nc, inp, out):
    with ExitStack() as ctx:
        def sb(name, shape, dt=F32):
            return ctx.enter_context(nc.sbuf_tensor(name, shape, dt))

        def sem(name):
            return ctx.enter_context(nc.semaphore(name))

        ps = ctx.enter_context(nc.psum_tensor("ps", [P, 8, 512], F32))

        x = sb("x", [P, T, D])
        adjT = sb("adjT", [P, 2, TB, N])
        ident = sb("ident", [P, P])
        ident16 = sb("ident16", [P, P], F16)
        tri = sb("tri", [P, P], BF16)
        ones = sb("ones", [P, P], BF16)
        tri_f = sb("tri_f", [P, P])
        iota_e = sb("iota_e", [P, TB, E])
        ecap = sb("ecap", [P, TB, E])
        mhalf = sb("mhalf", [P, T])
        sel3 = sb("sel3", [P, 3])
        w1_f = sb("w1_f", [P, H0])
        w1 = sb("w1", [P, 2, H0], F16)
        w2 = sb("w2", [P, HC, D])
        rmsw = sb("rmsw", [P, H0])
        epsx = sb("epsx", [P, 1])
        ew_f = sb("ew_f", [P, E, HE])
        beta_b = sb("beta_b", [P, P])
        rows = sb("rows", [3, H0 + 2 * D], BF16)
        gcol = sb("gcol", [P, 3])
        ew1 = sb("ew1", [P, E * 2, HE], F16)
        ew2 = sb("ew2", [P, E, 2 * HB * D], F16)
        eb1 = sb("eb1", [P, E * HB])
        eb2 = sb("eb2", [P, E, D])
        rw_f = sb("rw_f", [P, 2, E])
        rw = sb("rw", [P, 2, E], F16)
        rb = sb("rb", [P, TB, E])
        lng = sb("lng", [P, 2, D])
        wsn = sb("wsn", [P, 2, D])
        wi = sb("wi", [P, HE])
        bi = sb("bi", [P, HB])
        ws = sb("ws", [P, L1 * HB, HE])
        bs = sb("bs", [P, L1 * HB])
        btab = sb("btab", [P, L1 * HB, E1])
        wo = sb("wo", [P, HB, D])
        route = sb("route", [1, T], I32)
        din = sb("din", [P, T])
        s_in = sb("s_in", [P, T])
        dout = sb("dout", [P, T])
        s_out_neg = sb("s_out_neg", [P, T])
        smask = sb("smask", [P, T])
        gap = sb("gap", [P, T])
        gw = sb("gw", [P, 2, T])
        onehot = sb("onehot", [P, T, 2, E])
        rank = sb("rank", [P, T, E])
        etab = sb("etab", [1, NT], I32)
        btable = sb("btable", [1, NT], I32)
        back = sb("back", [P, T, 2], U32)
        WORK = 12016
        work = sb("work", [P, WORK])

        def carver(start=0):
            at = [start]

            def carve(shape, dt=F32):
                n = 1
                for k in shape:
                    n *= k
                words = (n * mybir.dt.size(dt) + 3) // 4
                a = work[:, at[0]:at[0] + words]
                at[0] += words
                assert at[0] <= WORK, at[0]
                if dt != F32:
                    a = a.bitcast(dt)
                names = " ".join("abcd"[:len(shape)])
                return a.rearrange(f"p ({names}) -> p {names}", **dict(zip("abcd", shape)))
            return carve

        xs_rows = nc.dram_tensor("expert_rows", [E * CAP + TS, 2 * D], F16, kind="Internal").ap()
        y_rows = nc.dram_tensor("expert_out", [NT * TS, D], F32, kind="Internal").ap()

        block = ctx.enter_context(nc.Block())

        s_const_rows = sem("s_const_rows")
        s_const = sem("s_const")
        s_const1 = sem("s_const1")
        s_x0 = sem("s_x0")
        s_x1 = sem("s_x1")
        s_bias = sem("s_bias")
        s_w1 = sem("s_w1")
        s_prep_v = sem("s_prep_v")
        s_prep_t = sem("s_prep_t")
        s_adj = [sem("s_adj0"), sem("s_adj1")]
        s_stats = sem("s_stats")
        s_rstd = sem("s_rstd")
        s_norm = sem("s_norm")
        s_agg = sem("s_agg")
        s_aggf = sem("s_aggf")
        s_aggv = sem("s_aggv")
        s_agglo = sem("s_agglo")
        s_aggt = sem("s_aggt")
        s_aggc = sem("s_aggc")
        s_h = sem("s_h")
        s_sq = sem("s_sq")
        s_rms = sem("s_rms")
        s_u = sem("s_u")
        s_silu = sem("s_silu")
        s_st = sem("s_st")
        s_stc = sem("s_stc")
        s_y = sem("s_y")
        s_x = sem("s_x")
        s_ms = sem("s_ms")
        s_var = sem("s_var")
        s_bn = sem("s_bn")
        s_passed_v = sem("s_passed_v")
        s_passed_p = sem("s_passed_p")
        s_out = sem("s_out")
        c_agg = sem("c_agg")
        s_dout = sem("s_dout")
        c_pc = sem("c_pc")
        c_factors = sem("c_factors")
        c_places = sem("c_places")
        c_comb = sem("c_comb")
        c_stats = sem("c_stats")
        c_pv = sem("c_pv")
        c_rs = sem("c_rs")
        c_q = sem("c_q")
        c_vp = sem("c_vp")
        c_gexp = sem("c_gexp")
        c_v0 = sem("c_v0")
        c_bn = sem("c_bn")
        c_z = sem("c_z")
        c_xn = sem("c_xn")
        c_xs = sem("c_xs")
        c_tr = sem("c_tr")
        c_tc = sem("c_tc")
        c_pre = sem("c_pre")
        c_abs = sem("c_abs")
        c_exp = sem("c_exp")
        c_ln = sem("c_ln")
        c_sp = sem("c_sp")
        c_x = sem("c_x")
        s_const3 = sem("s_const3")
        c_adj = [sem("c_adj0"), sem("c_adj1")]
        c_gath = [[sem(f"c_gath{p}{h}") for h in range(2)] for p in range(2)]
        d_wr = [sem(f"d_wr{l}") for l in range(L1)]
        d_bn = sem("d_bn")
        d_stats = sem("d_stats")
        d_pv = sem("d_pv")
        d_rs = sem("d_rs")
        d_z = sem("d_z")
        d_tr = sem("d_tr")
        d_zt = sem("d_zt")
        d_weff = [sem(f"d_weff{l}") for l in range(L1)]
        d_h = [sem(f"d_h{l}") for l in range(L1 + 1)]
        d_r = [sem(f"d_r{l}") for l in range(L1 + 1)]
        d_o = sem("d_o")
        d_x = sem("d_x")
        r_iota = sem("r_iota")
        r_padded = sem("r_padded")
        r_zero = sem("r_zero")
        r_oh = sem("r_oh")
        r_spot = sem("r_spot")
        r_end = sem("r_end")
        r_back = sem("r_back")
        s_const2 = sem("s_const2")
        r_stats = sem("r_stats")
        r_sc = sem("r_sc")
        r_z = sem("r_z")
        r_hi = sem("r_hi")
        r_lo = sem("r_lo")
        r_tr = sem("r_tr")
        r_zt = sem("r_zt")
        r_lg = sem("r_lg")
        r_pick = sem("r_pick")
        r_bn = sem("r_bn")
        r_pv = sem("r_pv")
        r_logit = sem("r_logit")
        r_top = sem("r_top")
        r_topi = sem("r_topi")
        r_topf = sem("r_topf")
        r_sum = sem("r_sum")
        r_hit = sem("r_hit")
        r_slotf = sem("r_slotf")
        r_chosen = sem("r_chosen")
        r_pos = sem("r_pos")
        r_slot = sem("r_slot")
        r_scat = [sem(f"r_scat{k}") for k in range(RINGS)]
        r_cnt = sem("r_cnt")
        r_tab = sem("r_tab")
        r_pad = sem("r_pad")
        b_load = [sem(f"b_load{k}") for k in range(ZIN)]
        b_tr = sem("b_tr")
        b_zt = sem("b_zt")
        b_h = sem("b_h")
        b_gelu = sem("b_gelu")
        b_w2 = sem("b_w2")
        b_lo = sem("b_lo")
        b_y = sem("b_y")
        b_out = sem("b_out")
        b_store = [sem(f"b_store{k}") for k in range(3)]

        in_ap = inp

        wa = carver()
        z = wa([RT, D])
        zT = wa([RT, 2, P], F16)
        zhl = wa([RINGS, RT, 2 * D], F16)
        rows_f = carver()([4, H0 + 2 * D])[0:3]
        xn = wa([UA, D + 1])
        agg_f = wa([D])
        agg_hl = wa([2, 2, D], F16)
        aggT = wa([2, 2, P], F16)
        u = wa([2, H0])
        su = wa([2, H0])
        sT = wa([2, H0])
        junk = wa([H0])
        junk_n = wa([N], BF16)
        mvA = wa([4, 2])
        bnA = wa([2, 6])
        rsA = wa([4, 2])
        ssA = wa([4, 2])
        bnR = wa([RT, 6])
        mvR = wa([RT, 2])
        scR = wa([RT])
        logit = wa([RT, E])
        top = wa([RT, 8])
        topi = wa([RT, 8], U32)
        topf = wa([RT, 2])
        pick = wa([RT, E], BF16)
        chosen = wa([E], BF16)
        chosen_g = wa([E])
        spot = wa([RT, E])
        hit = wa([2, RT, E])
        slot_f = wa([2, RT])
        slot = wa([RINGS, 2, RT], U32)
        zrow = wa([TS // P, 2 * D], F16)
        aggT_ps = ps[:, 2].bitcast(F16)[:, 0:2 * P].rearrange("p (h q) -> p h q", h=2)
        wt = carver((RINGS + 2) * RT * D)
        cnt_i = wt([E], I32)
        tiles_e = wt([E])
        first_t = wt([E + 1])
        first_r = wt([E])
        pad_f = wt([E])
        pad = wt([E], I32)
        iota_t = wt([NT])
        over = wt([NT, E])
        part = wt([NT, E])
        e_f = wt([NT])
        b_f = wt([NT])
        wh = wt([T, E])
        hit2 = wt([T, 2, E])
        back_f = wt([T, 2])

        CONST_ROWS = [(sel3[:], "c_sel3"), (rows_f[:, 0, :], "rows")]
        CONST = [
            (ident[:], "c_ident"), (epsx[:], "epsx"), (w1_f[:], "w1"), (rmsw[:], "rmsw"),
            (w2[:].rearrange("p c d -> p (c d)"), "w2"),
        ]
        CONST1 = [
            (tri_f[:], "c_tri"), (iota_e[:].rearrange("p t e -> p (t e)"), "c_iota"), (ecap[:].rearrange("p t e -> p (t e)"), "c_ecap"),
            (gcol[:, 0:2], "gcol"), (ew_f[:].rearrange("p e h -> p (e h)"), "ew1"), (eb1[:], "eb1"),
            (rw_f[:, 0, :], "rw"), (rb[:].rearrange("p t e -> p (t e)"), "rb"),
        ]
        CONST3 = [
            (lng[:].rearrange("p a d -> p (a d)"), "lng"), (wsn[:].rearrange("p a d -> p (a d)"), "wsn"), (wi[:], "wi"), (bi[:], "bi"),
            (ws[:].rearrange("p a h -> p (a h)"), "ws"), (bs[:], "bs"), (btab[:].rearrange("p a e -> p (a e)"), "br"),
            (wo[:].rearrange("p a d -> p (a d)"), "wo"), (route[:], "route"),
        ]
        PREPARED = 7
        CONST2 = [
            (ew_f[:].rearrange("p e h -> p (e h)"), "ew2"), (eb2[:].rearrange("p e d -> p (e d)"), "eb2"),
        ]

        SCATTERS = 2
        R_STATS, R_Z, R_LO, R_LG, R_PICK, R_POS, R_SCAT = 17, 19, 20, 22, 22, 23, 24
        LAG_A = R_SCAT + 2 * RT // SCATTERS - 1

        def graph_loads(t):
            return (t.g - (t.s // TB)) // 2 + 1 if isinstance(t.n, int) else t.base + t.j // UA + 1

        def group_at(tile, lag):
            t = tile(lag)
            return t if t and t.s % RT == 0 else None

        def group(t):
            return t.n // RT if isinstance(t.n, int) else t.base * RINGS + t.j // RT

        def ring_uses(t):
            return group(t) // RINGS if isinstance(t.n, int) else t.base + t.j // UA

        def route_dve_stats(dve, tile):
            V = nc.vector
            if t := group_at(tile, R_STATS):
                xg = x[:, bass.ds(t.n, RT), :]
                dve.wait_ge(s_x, (group(t) + 1) * RT)
                settled(dve, s_passed_v)
                for i in range(RT):
                    bn = V.bn_stats(bnR[:, i], xg[:, i])
                bn.then_inc(r_bn, 1)
                dve.wait_ge(r_bn, group(t) + 1)
                settled(dve, s_passed_v)
                for i in range(RT):
                    ag = V.bn_aggr(mvR[:, i], bnR[:, i])
                ag.then_inc(r_stats, 1)

        def route_dve(dve, tile):
            V = nc.vector
            if t := group_at(tile, R_Z):
                xg = x[:, bass.ds(t.n, RT), :]
                dve.wait_ge(r_sc, group(t) + 1)
                for i in range(RT):
                    zi = V.tensor_scalar(z[:, i], xg[:, i], mvR[:, i, 0:1], scR[:, i:i + 1], ALU.subtract, ALU.mult)
                zi.then_inc(r_z, 1)
            if t := group_at(tile, R_LO):
                zg = zhl[:, t.s // RT]
                dve.wait_ge(r_z, group(t) + 1)
                dve.wait_ge(r_hi, group(t) + 1)
                V.tensor_tensor(zg[:, :, D:2 * D], z, zg[:, :, 0:D], ALU.subtract).then_inc(r_lo, 1)
            if t := group_at(tile, R_LG):
                dve.wait_ge(r_lg, group(t) + 1)
                V.scalar_tensor_tensor(logit, ps[:, 7, 0:RT * E].rearrange("p (t e) -> p t e", e=E), 1.0 / WSCALE,
                                       rb[:, 0:RT], ALU.mult, ALU.add).then_inc(r_logit, 1)
                dve.wait_ge(r_logit, group(t) + 1)
                settled(dve, s_passed_v)
                for i in range(RT):
                    mx = V.max(top[:, i], logit[:, i])
                mx.then_inc(r_top, 1)
            if t := group_at(tile, R_PICK):
                dve.wait_ge(r_top, group(t) + 1)
                V.tensor_tensor(gap[:, bass.ds(t.n, RT)], top[:, :, 1], top[:, :, 0], ALU.subtract)
                for i in range(RT):
                    mi = V.max_index(topi[:, i], top[:, i], logit[:, i])
                mi.then_inc(r_topi, 1)
                dve.wait_ge(r_topi, group(t) + 1)
                V.tensor_copy(topf, topi[:, :, 0:2]).then_inc(r_topf, 1)
                dve.wait_ge(r_topf, group(t) + 1)
                oh = onehot[:, bass.ds(t.n, RT), :, :]
                for k in range(2):
                    eq = V.tensor_tensor(oh[:, :, k, :], iota_e[:, 0:RT], topf[:, :, k:k + 1].to_broadcast([P, RT, E]), ALU.is_equal)
                eq.then_inc(r_oh, 1)
                dve.wait_ge(r_oh, group(t) + 1)
                V.tensor_tensor(pick, oh[:, :, 0, :], oh[:, :, 1, :], ALU.add).then_inc(r_pick, 1)
            if t := group_at(tile, R_POS):
                oh = onehot[:, bass.ds(t.n, RT), :, :]
                dve.wait_ge(r_pick, group(t) + 1)
                V.tensor_reduce(chosen_g, pick.rearrange("p t e -> p e t"), AX_X, ALU.add).then_inc(r_sum, 1)
                dve.wait_ge(r_pos, group(t) + 1)
                pos = ps[:, 7, 0:RT * E].rearrange("p (t e) -> p t e", e=E)
                V.tensor_tensor(spot, pos, ecap[:, 0:RT], ALU.add).then_inc(r_spot, 1)
                V.tensor_copy(rank[:, bass.ds(t.n, RT), :], pos)
                dve.wait_ge(r_spot, group(t) + 1)
                for k in range(2):
                    ht = V.tensor_tensor(hit[:, k], spot, oh[:, :, k, :], ALU.mult)
                ht.then_inc(r_hit, 1)
                dve.wait_ge(r_sum, group(t) + 1)
                V.tensor_tensor(chosen, chosen, chosen_g, ALU.add)
                dve.wait_ge(r_hit, group(t) + 1)
                V.tensor_reduce(slot_f, hit, AX_X, ALU.add).then_inc(r_slotf, 1)
                dve.wait_ge(r_slotf, group(t) + 1)
                V.tensor_copy(slot[:, t.s // RT], slot_f).then_inc(r_slot, 1)

        def route_pool(pool, tile):
            G = nc.gpsimd
            if t := group_at(tile, R_Z):
                pool.wait_ge(r_stats, group(t) + 1)
                settled(pool, s_passed_p)
                G.tensor_scalar(mvR[:, :, 1], mvR[:, :, 1], 1.0 + LN_EPS, LN_EPS * LN_EPS, ALU.mult, ALU.add).then_inc(r_pv, 1)
                pool.wait_ge(r_pv, group(t) + 1)
                G.tensor_tensor(scR, mvR[:, :, 1], mhalf[:, 0:RT], ALU.pow).then_inc(r_sc, 1)
            for q in range(2 * RT // SCATTERS):
                if t := group_at(tile, R_SCAT + q):
                    if q == 0:
                        pool.wait_ge(r_slot, group(t) + 1)
                        settled(pool, s_passed_p)
                    ring = t.s // RT
                    for n in range(q * SCATTERS, (q + 1) * SCATTERS):
                        i, k = n // 2, n % 2
                        G.indirect_dma_start(xs_rows, bass.IndirectOffsetOnAxis(slot[:, ring, k, i:i + 1], 0),
                                             zhl[:, ring, i, :], None).then_inc(r_scat[ring], 16)

        def route_act_hi(act, tile):
            if t := group_at(tile, R_Z):
                act.wait_ge(r_z, group(t) + 1)
                at_least(act, r_scat[t.s // RT], ring_uses(t) * (2 * RT * 16))
                nc.scalar.copy(zhl[:, t.s // RT, :, 0:D], z).then_inc(r_hi, 1)

        def route_act(act, tile):
            if t := group_at(tile, R_LO + 1):
                act.wait_ge(r_tr, group(t) + 1)
                nc.scalar.copy(zT.rearrange("p t s q -> p (t s q)"), ps[:, 7].bitcast(F16)).then_inc(r_zt, 1)

        def route_transpose(pe, tile):
            if t := group_at(tile, R_LO):
                tr = ps[:, 7].bitcast(F16).rearrange("p (t s q) -> p t s q", t=RT, s=2)
                pe.wait_ge(r_lo, group(t) + 1)
                at_least(pe, r_slot, group(t))
                for i in range(RT):
                    for s in range(2):
                        mm = nc.tensor.transpose(tr[:, i, s], zhl[:, t.s // RT, i, s * D:(s + 1) * D], ident16[:])
                mm.then_inc(r_tr, 1)

        def route_logits(pe, tile):
            if t := group_at(tile, R_LG):
                pe.wait_ge(r_zt, group(t) + 1)
                for i in range(RT):
                    for n, (a, b) in enumerate(((0, 0), (1, 0), (0, 1))):
                        mm = nc.tensor.matmul(ps[:, 7, i * E:(i + 1) * E], zT[:, i, a], rw[:, b], start=(n == 0), stop=(n == 2))
                mm.then_inc(r_lg, 1)

        def route_ranks(pe, tile):
            M = nc.tensor
            if t := group_at(tile, R_POS):
                pe.wait_ge(r_pick, group(t) + 1)
                M.matmul(ps[:, 7, 0:RT * E], tri[:], pick.rearrange("p t e -> p (t e)"), start=True, stop=False)
                for i in range(RT - 1):
                    M.matmul(ps[:, 7, (i + 1) * E:RT * E].rearrange("p (t e) -> p t e", e=E), ones[:],
                             pick[:, i:i + 1, :].to_broadcast([P, RT - 1 - i, E]), start=False, stop=False)
                M.matmul(ps[:, 7, 0:RT * E].rearrange("p (t e) -> p t e", e=E), ones[:],
                         chosen.unsqueeze(1).to_broadcast([P, RT, E]), start=False, stop=True).then_inc(r_pos, 1)

        def route_end_dve(dve):
            V = nc.vector
            V.engine_nop().then_inc(r_chosen, 1)
            link_n = [0]

            def link(ins):
                link_n[0] += 1
                ins.then_inc(r_end, 1)
                dve.wait_ge(r_end, link_n[0])
            dve.wait_ge(r_cnt, 1)
            cnt = ps[:, 7, 0:E]
            V.tensor_tensor(pad_f, cnt, ecap[:, 0, :], ALU.add)
            link(V.tensor_scalar(tiles_e, cnt, float(TS - 1), None, ALU.add))
            V.tensor_copy(pad, pad_f).then_inc(r_pad, 1)
            link(V.tensor_copy(cnt_i, tiles_e))
            link(V.tensor_single_scalar(cnt_i, cnt_i, TS.bit_length() - 1, ALU.logical_shift_right))
            V.memset(first_t[:, 0:1], 0.0)
            link(V.tensor_copy(tiles_e, cnt_i))
            for e in range(E):
                link(V.tensor_tensor(first_t[:, e + 1:e + 2], first_t[:, e:e + 1], tiles_e[:, e:e + 1], ALU.add))
            it = iota_t[0:1]
            dve.wait_ge(r_iota, 16)
            link(V.tensor_tensor(over[0:1], it.unsqueeze(2).to_broadcast([1, NT, E]),
                                 first_t[0:1, 1:E + 1].unsqueeze(1).to_broadcast([1, NT, E]), ALU.is_ge))
            V.tensor_reduce(e_f[0:1], over[0:1], AX_X, ALU.add)
            link(V.tensor_tensor(part[0:1], over[0:1], tiles_e[0:1].unsqueeze(1).to_broadcast([1, NT, E]), ALU.mult))
            link(V.tensor_reduce(b_f[0:1], part[0:1], AX_X, ALU.add))
            link(V.tensor_tensor(b_f[0:1], it, b_f[0:1], ALU.subtract))
            link(V.tensor_scalar(b_f[0:1], b_f[0:1], float(TS), None, ALU.mult))
            link(V.scalar_tensor_tensor(b_f[0:1], e_f[0:1], float(CAP), b_f[0:1], ALU.mult, ALU.add))
            V.tensor_scalar(btable[:], b_f[0:1], float(E * CAP), None, ALU.min)
            link(V.tensor_scalar(etab[:], e_f[0:1], float(E - 1), None, ALU.min))
            V.engine_nop().then_inc(r_tab, 1)
            link(V.tensor_scalar(first_r, first_t[:, 0:E], float(TS), None, ALU.mult))
            link(V.tensor_tensor(wh, rank[:], first_r.unsqueeze(1).to_broadcast([P, T, E]), ALU.add))
            for k in range(2):
                ht = V.tensor_tensor(hit2[:, :, k, :], wh, onehot[:, :, k, :], ALU.mult)
            link(ht)
            link(V.tensor_reduce(back_f, hit2, AX_X, ALU.add))
            V.tensor_copy(back[:], back_f).then_inc(r_back, 1)
            dve.wait_ge(s_const2, 16 * len(CONST2))
            link(V.tensor_scalar(ew_f[:], ew_f[:], WSCALE, None, ALU.mult))
            link(V.tensor_copy(ew2[:, :, 0:HB * D], ew_f[:]))
            V.tensor_tensor(ew2[:, :, HB * D:2 * HB * D], ew_f[:], ew2[:, :, 0:HB * D], ALU.subtract).then_inc(b_w2, 1)

        def route_end_pe(pe):
            pe.wait_ge(r_chosen, 1)
            pe.wait_ge(r_slot, T // RT)
            nc.tensor.matmul(ps[:, 7, 0:E], ones[:], chosen, start=True, stop=True).then_inc(r_cnt, 1)

        def route_end_sp(sp):
            sp.wait_ge(s_x, T)
            sp.dma_start(iota_t[0:1], in_ap["c_iotat"]).then_inc(r_iota, 16)
            sp.wait_ge(r_zero, 1)
            z3 = zrow
            sp.dma_start(xs_rows[E * CAP:E * CAP + TS, :].rearrange("(s p) c -> p s c", p=P), z3).then_inc(r_padded, 16)
            sp.wait_ge(r_pad, 1)
            for e in range(E):
                first = sp.value_load(pad[0:1, e:e + 1], min_val=e * CAP, max_val=e * CAP + B * N)
                sp.dma_start(xs_rows[bass.ds(first, TS), :].rearrange("(s p) c -> p s c", p=P), z3).then_inc(r_padded, 16)

        SCATTERED = 16 * 2 * T // RINGS
        PADDED = 16 * (E + 1)

        wb = carver()
        zin = wb([ZIN, TS // P, 2 * D], F16)
        zTb = wb([2, 2, TS], F16)
        hT = wb([2, HB, TS])
        hhl = wb([3, 2, HB, TS], F16)
        w2t = wb([2, 2, HB * D], F16)
        yo = wb([3, TS // P, D])

        def stage_b_sp(sp):
            sp.wait_ge(r_tab, 1)
            for ring in range(RINGS):
                sp.wait_ge(r_scat[ring], SCATTERED)
            sp.wait_ge(r_padded, PADDED)
            sp.wait_ge(r_back, 1)

            SLICES = TB // (NT // UB - 1)

            def emit(tile):
                if t := tile(0):
                    b = t.s % ZIN
                    at_least(sp, b_tr, t.n - (ZIN - 1))
                    row0 = sp.value_load(btable[0:1, bass.ds(t.n, 1)], min_val=0, max_val=E * CAP)
                    sp.dma_start(zin[:, b], xs_rows[bass.ds(row0, TS), :].rearrange("(s p) c -> p s c", p=P)).then_inc(b_load[b], 16)
                    if is_tile(t, 2):
                        for dst, name in CONST3:
                            sp.dma_start(dst, in_ap[name]).then_inc(s_const3, 16)
                    if isinstance(t.n, int):
                        if UB - TB <= t.n < UB:
                            m = t.n - (UB - TB)
                            sp.dma_start(adjT[:, 0, m], in_ap["adjT"][0, :, m]).then_inc(c_adj[0], 16)
                    elif t.s % (UB // SLICES) == 0:
                        m = (t.base - 1) * SLICES + t.s // (UB // SLICES)
                        sp.dma_start(adjT[:, 1, bass.ds(m, 1)].rearrange("p a b -> p (a b)"),
                                     in_ap["adjT"][1, :, bass.ds(m, 1)].rearrange("p a b -> p (a b)")).then_inc(c_adj[1], 16)
            lagged(sp, emit, NT, UB, 0)

        def stage_b_pool(pool):
            def emit(tile):
                if t := tile(0):
                    b = t.s % 3
                    pool.wait_ge(b_out, t.n + 1)
                    nc.gpsimd.dma_start(y_rows[bass.ds(t.n * TS, TS), :].rearrange("(s p) c -> p s c", p=P), yo[:, b]).then_inc(b_store[b], 16)
            lagged(pool, emit, NT, UB, 0)

        def stage_b_pe(pe):
            M = nc.tensor

            pe.wait_ge(r_tab, 1)
            pe.wait_ge(s_const2, 16 * len(CONST2))

            def emit(tile):
                if t := tile(0):
                    b = t.s % ZIN
                    pe.wait_ge(b_load[b], uses_of(t, ZIN))
                    at_least(pe, b_zt, t.n - 1)
                    tr = ps[:, t.s % 2].bitcast(F16)[:, 0:2 * TS].rearrange("p (h q) -> p h q", h=2)
                    for s in range(TS // P):
                        for h in range(2):
                            mm = M.transpose(tr[:, h, s * P:(s + 1) * P], zin[:, b, s, h * D:(h + 1) * D], ident16[:])
                    mm.then_inc(b_tr, 1)
                if t := tile(1):
                    e = pe.value_load(etab[0:1, bass.ds(t.n, 1)], min_val=0, max_val=E - 1)
                    pe.wait_ge(b_zt, t.n + 1)
                    at_least(pe, b_gelu, t.n - 1)
                    for c in range(HB):
                        for n, (a, w) in enumerate(((0, 0), (0, 1), (1, 0))):
                            mm = M.matmul(ps[:, 2 + 2 * (t.s % 2) + c, 0:TS],
                                          ew1[:, bass.ds(e * 2 + w, 1), c * P:(c + 1) * P].rearrange("p a b -> p (a b)"),
                                          zTb[:, t.s % 2, a], start=(n == 0), stop=(n == 2))
                    mm.then_inc(b_h, 1)
                if t := tile(3):
                    pe.wait_ge(b_lo, t.n + 1)
                    at_least(pe, b_out, t.n - 1)
                    for s in range(TS // P):
                        for c in range(HB):
                            for n, (a, w) in enumerate(((0, 0), (0, 1), (1, 0))):
                                mm = M.matmul(ps[:, 6 + t.s % 2, s * D:(s + 1) * D], hhl[:, t.s % 3, a, c, s * P:(s + 1) * P],
                                              w2t[:, t.s % 2, w, c * D:(c + 1) * D],
                                              start=(c == 0 and n == 0), stop=(c == HB - 1 and n == 2))
                    mm.then_inc(b_y, 1)
            lagged(pe, emit, NT, UB, 3)

        def stage_b_act(act):
            S = nc.scalar
            act.wait_ge(r_tab, 1)
            act.wait_ge(r_back, 1)

            def emit(tile):
                if t := tile(1):
                    e = act.value_load(etab[0:1, bass.ds(t.n, 1)], min_val=0, max_val=E - 1)
                    act.wait_ge(b_h, t.n + 1)
                    at_least(act, b_lo, t.n - 1)
                    at_least(act, b_y, t.n - 2)
                    for c in range(HB):
                        for dst in (hT[:, t.s % 2, c], hhl[:, t.s % 3, 0, c]):
                            ge = S.activation(dst, ps[:, 2 + 2 * (t.s % 2) + c, 0:TS], ACT.Gelu,
                                              bias=eb1[:, bass.ds(e * HB + c, 1)], scale=1.0 / WSCALE)
                    ge.then_inc(b_gelu, 1)
            lagged(act, emit, NT, UB, 1)

        def stage_b_dve(dve):
            V = nc.vector
            dve.wait_ge(b_w2, 1)

            def emit(tile):
                if t := tile(0):
                    dve.wait_ge(b_tr, t.n + 1)
                    at_least(dve, b_h, t.n - 1)
                    V.tensor_copy(zTb[:, t.s % 2].rearrange("p h q -> p (h q)"), ps[:, t.s % 2].bitcast(F16)[:, 0:2 * TS]).then_inc(b_zt, 1)
                if t := tile(2):
                    e = dve.value_load(etab[0:1, bass.ds(t.n, 1)], min_val=0, max_val=E - 1)
                    at_least(dve, b_y, t.n - 1)
                    V.tensor_copy(w2t[:, t.s % 2].rearrange("p a b -> p (a b)"),
                                  ew2[:, bass.ds(e, 1), :].rearrange("p a b -> p (a b)"))
                    dve.wait_ge(b_gelu, t.n + 1)
                    V.tensor_tensor(hhl[:, t.s % 3, 1], hT[:, t.s % 2], hhl[:, t.s % 3, 0], ALU.subtract).then_inc(b_lo, 1)
                if t := tile(3):
                    e = dve.value_load(etab[0:1, bass.ds(t.n, 1)], min_val=0, max_val=E - 1)
                    dve.wait_ge(b_y, t.n + 1)
                    if not (isinstance(t.n, int) and t.n < 3):
                        dve.wait_ge(b_store[t.s % 3], uses_of(t, 3) - 16)
                    V.scalar_tensor_tensor(yo[:, t.s % 3], ps[:, 6 + t.s % 2, 0:TS // P * D].rearrange("p (s d) -> p s d", d=D),
                                           1.0 / WSCALE, eb2[:, bass.ds(e, 1), :].to_broadcast([P, TS // P, D]),
                                           ALU.mult, ALU.add).then_inc(b_out, 1)
            lagged(dve, emit, NT, UB, 3)

        def uses_of(t, ring):
            return 16 * (t.n // ring + 1) if isinstance(t.n, int) else t.base * (16 * UB // ring) + 16 * (t.j // ring + 1)

        wc = carver()
        yg = wc([2, TB, 2, D])
        xnC = wc([2, TB, D])
        xsC = wc([2, TB, D])
        qC = wc([2, D])
        qxT = wc([2, 2 * D])
        soft = wc([TB, D])
        bnC = wc([TB, 6])
        mvC = wc([TB, 2])
        rsC = wc([TB])
        gexp = wc([T])
        places = wc([2, TB, 2], U32)
        gden = wc([T])
        HALF = TB // 2
        FRONT, MAIN = TB, 2 * TB
        LAG_C = MAIN + 15
        D_START = T + MAIN + 1
        D_BEGUN = T + LAG_C - D_START

        def begin_d(eng, emit_d):
            return lambda step: emit_d(eng, at_step(step - D_START, T, UD)) if step >= D_START else None

        def stage_c_sp_loop(sp):
            with sp.Fori(1, B // 2) as bb:
                for p in range(2):
                    for i in range(TB):
                        sp.wait_ge(c_agg, (bb * 2 + p - 2) * TB + i + 1)
                        sp.dma_start(adjT[:, p, i], in_ap["adjT"][bass.ds(bb * 2 + p, 1), :, i].rearrange("g p n -> (g p) n")).then_inc(c_adj[p], 16)

        def b_is_over(eng):
            eng.wait_ge(b_out, NT)
            for k in range(3):
                eng.wait_ge(b_store[k], 16 * len(range(k, NT, 3)))

        def factors_pool(pool):
            G = nc.gpsimd
            pool.wait_ge(s_aggv, T)
            pool.wait_ge(s_dout, T)
            chain = [0]

            def link(ins):
                chain[0] += 1
                ins.then_inc(c_pc, 1)
                pool.wait_ge(c_pc, chain[0])
            for sums, factor, sign in ((din, s_in, 1.0), (dout, s_out_neg, -1.0)):
                link(G.tensor_scalar(smask[:], sums[:], 0.0, None, ALU.is_equal))
                link(G.tensor_tensor(factor[:], sums[:], smask[:], ALU.add))
                link(G.tensor_tensor(factor[:], factor[:], mhalf[:], ALU.pow))
                link(G.tensor_scalar(smask[:], smask[:], -sign, sign, ALU.mult, ALU.add))
                link(G.tensor_tensor(factor[:], factor[:], smask[:], ALU.mult))
            G.engine_nop().then_inc(c_factors, 1)

        def stage_c_pool(pool):
            G = nc.gpsimd
            b_is_over(pool)
            def emit(tile):
                if (t := tile(FRONT)) and t.s % TB == 3:
                    pool.wait_ge(c_stats, t.g + 1)
                    settled(pool, s_passed_p)
                    G.tensor_scalar(mvC[:, :, 1], mvC[:, :, 1], 1.0 + LN_EPS, LN_EPS * LN_EPS, ALU.mult, ALU.add).then_inc(c_pv, 1)
                    pool.wait_ge(c_pv, t.g + 1)
                    G.tensor_tensor(rsC, mvC[:, :, 1], mhalf[:, 0:TB], ALU.pow).then_inc(c_rs, 1)
                if t := tile(0):
                    par, i = t.s // TB, t.s % TB
                    if i == 0:
                        at_least(pool, c_comb, (t.g - 1) * 2)
                        settled(pool, s_passed_p)
                        G.tensor_copy(places[:, par], back[:, bass.ds(t.n, TB), :]).then_inc(c_places, 1)
                        pool.wait_ge(c_places, t.g + 1)
                        settled(pool, s_passed_p)
                    for k in range(2):
                        G.indirect_dma_start(yg[:, par, i, k, :], None, y_rows,
                                             bass.IndirectOffsetOnAxis(places[:, par, i, k:k + 1], 0)).then_inc(c_gath[par][i // HALF], 16)
            lagged(pool, emit, T, UA, LAG_C, following=begin_d(pool, emit_d_pool))

        def stage_c_dve(dve):
            V = nc.vector
            chain = [0]

            def link(ins):
                chain[0] += 1
                ins.then_inc(c_vp, 1)
                dve.wait_ge(c_vp, chain[0])
            dve.wait_ge(s_const3, 16 * len(CONST3))
            V.tensor_tensor(wsn[:, 0], wsn[:, 0], wsn[:, 1], ALU.add)
            for l in range(L1):
                for c in range(HB):
                    k = l * HB + c
                    V.tensor_tensor(ws[:, k, c * P:(c + 1) * P], ws[:, k, c * P:(c + 1) * P], ident[:], ALU.add)
            V.tensor_tensor(btab[:], btab[:], bs[:].unsqueeze(2).to_broadcast([P, L1 * HB, E1]), ALU.add)
            dve.wait_ge(c_factors, 1)
            dve.wait_ge(c_gexp, 1)
            link(V.tensor_scalar(gden, gexp, 1.0, None, ALU.add))
            link(V.reciprocal(gw[:, 0], gden))
            link(V.tensor_tensor(gw[:, 1], gw[:, 0], gexp, ALU.mult))

            def emit(tile):
                if t := tile(FRONT):
                    par, i = t.s // TB, t.s % TB
                    tiles = [t.n - i + k for k in range(TB)]
                    if i in (0, 2):
                        h = i // 2
                        dve.wait_ge(c_gath[par][h], graph_loads(t) * (2 * HALF * 16))
                        for pick_n, done in enumerate((c_v0, c_comb)):
                            if pick_n:
                                dve.wait_ge(c_v0, t.g * 2 + h + 1)
                            for k in range(h * HALF, (h + 1) * HALF):
                                ins = V.scalar_tensor_tensor(row(x, tiles[k]), yg[:, par, k, pick_n],
                                                             gw[:, pick_n, bass.ds(tiles[k], 1)],
                                                             row(x, tiles[k]), ALU.mult, ALU.add)
                            ins.then_inc(done, 1)
                    elif i in (1, 3):
                        h = i // 2
                        dve.wait_ge(c_comb, t.g * 2 + h + 1)
                        settled(dve, s_passed_v)
                        for k in range(h * HALF, (h + 1) * HALF):
                            ins = V.bn_stats(bnC[:, k], row(x, tiles[k]))
                        ins.then_inc(c_bn, 1)
                        dve.wait_ge(c_bn, t.g * 2 + h + 1)
                        settled(dve, s_passed_v)
                        for k in range(h * HALF, (h + 1) * HALF):
                            ins = V.bn_aggr(mvC[:, k], bnC[:, k])
                        if h:
                            ins.then_inc(c_stats, 1)
                    elif i == 4:
                        dve.wait_ge(c_stats, t.g + 1)
                        at_least(dve, c_tr, (t.g - 1) * TB)
                        for k in range(TB):
                            ins = V.scalar_tensor_tensor(xnC[:, par, k], row(x, tiles[k]), mvC[:, k, 0:1], lng[:, 0],
                                                         ALU.subtract, ALU.mult)
                        ins.then_inc(c_z, 1)
                    elif i == 5:
                        dve.wait_ge(c_z, t.g + 1)
                        dve.wait_ge(c_rs, t.g + 1)
                        for k in range(TB):
                            ins = V.scalar_tensor_tensor(xnC[:, par, k], xnC[:, par, k], rsC[:, k:k + 1], lng[:, 1],
                                                         ALU.mult, ALU.add)
                        ins.then_inc(c_xn, 1)
                    elif i == 6:
                        dve.wait_ge(c_xn, t.g + 1)
                        at_least(dve, c_agg, (t.g - 1) * TB)
                        for k in range(TB):
                            ins = V.tensor_scalar(xsC[:, par, k], xnC[:, par, k], s_in[:, bass.ds(tiles[k], 1)], None, ALU.mult)
                        ins.then_inc(c_xs, 1)
                if t := tile(MAIN):
                    par, i = t.s // TB, t.s % TB
                    dve.wait_ge(c_agg, t.n + 1)
                    at_least(dve, c_tr, t.n - 1)
                    V.tensor_scalar(qC[:, t.s % 2], ps[:, t.s % 2, 0:D], s_out_neg[:, bass.ds(t.n, 1)], None, ALU.mult).then_inc(c_q, 1)
                if (t := tile(MAIN + 14)) and t.s % TB == 0:
                    b0 = 4 + 2 * (t.s // TB)
                    dve.wait_ge(c_ln, t.g + 1)
                    V.scalar_tensor_tensor(soft.rearrange("p t d -> p (t d)"), ps[:, b0:b0 + 2].rearrange("p a b -> p (a b)"), 0.0,
                                           soft.rearrange("p t d -> p (t d)"), ALU.max, ALU.add).then_inc(c_sp, 1)
                if (t := tile(MAIN + 15)) and t.s % TB == 0:
                    dve.wait_ge(c_sp, t.g + 1)
                    xg = x[:, bass.ds(t.n, TB), :]
                    V.tensor_tensor(xg, xg, soft, ALU.add).then_inc(c_x, 1)
            lagged(dve, emit, T, UA, LAG_C, following=begin_d(dve, emit_d_dve))

        def stage_c_act(act):
            S = nc.scalar
            b_is_over(act)
            S.activation(gexp, gap[:], ACT.Exp).then_inc(c_gexp, 1)

            def emit(tile):
                if t := tile(MAIN + 1):
                    act.wait_ge(c_tr, t.n + 1)
                    at_least(act, c_pre, t.n - 1)
                    S.copy(qxT[:, t.s % 2], ps[:, 2 + t.s % 2, 0:2 * D]).then_inc(c_tc, 1)
                sf = soft.rearrange("p t d -> p (t d)")
                if (t := tile(MAIN + 10)) and t.s % TB == 0:
                    b0 = 4 + 2 * (t.s // TB)
                    act.wait_ge(c_pre, (t.g + 1) * TB)
                    at_least(act, c_x, t.g)
                    S.activation(sf, ps[:, b0:b0 + 2].rearrange("p a b -> p (a b)"), ACT.Abs).then_inc(c_abs, 1)
                if (t := tile(MAIN + 11)) and t.s % TB == 0:
                    act.wait_ge(c_abs, t.g + 1)
                    S.activation(sf, sf, ACT.Exp, scale=-1.0).then_inc(c_exp, 1)
                if (t := tile(MAIN + 13)) and t.s % TB == 0:
                    act.wait_ge(c_exp, t.g + 1)
                    S.activation(sf, sf, ACT.Ln, bias=1.0).then_inc(c_ln, 1)
            lagged(act, emit, T, UA, LAG_C, following=begin_d(act, emit_d_act))

        def stage_c_pe(pe):
            M = nc.tensor
            b_is_over(pe)

            def emit(tile):
                if t := tile(MAIN):
                    par, i = t.s // TB, t.s % TB
                    pe.wait_ge(c_xs, t.g + 1)
                    at_least(pe, c_q, t.n - 1)
                    pe.wait_ge(c_adj[par], graph_loads(t) * (TB * 16))
                    for m in range(TB):
                        mm = M.matmul(ps[:, t.s % 2, 0:D], adjT[:, par, i, m * P:(m + 1) * P], xsC[:, par, m],
                                      start=(m == 0), stop=(m == TB - 1))
                    mm.then_inc(c_agg, 1)
                if t := tile(MAIN + 1):
                    par, i = t.s // TB, t.s % TB
                    pe.wait_ge(c_q, t.n + 1)
                    at_least(pe, c_tc, t.n - 1)
                    M.transpose(ps[:, 2 + t.s % 2, 0:D], xnC[:, par, i], ident[:])
                    M.transpose(ps[:, 2 + t.s % 2, D:2 * D], qC[:, t.s % 2], ident[:]).then_inc(c_tr, 1)
                if t := tile(MAIN + 2):
                    par, i = t.s // TB, t.s % TB
                    pe.wait_ge(c_tc, t.n + 1)
                    if i == 0:
                        at_least(pe, c_x, t.g - 1)
                    o = ps[:, 4 + 2 * par + i // 4, (i % 4) * D:(i % 4 + 1) * D]
                    M.matmul(o, qxT[:, t.s % 2, 0:D], wsn[:, 0], start=True, stop=False)
                    M.matmul(o, qxT[:, t.s % 2, D:2 * D], wsn[:, 1], start=False, stop=True).then_inc(c_pre, 1)
            lagged(pe, emit, T, UA, LAG_C, following=begin_d(pe, emit_d_pe))

        wd = carver()
        zD = wd([2, D])
        zTD = wd([2, D])
        hD = [wd([2, HB * P]) for _ in range(L1 + 1)]
        weff = [wd([2, HB, HE]) for _ in range(L1)]
        bnD = wd([2, 6])
        mvD = wd([4, 2])
        rsD = wd([4])

        def stage_d_sp(sp):
            for l in range(L1):
                for i in range(TB):
                    sp.wait_ge(c_agg, (B - L1 + l) * TB + i + 1)
                    sp.dma_start(adjT[:, l, i], in_ap["wr"][:, l, i * N:(i + 1) * N]).then_inc(d_wr[l], 16)

        def stage_d_out(sp):
            with sp.Fori(0, T // UD) as b:
                sp.wait_ge(d_x, (b + 1) * UD)
                sp.dma_start(out[:, bass.ds(b * UD, UD), :], x[:, bass.ds(b * UD, UD), :]).then_inc(s_out, 16)
            sp.wait_ge(s_out, 16 * (T // UD))

        known_d_dve = {}

        def emit_d_dve(dve, tile):
            V = nc.vector
            wrv = [adjT[:, l].rearrange("p a b -> p (a b)").rearrange("p (e c h) -> p e c h", e=E1, c=HB) for l in range(L1)]
            if t := tile(0):
                V.bn_stats(bnD[:, t.s % 2], row(x, t.n)).then_inc(d_bn, 1)
            for l in range(L1):
                if t := tile(3 + l):
                    e = expert_of(known_d_dve, dve, route, t, E1)
                    if is_tile(t, 0):
                        dve.wait_ge(d_wr[l], 16 * TB)
                    at_least(dve, d_h[l + 1], t.n - 1)
                    V.tensor_tensor(weff[l][:, t.s % 2], wrv[l][:, bass.ds(e, 1)].rearrange("p a c h -> p (a c) h"),
                                    ws[:, l * HB:(l + 1) * HB], ALU.add).then_inc(d_weff[l], 1)
            if t := tile(0):
                dve.wait_ge(d_bn, t.n + 1)
                settled(dve, s_passed_v)
                V.bn_aggr(mvD[:, t.s % 4], bnD[:, t.s % 2]).then_inc(d_stats, 1)
            if t := tile(1):
                dve.wait_ge(d_rs, t.n + 1)
                at_least(dve, d_tr, t.n - 1)
                V.tensor_scalar(zD[:, t.s % 2], row(x, t.n), mvD[:, t.s % 4, 0:1], rsD[:, t.s % 4:t.s % 4 + 1],
                                ALU.subtract, ALU.mult).then_inc(d_z, 1)
            if t := tile(7):
                dve.wait_ge(d_o, t.n + 1)
                V.tensor_tensor(row(x, t.n), row(x, t.n), ps[:, 6 + t.s % 2, 0:D], ALU.add).then_inc(d_x, 1)

        def stage_d_dve(dve):
            lagged(dve, lambda tile: emit_d_dve(dve, tile), T, UD, LAG_D, begun=D_BEGUN)

        def emit_d_pool(pool, tile):
            G = nc.gpsimd
            if t := tile(0):
                pool.wait_ge(d_stats, t.n + 1)
                at_least(pool, d_z, t.n - 3)
                settled(pool, s_passed_p)
                G.tensor_scalar(mvD[:, t.s % 4, 1:2], mvD[:, t.s % 4, 1:2], LN_EPS, None, ALU.add).then_inc(d_pv, 1)
                pool.wait_ge(d_pv, t.n + 1)
                G.tensor_tensor(rsD[:, t.s % 4:t.s % 4 + 1], mvD[:, t.s % 4, 1:2], mhalf[:, 0:1], ALU.pow).then_inc(d_rs, 1)

        def stage_d_pool(pool):
            lagged(pool, lambda tile: emit_d_pool(pool, tile), T, UD, LAG_D, begun=D_BEGUN)

        known_d_act = {}

        def emit_d_act(act, tile):
            S = nc.scalar
            if t := tile(2):
                act.wait_ge(d_tr, t.n + 1)
                at_least(act, d_h[0], t.n - 1)
                S.copy(zTD[:, t.s % 2], ps[:, 0, 0:P]).then_inc(d_zt, 1)
            for l in range(L1 + 1):
                if t := tile(3 + l):
                    if l:
                        e = expert_of(known_d_act, act, route, t, E1)
                    act.wait_ge(d_h[l], t.n + 1)
                    at_least(act, d_h[l + 1] if l < L1 else d_o, t.n - 1)
                    for c in range(HB):
                        src = (ps[:, 1, c * P:(c + 1) * P] if l == 0 else
                               ps[:, 2 * l + t.s % 2, c * P:(c + 1) * P])
                        bias = bi[:, c:c + 1] if l == 0 else btab[:, (l - 1) * HB + c, bass.ds(e, 1)]
                        ins = S.activation(hD[l][:, t.s % 2, c * P:(c + 1) * P], src, ACT.Relu, bias=bias)
                    ins.then_inc(d_r[l], 1)

        def stage_d_act(act):
            lagged(act, lambda tile: emit_d_act(act, tile), T, UD, LAG_D, begun=D_BEGUN)

        def emit_d_pe(pe, tile):
            M = nc.tensor
            if t := tile(2):
                pe.wait_ge(d_z, t.n + 1)
                at_least(pe, d_zt, t.n)
                M.transpose(ps[:, 0, 0:P], zD[:, t.s % 2], ident[:]).then_inc(d_tr, 1)
            if t := tile(3):
                pe.wait_ge(d_zt, t.n + 1)
                at_least(pe, d_r[0], t.n)
                for c in range(HB):
                    mm = M.matmul(ps[:, 1, c * P:(c + 1) * P], wi[:, c * P:(c + 1) * P],
                                  zTD[:, t.s % 2], start=True, stop=True)
                mm.then_inc(d_h[0], 1)
            for l in range(L1):
                if t := tile(4 + l):
                    if is_tile(t, 0) and l:
                        pe.wait_ge(c_x, B - 1)
                    pe.wait_ge(d_weff[l], t.n + 1)
                    pe.wait_ge(d_r[l], t.n + 1)
                    at_least(pe, d_r[l + 1], t.n - 1)
                    for c in range(HB):
                        for k in range(HB):
                            mm = M.matmul(ps[:, 2 + 2 * l + t.s % 2, c * P:(c + 1) * P], weff[l][:, t.s % 2, k, c * P:(c + 1) * P],
                                          hD[l][:, t.s % 2, k * P:(k + 1) * P], start=(k == 0), stop=(k == HB - 1))
                    mm.then_inc(d_h[l + 1], 1)
            if t := tile(6):
                if is_tile(t, 0):
                    pe.wait_ge(c_x, B)
                pe.wait_ge(d_r[L1], t.n + 1)
                at_least(pe, d_x, t.n - 1)
                o = ps[:, 6 + t.s % 2, 0:D]
                for k in range(HB):
                    M.matmul(o, hD[L1][:, t.s % 2, k * P:(k + 1) * P], wo[:, k], start=(k == 0), stop=False)
                M.matmul(o, ones[0:3, :], rows[:, H0 + D:H0 + 2 * D], start=False, stop=True).then_inc(d_o, 1)

        def stage_d_pe(pe):
            lagged(pe, lambda tile: emit_d_pe(pe, tile), T, UD, LAG_D, begun=D_BEGUN)


        @block.sync
        def _(sp):
            for dst, name in CONST_ROWS:
                sp.dma_start(dst, in_ap[name]).then_inc(s_const_rows, 16)
            half = 2 * TB
            sp.dma_start(x[:, 0:half, :], in_ap["x"][:, 0:half, :]).then_inc(s_x0, 16)

            def load(g, p, first):
                if not first:
                    sp.wait_ge(s_agg, (g - 1) * TB)
                    sp.wait_ge(s_dout, (g - 1) * TB)
                sp.dma_start(adjT[:, p], in_ap["adjT"][bass.ds(g, 1)].rearrange("g p m n -> (g p) m n")).then_inc(s_adj[p], 16)
            load(0, 0, True)
            for dst, name in CONST:
                sp.dma_start(dst, in_ap[name]).then_inc(s_const, 16)
            load(1, 1, True)
            sp.dma_start(x[:, half:T, :], in_ap["x"][:, half:T, :]).then_inc(s_x1, 16)
            for dst, name in CONST1:
                sp.dma_start(dst, in_ap[name]).then_inc(s_const1, 16)
            with sp.Fori(1, B // 2) as bb:
                load(bb * 2, 0, False)
                load(bb * 2 + 1, 1, False)
            sp.wait_ge(s_prep_v, PREPARED)
            for dst, name in CONST2:
                sp.dma_start(dst, in_ap[name]).then_inc(s_const2, 16)
            route_end_sp(sp)
            stage_b_sp(sp)
            stage_c_sp_loop(sp)
            stage_d_sp(sp)
            stage_d_out(sp)

        @block.vector
        def _(dve):
            V = nc.vector
            V.memset(mhalf[:], -0.5)
            V.memset(ones[:], 1.0)
            V.memset(xn[:, :, D:D + 1], 1.0)
            V.memset(chosen, 0.0)
            V.memset(zrow, 0.0).then_inc(r_zero, 1)
            bias_n = [0]

            def bias_link(ins):
                bias_n[0] += 1
                ins.then_inc(s_bias, 1)
                dve.wait_ge(s_bias, bias_n[0])

            dve.wait_ge(s_const_rows, 16 * len(CONST_ROWS))
            bf = rows[:]
            src, a, b, c = (rows_f[:, k, :] for k in range(4))
            bias_link(V.tensor_scalar(src[:, 0:H0], src[:, 0:H0], WSCALE, None, ALU.mult))
            bias_link(V.tensor_copy(bf, src))
            bias_link(V.tensor_copy(a, bf))
            bias_link(V.tensor_tensor(b, src, a, ALU.subtract))
            bias_link(V.tensor_scalar(c, a, sel3[0:3, 0:1], None, ALU.mult))
            bias_link(V.tensor_copy(bf, b))
            bias_link(V.tensor_copy(a, bf))
            bias_link(V.tensor_tensor(b, b, a, ALU.subtract))
            bias_link(V.scalar_tensor_tensor(c, a, sel3[0:3, 1:2], c, ALU.mult, ALU.add))
            bias_link(V.scalar_tensor_tensor(c, b, sel3[0:3, 2:3], c, ALU.mult, ALU.add))
            bias_link(V.tensor_copy(bf, c))

            prep_n = [0]

            def link(ins):
                prep_n[0] += 1
                ins.then_inc(s_prep_v, 1)
                dve.wait_ge(s_prep_v, prep_n[0])

            def split_w1():
                dve.wait_ge(s_const, 16 * len(CONST))
                V.tensor_copy(ident16[:], ident[:])
                V.tensor_scalar(w1_f[:], w1_f[:], WSCALE, None, ALU.mult).then_inc(s_w1, 1)
                dve.wait_ge(s_w1, 1)
                V.tensor_copy(w1[:, 0], w1_f[:]).then_inc(s_w1, 1)
                dve.wait_ge(s_w1, 2)
                V.tensor_tensor(w1[:, 1], w1_f[:], w1[:, 0], ALU.subtract).then_inc(s_w1, 1)

            def prepare_first():
                dve.wait_ge(s_const1, 16 * len(CONST1))
                V.tensor_copy(tri[:], tri_f[:])
                link(V.tensor_scalar(beta_b[:], ident[:], 0.0, gcol[:, 1:2], ALU.mult, ALU.add))
                link(V.tensor_scalar(gcol[:, 2:3], gcol[:, 0:1], WSCALE, None, ALU.mult))

            def prepare_second():
                dve.wait_ge(s_prep_t, 1)
                V.tensor_tensor(eb1[:], eb1[:], ps[:, 7, 0:E * HB], ALU.add)
                V.tensor_tensor(rb[:], rb[:], ps[:, 7, E * HB:E * HB + E].unsqueeze(1).to_broadcast([P, TB, E]), ALU.add)
                link(V.tensor_scalar(ew_f[:], ew_f[:], gcol[:, 2:3], None, ALU.mult))
                link(V.tensor_scalar(rw_f[:, 0, :], rw_f[:, 0, :], gcol[:, 2:3], None, ALU.mult))

            def prepare_third():
                ew1v = ew1[:].rearrange("p (e s) h -> p e s h", s=2)
                link(V.tensor_copy(ew1v[:, :, 0, :], ew_f[:]))
                V.tensor_tensor(ew1v[:, :, 1, :], ew_f[:], ew1v[:, :, 0, :], ALU.subtract)
                link(V.tensor_copy(rw[:, 0, :], rw_f[:, 0, :]))
                link(V.tensor_tensor(rw[:, 1, :], rw_f[:, 0, :], rw[:, 0, :], ALU.subtract))

            def emit(tile):
                if t := tile(0):
                    dve.wait_ge(s_x0 if isinstance(t.n, int) and t.n < 2 * TB else s_x1, 16)
                    V.bn_stats(bnA[:, t.s % 2], row(x, t.n)).then_inc(s_bn, 1)
                    dve.wait_ge(s_bn, t.n + 1)
                    settled(dve, s_passed_v)
                    V.bn_aggr(mvA[:, t.s % 4, :], bnA[:, t.s % 2]).then_inc(s_stats, 1)
                if t := tile(12):
                    dve.wait_ge(s_rms, t.n + 1)
                    at_least(dve, s_silu, t.n - 1)
                    V.scalar_tensor_tensor(u[:, t.s % 2], ps[:, 3 + t.s % 2], rsA[:, t.s % 4, 1:2], rmsw[:],
                                           ALU.mult, ALU.mult).then_inc(s_u, 1)
                if t := tile(1):
                    dve.wait_ge(s_rstd, t.n + 1)
                    at_least(dve, s_agg, (t.g - 1) * TB)
                    V.tensor_scalar(xn[:, t.s, 0:D], row(x, t.n), mvA[:, t.s % 4, 0:1], rsA[:, t.s % 4, 0:1],
                                    ALU.subtract, ALU.mult).then_inc(s_norm, 1)
                if t := tile(14):
                    dve.wait_ge(s_y, t.n + 1)
                    V.tensor_tensor(row(x, t.n), row(x, t.n), ps[:, 6, 0:D], ALU.add).then_inc(s_x, 1)
                if t := tile(9):
                    if is_tile(t, 0):
                        split_w1()
                    dve.wait_ge(s_agg, t.n + 1)
                    at_least(dve, s_aggt, t.n - 1)
                    for dst in (agg_f, agg_hl[:, t.s % 2, 0]):
                        ins = V.scalar_tensor_tensor(dst, xn[:, t.s, 0:D], epsx[:, 0:1], ps[:, t.s % 2, 0:D], ALU.mult, ALU.add)
                    ins.then_inc(s_aggf, 1)
                    V.tensor_copy(din[:, bass.ds(t.n, 1)], ps[:, t.s % 2, D:D + 1]).then_inc(s_aggv, 1)
                    dve.wait_ge(s_aggf, t.n + 1)
                    V.tensor_tensor(agg_hl[:, t.s % 2, 1], agg_f, agg_hl[:, t.s % 2, 0], ALU.subtract).then_inc(s_agglo, 1)
                if is_tile(tile(16), 0):
                    prepare_first()
                if is_tile(tile(17), 0):
                    prepare_second()
                if is_tile(tile(18), 0):
                    prepare_third()
                route_dve_stats(dve, tile)
                route_dve(dve, tile)
            lagged(dve, emit, T, UA, LAG_A)
            route_end_dve(dve)
            stage_b_dve(dve)
            stage_c_dve(dve)
            stage_d_dve(dve)

        @block.gpsimd
        def _(pool):
            G = nc.gpsimd
            pool.wait_ge(s_bias, 1)

            def emit(tile):
                if t := tile(11):
                    pool.wait_ge(s_sq, t.n + 1)
                    at_least(pool, s_u, t.n - 3)
                    settled(pool, s_passed_p)
                    G.tensor_scalar(ssA[:, t.s % 4, 1:2], ssA[:, t.s % 4, 0:1], 1.0 / H0, RMS_EPS * WSCALE ** 2, ALU.mult, ALU.add).then_inc(s_ms, 1)
                    pool.wait_ge(s_ms, t.n + 1)
                    G.tensor_tensor(rsA[:, t.s % 4, 1:2], ssA[:, t.s % 4, 1:2], mhalf[:, 0:1], ALU.pow).then_inc(s_rms, 1)
                if t := tile(0):
                    pool.wait_ge(s_stats, t.n + 1)
                    at_least(pool, s_norm, t.n - 3)
                    settled(pool, s_passed_p)
                    G.tensor_scalar(mvA[:, t.s % 4, 1:2], mvA[:, t.s % 4, 1:2], LN_EPS, None, ALU.add).then_inc(s_var, 1)
                    pool.wait_ge(s_var, t.n + 1)
                    G.tensor_tensor(rsA[:, t.s % 4, 0:1], mvA[:, t.s % 4, 1:2], mhalf[:, 0:1], ALU.pow).then_inc(s_rstd, 1)
                route_pool(pool, tile)
            lagged(pool, emit, T, UA, LAG_A)
            factors_pool(pool)
            stage_b_pool(pool)
            stage_c_pool(pool)
            stage_d_pool(pool)

        @block.scalar
        def _(act):
            S = nc.scalar

            def emit(tile):
                if t := tile(10):
                    act.wait_ge(s_aggt, t.n + 1)
                    at_least(act, s_h, t.n - 1)
                    S.copy(aggT[:, t.s % 2], aggT_ps).then_inc(s_aggc, 1)
                if t := tile(12):
                    act.wait_ge(s_u, t.n + 1)
                    at_least(act, s_st, t.n - 1)
                    S.activation(su[:, t.s % 2], u[:, t.s % 2], ACT.Silu).then_inc(s_silu, 1)
                if t := tile(9):
                    p, i = t.s // TB, t.s % TB
                    act.wait_ge(s_adj[p], t.g * 8 + 16 - 8 * p)
                    at_least(act, s_dout, t.n)
                    S.activation(junk_n.rearrange("p (a b) -> p a b", b=P), adjT[:, p, :, i * P:(i + 1) * P], ACT.Identity,
                                 accum_out=dout[:, bass.ds(t.n, 1)]).then_inc(s_dout, 1)
                route_act(act, tile)
                if t := tile(10):
                    act.wait_ge(s_h, t.n + 1)
                    at_least(act, s_rms, t.n - 3)
                    S.activation(junk, ps[:, 3 + t.s % 2], ACT.Square, accum_out=ssA[:, t.s % 4, 0:1]).then_inc(s_sq, 1)
                if t := tile(12):
                    act.wait_ge(s_st, t.n + 1)
                    at_least(act, s_y, t.n - 1)
                    S.copy(sT[:, t.s % 2], ps[:, 5]).then_inc(s_stc, 1)
                route_act_hi(act, tile)
            lagged(act, emit, T, UA, LAG_A)
            stage_b_act(act)
            stage_c_act(act)
            stage_d_act(act)

        @block.tensor
        def _(pe):
            M = nc.tensor

            def prepare():
                pe.wait_ge(s_prep_v, 1)
                for k in range(E * HB):
                    M.matmul(ps[:, 7, k:k + 1], ew_f[:, k // HB, (k % HB) * P:(k % HB + 1) * P], gcol[:, 1:2],
                             start=True, stop=True)
                M.matmul(ps[:, 7, E * HB:E * HB + E], beta_b[:], rw_f[:, 0, :], start=True, stop=True).then_inc(s_prep_t, 1)

            def emit(tile):
                if t := tile(10):
                    if is_tile(t, 0):
                        pe.wait_ge(s_const, 16 * len(CONST))
                        pe.wait_ge(s_bias, 11)
                        pe.wait_ge(s_w1, 3)
                    pe.wait_ge(s_agglo, t.n + 1)
                    at_least(pe, s_aggc, t.n)
                    for h in range(2):
                        mm = M.transpose(aggT_ps[:, h], agg_hl[:, t.s % 2, h], ident16[:])
                    mm.then_inc(s_aggt, 1)
                if t := tile(9):
                    p, i = t.s // TB, t.s % TB
                    pe.wait_ge(s_adj[p], t.g * 8 + 16 - 8 * p)
                    pe.wait_ge(s_norm, (t.g + 1) * TB)
                    at_least(pe, s_aggv, t.n - 1)
                    for m in range(TB):
                        mm = M.matmul(ps[:, t.s % 2, 0:D + 1], adjT[:, p, i, m * P:(m + 1) * P],
                                      xn[:, p * TB + m, :], start=(m == 0), stop=(m == TB - 1))
                    mm.then_inc(s_agg, 1)
                route_logits(pe, tile)
                route_ranks(pe, tile)
                if t := tile(10):
                    pe.wait_ge(s_aggc, t.n + 1)
                    at_least(pe, s_u, t.n - 1)
                    bank = ps[:, 3 + t.s % 2]
                    for n, (a, w) in enumerate(((0, 0), (0, 1), (1, 0))):
                        M.matmul(bank, aggT[:, t.s % 2, a], w1[:, w], start=(n == 0), stop=False)
                    M.matmul(bank, ones[0:3, :], rows[:, 0:H0], start=False, stop=True).then_inc(s_h, 1)
                if t := tile(12):
                    pe.wait_ge(s_silu, t.n + 1)
                    at_least(pe, s_stc, t.n)
                    for c in range(HC):
                        mm = M.transpose(ps[:, 5, c * P:(c + 1) * P], su[:, t.s % 2, c * P:(c + 1) * P], ident[:])
                    mm.then_inc(s_st, 1)
                if t := tile(13):
                    pe.wait_ge(s_stc, t.n + 1)
                    at_least(pe, s_x, t.n)
                    for c in range(HC):
                        M.matmul(ps[:, 6, 0:D], sT[:, t.s % 2, c * P:(c + 1) * P], w2[:, c, :],
                                 start=(c == 0), stop=False)
                    M.matmul(ps[:, 6, 0:D], ones[0:3, :], rows[:, H0:H0 + D], start=False, stop=True).then_inc(s_y, 1)
                if is_tile(tile(17), 0):
                    prepare()
                route_transpose(pe, tile)
            lagged(pe, emit, T, UA, LAG_A)
            route_end_pe(pe)
            stage_b_pe(pe)
            stage_c_pe(pe)
            stage_d_pe(pe)


_OUTS = [((B, N, D), "float32")]


def kernel(**inputs):
    import numpy as np
    import concourse.bacc as _bacc
    from concourse import mybir as _mybir
    from concourse.bass_utils import run_bass_kernel_spmd as _run

    f = lambda k: np.asarray(inputs[k])
    rep = lambda v, n=P: np.ascontiguousarray(np.broadcast_to(v.reshape(1, -1), (n, v.size)))
    arrays = {
        "x": f("x").reshape(T, P, D).transpose(1, 0, 2),
        "adjT": f("adj").reshape(B, TB, P, TB, P).transpose(0, 4, 1, 3, 2).reshape(B, P, TB, N),
        "c_ident": np.eye(P, dtype=np.float32),
        "c_tri": np.triu(np.ones((P, P), np.float32), 1),
        "c_iota": rep(np.tile(np.arange(E, dtype=np.float32), TB)),
        "c_ecap": rep(np.tile(np.arange(E, dtype=np.float32) * CAP, TB)),
        "c_iotat": np.arange(NT, dtype=np.float32).reshape(1, NT),
        "c_sel3": np.eye(P, 3, dtype=np.float32),
        "w1": f("L0_gnn_W1"),
        "w2": f("L0_gnn_W2").reshape(HC, P, D).transpose(1, 0, 2).reshape(P, HC * D),
        "rmsw": rep(f("L0_gnn_rms_weight")),
        "epsx": rep(f("L0_gnn_epsilon")),
        "rows": rep(np.concatenate([f("L0_gnn_b1"), f("L0_gnn_b2"), f("L1_ffn_bo")]), 3),
    }
    arrays |= {
        "gcol": np.stack([f("L0_ffn_gamma"), f("L0_ffn_beta")], 1),
        "ew1": f("L0_ffn_W1").transpose(1, 0, 2).reshape(P, E * HE),
        "eb1": f("L0_ffn_b1").reshape(E, HB, P).transpose(2, 0, 1).reshape(P, E * HB),
        "rw": f("L0_ffn_Wr"),
        "rb": rep(np.tile(f("L0_ffn_br"), TB)),
        "ew2": f("L0_ffn_W2").reshape(E, HB, P, D).transpose(2, 0, 1, 3).reshape(P, E * HB * D),
        "eb2": rep(f("L0_ffn_b2")),
        "lng": rep(np.concatenate([f("L1_gnn_gamma"), f("L1_gnn_beta")])),
        "wsn": np.concatenate([f("L1_gnn_W_self"), f("L1_gnn_W_neigh")], 1),
        "wi": f("L1_ffn_Wi").T,
        "bi": f("L1_ffn_bi").reshape(HB, P).T,
        "ws": f("L1_ffn_Ws").reshape(L1, HE, HB, P).transpose(3, 0, 2, 1).reshape(P, -1),
        "bs": f("L1_ffn_bs").reshape(L1 * HB, P).T,
        "br": f("L1_ffn_br").reshape(L1, E1, HB, P).transpose(3, 0, 2, 1).reshape(P, -1),
        "wo": f("L1_ffn_Wo").T.reshape(HB, P, D).transpose(1, 0, 2).reshape(P, HB * D),
        "wr": f("L1_ffn_Wr").reshape(L1, E1, HE, HB, P).transpose(4, 0, 1, 3, 2).reshape(P, L1, -1),
        "route": f("L1_ffn_route_id").reshape(1, T),
    }
    nc = _bacc.Bacc("TRN2", target_bir_lowering=False, num_devices=1)
    aps, data = {}, {}
    for name, a in arrays.items():
        a = np.ascontiguousarray(a)
        data[f"in_{name}"] = a
        aps[name] = nc.dram_tensor(f"in_{name}", a.shape, _mybir.dt.from_np(a.dtype), kind="ExternalInput").ap()
    out = nc.dram_tensor("out_0", (P, T, D), F32, kind="ExternalOutput").ap()
    build(nc, aps, out)
    r = _run(nc, [data], core_ids=[0])
    got = np.asarray(r.results[0]["out_0"])
    return np.ascontiguousarray(got.transpose(1, 0, 2)).reshape(B, N, D)
```
